# Optimizing a Trainium2 kernel written in Bass

```python
import numpy as np
import jax
import jax.numpy as jnp

def _softmax(x, axis=-1):
    return jax.nn.softmax(x, axis=axis)

def _gelu(x):
    return jax.nn.gelu(x, approximate=True)

def _silu(x):
    return jax.nn.silu(x)

def _sigmoid(x):
    return jax.nn.sigmoid(x)

def _layernorm(x, axis=-1, eps=1e-05):
    m = jnp.mean(x, axis=axis, keepdims=True)
    v = jnp.var(x, axis=axis, keepdims=True)
    return (x - m) / jnp.sqrt(v + eps)

def _scatter_add(tgt, idx, src, axis=0):
    return tgt.at[idx].add(src)

def _segment_sum(src, seg, n):
    return jax.ops.segment_sum(src, seg, n)
kernel_name = 'mk_seq_preln_d2_jaxref_r8_156705'

def setup_inputs(seed: int=0):
    np.random.seed(seed)
    _w = jnp.asarray

    def _L0_attn_setup():
        import jax, jax.numpy as jnp
        import numpy as np
        import math
        B, T, D_IN, D_OUT = (2, 256, 512, 512)
        N_HEADS, N_KV = (32, 8)
        HEAD_DIM = D_OUT // N_HEADS
        GROUP_SIZE = N_HEADS // N_KV
        ROPE_BASE = 500000.0
        CTX = 256

        def _rope_tables(head_dim, base, seq_len):
            inv_freq = 1.0 / base ** (jnp.arange(0, head_dim, 2, dtype=jnp.float32) / head_dim)
            t = jnp.arange(seq_len, dtype=jnp.float32)
            freqs = jnp.einsum('i,j->ij', t, inv_freq)
            return (jnp.cos(freqs), jnp.sin(freqs))

        def _apply_rope(x, cos, sin):
            x1, x2 = jnp.split(x, 2, axis=-1)
            c = cos[None, None]
            s = sin[None, None]
            return jnp.concatenate([x1 * c - x2 * s, x1 * s + x2 * c], axis=-1)
        key = jax.random.key(seed)
        ks = jax.random.split(key, 5)
        scale = 0.02
        return {'x': jax.random.normal(ks[0], (B, T, D_IN), dtype=jnp.float32), 'Wq': jax.random.normal(ks[1], (D_IN, D_OUT), dtype=jnp.float32) * scale, 'Wk': jax.random.normal(ks[2], (D_IN, N_KV * HEAD_DIM), dtype=jnp.float32) * scale, 'Wv': jax.random.normal(ks[3], (D_IN, N_KV * HEAD_DIM), dtype=jnp.float32) * scale, 'Wo': jax.random.normal(ks[4], (D_OUT, D_OUT), dtype=jnp.float32) * scale}
    _L0_attn_in = _L0_attn_setup()

    def _L0_ffn_setup():
        import jax, jax.numpy as jnp
        import numpy as np
        LORA_SCALING = 1.0 / 2.0

        def _qlora_linear(x, wq, A, B):
            w = jnp.tile(wq, (1, 4))
            base = x @ w.T
            lora = x @ A.T @ B.T
            return base + lora * LORA_SCALING
        key = jax.random.key(seed)
        ks = jax.random.split(key, 10)
        d, h, r = (512, 1376, 2)
        return {'x': jax.random.normal(ks[0], (16, 1, d), dtype=jnp.float32), 'w1q': jax.random.normal(ks[1], (h, d // 4), dtype=jnp.float32) * 0.02, 'a1': jax.random.normal(ks[2], (r, d), dtype=jnp.float32) * 0.02, 'b1': jax.random.normal(ks[3], (h, r), dtype=jnp.float32) * 0.02, 'w3q': jax.random.normal(ks[4], (h, d // 4), dtype=jnp.float32) * 0.02, 'a3': jax.random.normal(ks[5], (r, d), dtype=jnp.float32) * 0.02, 'b3': jax.random.normal(ks[6], (h, r), dtype=jnp.float32) * 0.02, 'w2q': jax.random.normal(ks[7], (d, h // 4), dtype=jnp.float32) * 0.02, 'a2': jax.random.normal(ks[8], (r, h), dtype=jnp.float32) * 0.02, 'b2': jax.random.normal(ks[9], (d, r), dtype=jnp.float32) * 0.02}
    _L0_ffn_in = _L0_ffn_setup()

    def _L1_attn_setup():
        import jax, jax.numpy as jnp
        import numpy as np
        H, KV, HD, HID = (32, 8, 128, 512)
        THETA, FACTOR, HI_FF, LO_FF, ORIG_MAX = (500000.0, 8.0, 4.0, 1.0, 1024)

        def _llama3_inv_freq():
            inv = 1.0 / THETA ** (np.arange(0, HD, 2, dtype=np.float64) / HD)
            wavelen = 2.0 * np.pi / inv
            low_wl = ORIG_MAX / LO_FF
            high_wl = ORIG_MAX / HI_FF
            smooth = (ORIG_MAX / wavelen - LO_FF) / (HI_FF - LO_FF)
            scaled = np.where(wavelen > low_wl, inv / FACTOR, inv)
            mid = (wavelen <= low_wl) & (wavelen >= high_wl)
            scaled = np.where(mid, (1 - smooth) * inv / FACTOR + smooth * inv, scaled)
            return scaled.astype(np.float32)

        def _rope_cos_sin(T):
            inv = _llama3_inv_freq()
            pos = np.arange(T, dtype=np.float32)
            freqs = pos[:, None] * inv[None, :]
            emb = np.concatenate([freqs, freqs], axis=-1)
            return (jnp.asarray(np.cos(emb)), jnp.asarray(np.sin(emb)))

        def _rotate_half(x):
            x1, x2 = jnp.split(x, 2, axis=-1)
            return jnp.concatenate([-x2, x1], axis=-1)
        key = jax.random.key(seed)
        ks = jax.random.split(key, 5)
        s = 1.0 / np.sqrt(HID)
        return {'x': jax.random.normal(ks[0], (1, 256, HID), jnp.float32), 'wq': jax.random.normal(ks[1], (HID, H * HD), jnp.float32) * s, 'wk': jax.random.normal(ks[2], (HID, KV * HD), jnp.float32) * s, 'wv': jax.random.normal(ks[3], (HID, KV * HD), jnp.float32) * s, 'wo': jax.random.normal(ks[4], (H * HD, HID), jnp.float32) * s}
    _L1_attn_in = _L1_attn_setup()

    def _L1_ffn_setup():
        import jax, jax.numpy as jnp
        import numpy as np
        H = 512
        I = 1376
        B, S = (2, 256)
        key = jax.random.key(seed)
        k1, k2, k3 = jax.random.split(key, 3)
        x = jax.random.normal(k1, (B, S, H), dtype=jnp.float32)
        w_gate_up = jax.random.normal(k2, (2 * I, H), dtype=jnp.float32) * 0.02
        w_down = jax.random.normal(k3, (H, I), dtype=jnp.float32) * 0.02
        return {'x': x, 'w_gate_up': w_gate_up, 'w_down': w_down}
    _L1_ffn_in = _L1_ffn_setup()
    _d = {'L0_attn_x': _L0_attn_in['x'], 'L0_attn_Wq': _L0_attn_in['Wq'], 'L0_attn_Wk': _L0_attn_in['Wk'], 'L0_attn_Wv': _L0_attn_in['Wv'], 'L0_attn_Wo': _L0_attn_in['Wo'], 'L0_ffn_w1q': _L0_ffn_in['w1q'], 'L0_ffn_a1': _L0_ffn_in['a1'], 'L0_ffn_b1': _L0_ffn_in['b1'], 'L0_ffn_w3q': _L0_ffn_in['w3q'], 'L0_ffn_a3': _L0_ffn_in['a3'], 'L0_ffn_b3': _L0_ffn_in['b3'], 'L0_ffn_w2q': _L0_ffn_in['w2q'], 'L0_ffn_a2': _L0_ffn_in['a2'], 'L0_ffn_b2': _L0_ffn_in['b2'], 'L1_attn_wq': _L1_attn_in['wq'], 'L1_attn_wk': _L1_attn_in['wk'], 'L1_attn_wv': _L1_attn_in['wv'], 'L1_attn_wo': _L1_attn_in['wo'], 'L1_ffn_w_gate_up': _L1_ffn_in['w_gate_up'], 'L1_ffn_w_down': _L1_ffn_in['w_down']}
    _x0 = _d['L0_attn_x']
    _d['L0_attn_x'] = jax.random.normal(jax.random.fold_in(jax.random.key(seed), 1), (2, 512, 512), dtype=_x0.dtype)
    del _x0
    return _d

def reference(L0_attn_x, L0_attn_Wq, L0_attn_Wk, L0_attn_Wv, L0_attn_Wo, L0_ffn_w1q, L0_ffn_a1, L0_ffn_b1, L0_ffn_w3q, L0_ffn_a3, L0_ffn_b3, L0_ffn_w2q, L0_ffn_a2, L0_ffn_b2, L1_attn_wq, L1_attn_wk, L1_attn_wv, L1_attn_wo, L1_ffn_w_gate_up, L1_ffn_w_down):

    def _L0_attn_ref(x, Wq, Wk, Wv, Wo):
        import jax, jax.numpy as jnp
        import numpy as np
        import math
        B, T, D_IN, D_OUT = (2, 256, 512, 512)
        N_HEADS, N_KV = (32, 8)
        HEAD_DIM = D_OUT // N_HEADS
        GROUP_SIZE = N_HEADS // N_KV
        ROPE_BASE = 500000.0
        CTX = 256

        def _rope_tables(head_dim, base, seq_len):
            inv_freq = 1.0 / base ** (jnp.arange(0, head_dim, 2, dtype=jnp.float32) / head_dim)
            t = jnp.arange(seq_len, dtype=jnp.float32)
            freqs = jnp.einsum('i,j->ij', t, inv_freq)
            return (jnp.cos(freqs), jnp.sin(freqs))

        def _apply_rope(x, cos, sin):
            x1, x2 = jnp.split(x, 2, axis=-1)
            c = cos[None, None]
            s = sin[None, None]
            return jnp.concatenate([x1 * c - x2 * s, x1 * s + x2 * c], axis=-1)
        b, t, _ = x.shape
        cos, sin = _rope_tables(HEAD_DIM, ROPE_BASE, t)
        q = (x @ Wq).reshape(b, t, N_HEADS, HEAD_DIM).transpose(0, 2, 1, 3)
        k = (x @ Wk).reshape(b, t, N_KV, HEAD_DIM).transpose(0, 2, 1, 3)
        v = (x @ Wv).reshape(b, t, N_KV, HEAD_DIM).transpose(0, 2, 1, 3)
        q = _apply_rope(q, cos, sin)
        k = _apply_rope(k, cos, sin)
        k_h = jnp.repeat(k, GROUP_SIZE, axis=1)
        v_h = jnp.repeat(v, GROUP_SIZE, axis=1)
        scores = jnp.einsum('bhqd,bhkd->bhqk', q, k_h) / math.sqrt(HEAD_DIM)
        causal = jnp.triu(jnp.ones((t, t), dtype=bool), k=1)
        scores = jnp.where(causal[None, None], jnp.finfo(scores.dtype).min, scores)
        attn = jax.nn.softmax(scores, axis=-1)
        ctx = jnp.einsum('bhqk,bhkd->bhqd', attn, v_h)
        ctx = ctx.transpose(0, 2, 1, 3).reshape(b, t, D_OUT)
        return ctx @ Wo

    def _L0_ffn_ref(x, w1q, a1, b1, w3q, a3, b3, w2q, a2, b2):
        import jax, jax.numpy as jnp
        import numpy as np
        LORA_SCALING = 1.0 / 2.0

        def _qlora_linear(x, wq, A, B):
            w = jnp.tile(wq, (1, 4))
            base = x @ w.T
            lora = x @ A.T @ B.T
            return base + lora * LORA_SCALING
        gate = jax.nn.silu(_qlora_linear(x, w1q, a1, b1))
        up = _qlora_linear(x, w3q, a3, b3)
        return _qlora_linear(gate * up, w2q, a2, b2)

    def _L1_attn_ref(x, wq, wk, wv, wo):
        import jax, jax.numpy as jnp
        import numpy as np
        H, KV, HD, HID = (32, 8, 128, 512)
        THETA, FACTOR, HI_FF, LO_FF, ORIG_MAX = (500000.0, 8.0, 4.0, 1.0, 1024)

        def _llama3_inv_freq():
            inv = 1.0 / THETA ** (np.arange(0, HD, 2, dtype=np.float64) / HD)
            wavelen = 2.0 * np.pi / inv
            low_wl = ORIG_MAX / LO_FF
            high_wl = ORIG_MAX / HI_FF
            smooth = (ORIG_MAX / wavelen - LO_FF) / (HI_FF - LO_FF)
            scaled = np.where(wavelen > low_wl, inv / FACTOR, inv)
            mid = (wavelen <= low_wl) & (wavelen >= high_wl)
            scaled = np.where(mid, (1 - smooth) * inv / FACTOR + smooth * inv, scaled)
            return scaled.astype(np.float32)

        def _rope_cos_sin(T):
            inv = _llama3_inv_freq()
            pos = np.arange(T, dtype=np.float32)
            freqs = pos[:, None] * inv[None, :]
            emb = np.concatenate([freqs, freqs], axis=-1)
            return (jnp.asarray(np.cos(emb)), jnp.asarray(np.sin(emb)))

        def _rotate_half(x):
            x1, x2 = jnp.split(x, 2, axis=-1)
            return jnp.concatenate([-x2, x1], axis=-1)
        B, T, _ = x.shape
        q = (x @ wq).reshape(B, T, H, HD).transpose(0, 2, 1, 3)
        k = (x @ wk).reshape(B, T, KV, HD).transpose(0, 2, 1, 3)
        v = (x @ wv).reshape(B, T, KV, HD).transpose(0, 2, 1, 3)
        cos, sin = _rope_cos_sin(T)
        q = q * cos + _rotate_half(q) * sin
        k = k * cos + _rotate_half(k) * sin
        rep = H // KV
        k = jnp.repeat(k, rep, axis=1)
        v = jnp.repeat(v, rep, axis=1)
        scores = jnp.einsum('bhtd,bhsd->bhts', q, k) * (1.0 / np.sqrt(HD))
        mask = jnp.tril(jnp.ones((T, T), dtype=bool))
        scores = jnp.where(mask, scores, -jnp.inf)
        att = jax.nn.softmax(scores, axis=-1)
        out = jnp.einsum('bhts,bhsd->bhtd', att, v)
        out = out.transpose(0, 2, 1, 3).reshape(B, T, H * HD)
        return out @ wo

    def _L1_ffn_ref(x, w_gate_up, w_down):
        import jax, jax.numpy as jnp
        import numpy as np
        H = 512
        I = 1376
        B, S = (2, 256)
        gate_up = jnp.einsum('bsh,oh->bso', x, w_gate_up)
        d = gate_up.shape[-1] // 2
        h = jax.nn.silu(gate_up[..., :d]) * gate_up[..., d:]
        return jnp.einsum('bsi,hi->bsh', h, w_down)
    x = L0_attn_x
    x = x + _L0_attn_ref(_layernorm(x, axis=-1), L0_attn_Wq, L0_attn_Wk, L0_attn_Wv, L0_attn_Wo)
    x = x + _L0_ffn_ref(_layernorm(x, axis=-1), L0_ffn_w1q, L0_ffn_a1, L0_ffn_b1, L0_ffn_w3q, L0_ffn_a3, L0_ffn_b3, L0_ffn_w2q, L0_ffn_a2, L0_ffn_b2)
    x = x + _L1_attn_ref(_layernorm(x, axis=-1), L1_attn_wq, L1_attn_wk, L1_attn_wv, L1_attn_wo)
    x = x + _L1_ffn_ref(_layernorm(x, axis=-1), L1_ffn_w_gate_up, L1_ffn_w_down)
    return x

_drawn_inputs = setup_inputs


def setup_inputs(seed=0):
    import zlib

    import numpy as np

    out = dict(_drawn_inputs(seed))
    spreads = {}
    factors = {'L0_attn_Wq': 7.37,
     'L0_attn_Wk': 7.151,
     'L0_ffn_a1': 8.0,
     'L0_ffn_b1': 8.0,
     'L0_ffn_a3': 8.0,
     'L0_ffn_b3': 8.0,
     'L0_ffn_a2': 8.0,
     'L0_ffn_b2': 8.0}
    for name, (base, spread) in spreads.items():
        noise = np.random.default_rng([zlib.crc32(name.encode()), seed]).standard_normal(out[name].shape)
        drawn = base * np.exp(spread * noise) if base else spread * noise
        out[name] = jnp.asarray(drawn.astype(out[name].dtype))
    for name, factor in factors.items():
        out[name] = (out[name] * factor).astype(out[name].dtype)
    return out
```

```python
from contextlib import ExitStack

import concourse.bass as bass
from concourse import mybir

F32 = mybir.dt.float32
F32R = mybir.dt.float32r
BF16 = mybir.dt.bfloat16
ALU = mybir.AluOpType
ACT = mybir.ActivationFunctionType
AX_X = mybir.AxisListType.X

P = 128
B, T, D = 2, 512, 512
KT = D // P
NT = B * T // P
QT = T // P
NG, HPG = 8, 4
HD0, HD1 = 16, 128
FF = 1376
R = 2
EPS = 1e-5

J_CUM = [0, 1, 3, 6]
J_ALL = 10


def layer_norm(nc, m, name, folded=False):
    with ExitStack() as ctx:
        sb = lambda n, shape, dt=F32: ctx.enter_context(nc.sbuf_tensor(f"{name}_{n}", shape, dt))
        ps = lambda n: ctx.enter_context(nc.psum_tensor(f"{name}_{n}", [P, 512], F32))
        sem = lambda n: ctx.enter_context(nc.semaphore(f"{name}_{n}"))
        stats = sb("stats", [P, NT, 6])
        mv = sb("mv", [P, NT, 2])
        ve = sb("ve", [P, NT])
        sd = sb("sd", [P, NT])
        y0 = sb("y0", [P, NT])
        y1 = sb("y1", [P, NT])
        y2 = sb("y2", [P, NT])
        rstd = sb("rstd", [P, NT])
        row = sb("row", [P, 2, D])
        bank = [ps("bank0"), ps("bank1")]
        if folded:
            quarter = sb("quarter", [P, 2, P])
            fbank = [ps("fbank0"), ps("fbank1")]
            row_made, f_hi_done = sem("row_made"), sem("f_hi_done")
        moments, chain, root, row_ready = sem("moments"), sem("chain"), sem("root"), sem("row_ready")
        turned, hi_done, lo_done = sem("turned"), sem("hi_done"), sem("lo_done")

        block = ctx.enter_context(nc.Block())

        @block.vector
        def _(dve):
            steps = [0]

            def link(ins):
                steps[0] += 1
                ins.then_inc(chain, 1)
                dve.wait_ge(chain, steps[0])

            def low(t):
                dve.wait_ge(hi_done, t + 1)
                nc.vector.tensor_tensor(m.h_lo[:, :, t * P:(t + 1) * P],
                                        bank[t % 2][:, :].rearrange("p (k n) -> p k n", k=KT),
                                        m.h_hi[:, :, t * P:(t + 1) * P].bitcast(F32),
                                        ALU.subtract).then_inc(lo_done, 1)
                if folded:
                    dve.wait_ge(f_hi_done, t + 1)
                    nc.vector.tensor_tensor(m.f_lo[:, t * P:(t + 1) * P], fbank[t % 2][:, 0:P],
                                            m.f_hi[:, t * P:(t + 1) * P].bitcast(F32),
                                            ALU.subtract).then_inc(lo_done, 1)

            for t in range(NT):
                last = nc.vector.bn_stats(stats[:, t, :], m.x[:, t, :])
            link(last)
            for t in range(NT):
                last = nc.vector.bn_aggr(mv[:, t, :], stats[:, t, :])
            link(last)
            nc.vector.tensor_scalar(ve[:, :], mv[:, :, 1], EPS, None, ALU.add).then_inc(moments, 1)
            dve.wait_ge(root, 1)
            link(nc.vector.reciprocal(y0[:, :], sd[:, :]))
            link(nc.vector.tensor_tensor(y1[:, :], y0[:, :], y0[:, :], ALU.mult))
            link(nc.vector.tensor_tensor(y2[:, :], y1[:, :], ve[:, :], ALU.mult))
            link(nc.vector.tensor_scalar(y1[:, :], y2[:, :], -0.5, 1.5, ALU.mult, ALU.add))
            link(nc.vector.tensor_tensor(rstd[:, :], y0[:, :], y1[:, :], ALU.mult))
            for t in range(NT):
                if t >= 2:
                    dve.wait_ge(turned, t - 1)
                made = nc.vector.tensor_scalar(row[:, t % 2, :], m.x[:, t, :], mv[:, t, 0:1], rstd[:, t:t + 1],
                                               ALU.subtract, ALU.mult)
                if folded:
                    made.then_inc(row_made, 1)
                    dve.wait_ge(row_made, t + 1)
                    made = nc.vector.tensor_reduce(quarter[:, t % 2, :],
                                                   row[:, t % 2, :].rearrange("p (k n) -> p n k", k=KT), AX_X, ALU.add)
                made.then_inc(row_ready, 1)
                if t >= 1:
                    low(t - 1)
            low(NT - 1)

        @block.scalar
        def _(act):
            act.wait_ge(moments, 1)
            nc.scalar.activation(sd[:, :], ve[:, :], ACT.Sqrt).then_inc(root, 1)
            for t in range(NT):
                act.wait_ge(turned, t + 1)
                nc.scalar.activation(m.h_hi[:, :, t * P:(t + 1) * P],
                                     bank[t % 2][:, :].rearrange("p (k n) -> p k n", k=KT),
                                     ACT.Copy).then_inc(hi_done, 1)
                if folded:
                    nc.scalar.activation(m.f_hi[:, t * P:(t + 1) * P], fbank[t % 2][:, 0:P],
                                         ACT.Copy).then_inc(f_hi_done, 1)

        @block.tensor
        def _(pe):
            for t in range(NT):
                pe.wait_ge(row_ready, t + 1)
                if t >= 2:
                    pe.wait_ge(lo_done, (2 if folded else 1) * (t - 1))
                for k in range(KT):
                    last = nc.tensor.transpose(bank[t % 2][:, k * P:(k + 1) * P],
                                               row[:, t % 2, k * P:(k + 1) * P], m.ident[:, :])
                if folded:
                    last = nc.tensor.transpose(fbank[t % 2][:, 0:P], quarter[:, t % 2, :], m.ident[:, :])
                last.then_inc(turned, 1)


def attention1(nc, m, wq, wk, wv, wo):
    scale = float(HD1) ** -0.5
    RING = [J_CUM[i] + i for i in range(QT)]
    RING_ALL = J_ALL + QT
    S_BANK0 = [0, 1, 0, 0]
    S_BANKS = [1, 2, 4, 4]
    S_CUM = [0, 1, 3, 7]
    S_ALL = 11
    NC = 6
    V = NC - 1
    NRAW = 5

    wk_v = wk.rearrange("(k p) n -> p k n", p=P)
    wq_v = wq.rearrange("(k p) n -> p k n", p=P)
    wv_v = wv.rearrange("(k p) n -> p k n", p=P)
    wo_v = wo.rearrange("(h p) n -> h p n", p=P)

    with ExitStack() as ctx:
        sb = lambda n, shape, dt=F32: ctx.enter_context(nc.sbuf_tensor(f"a1_{n}", shape, dt))
        ps = lambda n: ctx.enter_context(nc.psum_tensor(f"a1_{n}", [P, 512], F32))
        sem = lambda n: ctx.enter_context(nc.semaphore(f"a1_{n}"))
        raw_w = sb("raw_w", [P, NRAW, 512])
        w_hi, w_lo = sb("w_hi", [P, NC, KT, P], F32R), sb("w_lo", [P, NC, KT, P], F32R)
        wo_hi, wo_lo = sb("wo_hi", [P, HPG, D], F32R), sb("wo_lo", [P, HPG, D], F32R)
        p_hi, p_lo = sb("p_hi", [P, B, NC, T], F32R), sb("p_lo", [P, B, NC, T], F32R)
        raw_p = sb("raw_p", [P, 2, T])
        rot_a, rot_b = sb("rot_a", [P, 2, T]), sb("rot_b", [P, 2, T])
        prob = [sb("prob0", [P, HPG, 3 * P]), sb("prob1", [P, HPG, 4 * P])]
        pt_hi, pt_lo = sb("pt_hi", [P, 2, 512], F32R), sb("pt_lo", [P, 2, 512], F32R)
        c_hi, c_lo = sb("c_hi", [P, 2, 512], F32R), sb("c_lo", [P, 2, 512], F32R)
        nmax, rsum, rinv = sb("nmax", [P, 2, HPG]), sb("rsum", [P, 2, HPG]), sb("rinv", [P, 2, HPG])
        score = [ps(f"score{k}") for k in range(4)]
        ring = [ps("ring0"), ps("ring1")]
        cbank, xbank = ps("cbank"), ps("xbank")

        loaded = [sem(f"loaded{k}") for k in range(NRAW)]
        scored, ringed, pt_used, x_made = (sem(n) for n in ("scored", "ringed", "pt_used", "x_made"))
        maxed, inverted, normed, ring_read, c_ready, rotated = (
            sem(n) for n in ("maxed", "inverted", "normed", "ring_read", "c_ready", "rotated"))
        exped, pt_hi_done, c_hi_done, x_read, p_hi_done, w_hi_done, wo_hi_done = (
            sem(n) for n in ("exped", "pt_hi_done", "c_hi_done", "x_read", "p_hi_done", "w_hi_done", "wo_hi_done"))
        summed, p_ready, w_ready, wo_ready = (sem(n) for n in ("summed", "p_ready", "w_ready", "wo_ready"))

        def piece(g, k):
            return k % NRAW, loaded[k % NRAW], 16 * (10 // NRAW * g + k // NRAW + 1)

        block = ctx.enter_context(nc.Block())

        @block.sync
        def _(sp):
            def load(g, k):
                slot, done, _ = piece(g, k)
                n = 10 * g + k - NRAW
                if n >= 0:
                    if n % 10 < NC:
                        sp.wait_ge(w_ready, NC * (n // 10) + n % 10 + 1)
                    else:
                        sp.wait_ge(wo_ready, HPG * (n // 10) + n % 10 - NC + 1)
                if k == 0:
                    src = wk_v[:, :, g * P:(g + 1) * P]
                elif k == V:
                    src = wv_v[:, :, g * P:(g + 1) * P]
                elif k < V:
                    src = wq_v[:, :, (HPG * g + k - 1) * P:(HPG * g + k) * P]
                else:
                    sp.dma_start(raw_w[:, slot, :], wo_v[HPG * g + k - NC]).then_inc(done, 16)
                    return
                sp.dma_start(raw_w[:, slot, :].rearrange("p (k n) -> p k n", k=KT), src).then_inc(done, 16)

            for g in range(NG):
                for k in range(NC + HPG):
                    load(g, k)

        @block.tensor
        def _(pe):
            def three(out, l_hi, l_lo, r_hi, r_lo, start, stop):
                nc.tensor.matmul(out, l_hi, r_hi, start=start, stop=False)
                nc.tensor.matmul(out, l_hi, r_lo, start=False, stop=False)
                return nc.tensor.matmul(out, l_lo, r_hi, start=False, stop=stop)

            def project(u, c):
                g, b = u // 2, u % 2
                pe.wait_ge(w_ready, NC * g + c + 1)
                if NC * u + c >= 1:
                    pe.wait_ge(x_read, NC * u + c)
                for k in range(KT):
                    if c < V:
                        last = three(xbank[:, :], w_hi[:, c, k, :], w_lo[:, c, k, :],
                                     m.h_hi[:, k, b * T:(b + 1) * T], m.h_lo[:, k, b * T:(b + 1) * T],
                                     k == 0, k == KT - 1)
                if c == V:
                    for t in range(QT):
                        for k in range(KT):
                            tok = slice(b * T + t * P, b * T + (t + 1) * P)
                            last = three(xbank[:, t * P:(t + 1) * P], m.h_hi[:, k, tok], m.h_lo[:, k, tok],
                                         w_hi[:, c, k, :], w_lo[:, c, k, :], k == 0, k == KT - 1)
                last.then_inc(x_made, 1)

            def scores(u, i):
                b, n = u % 2, (i + 1) * P
                if i == 0:
                    pe.wait_ge(p_ready, NC * u + V)
                for h in range(HPG):
                    per = HPG // S_BANKS[i]
                    bank = S_BANK0[i] + h // per
                    before = 16 * u + [-3, -2 + h // per, [4, 6, 8, 0][h], 8 + h + 1][i]
                    if h % per == 0 and before > 0:
                        pe.wait_ge(exped, before)
                    out = score[bank][:, (h % per) * n:(h % per + 1) * n]
                    q = slice(i * P, (i + 1) * P)
                    three(out, p_hi[:, b, 1 + h, q], p_lo[:, b, 1 + h, q], p_hi[:, b, 0, 0:n], p_lo[:, b, 0, 0:n],
                          True, False)
                    last = nc.tensor.matmul(out[:, i * P:n], m.ident_b[:, :], m.mask_b[:, :], start=False, stop=True)
                    if h % per == per - 1:
                        last.then_inc(scored, 1)

            def turn(u, i, j):
                n = RING_ALL * u + RING[i] + j
                if j == 0:
                    pe.wait_ge(normed, QT * u + i + 1)
                if n >= 2:
                    pe.wait_ge(ring_read, n - 1)
                for h in range(HPG):
                    last = nc.tensor.transpose(ring[n % 2][:, h * P:(h + 1) * P],
                                               prob[i % 2][:, h, j * P:(j + 1) * P], m.ident[:, :])
                last.then_inc(ringed, 1)

            def weigh(u, i, j):
                n, b = J_ALL * u + J_CUM[i] + j, u % 2
                pe.wait_ge(ring_read, RING_ALL * u + RING[i] + j + 1)
                if j == 0:
                    if i == 0:
                        pe.wait_ge(p_ready, NC * u + NC)
                    if QT * u + i >= 1:
                        pe.wait_ge(c_ready, QT * u + i)
                v = slice(j * P, (j + 1) * P)
                last = three(cbank[:, :], p_hi[:, b, V, v], p_lo[:, b, V, v], pt_hi[:, n % 2, :], pt_lo[:, n % 2, :],
                             j == 0, j == i)
                last.then_inc(pt_used, 1)

            def out_project(u, i):
                g, n = u // 2, RING_ALL * u + RING[i] + i + 1
                pe.wait_ge(c_ready, QT * u + i + 1)
                pe.wait_ge(ring_read, n - 1)
                pe.wait_ge(wo_ready, HPG * (g + 1))
                for h in range(HPG):
                    last = three(ring[n % 2][:, :], c_hi[:, i % 2, h * P:(h + 1) * P], c_lo[:, i % 2, h * P:(h + 1) * P],
                                 wo_hi[:, h, :], wo_lo[:, h, :], h == 0, h == HPG - 1)
                last.then_inc(ringed, 1)

            for c in range(NC):
                project(0, c)
            scores(0, 0)
            for u in range(2 * NG):
                more = u + 1 < 2 * NG
                for i in range(QT):
                    for j in range(min(2, i + 1)):
                        turn(u, i, j)
                    if i < QT - 1:
                        scores(u, i + 1)
                        if more:
                            project(u + 1, 2 * i)
                    for j in range(i + 1):
                        weigh(u, i, j)
                        if j + 2 <= i:
                            turn(u, i, j + 2)
                    if i < QT - 1 and more:
                        project(u + 1, 2 * i + 1)
                    if i == QT - 1 and more:
                        scores(u + 1, 0)
                    out_project(u, i)

        @block.vector
        def _(dve):
            def maxima(u, i):
                per, n = HPG // S_BANKS[i], (i + 1) * P
                for k in range(S_BANKS[i]):
                    dve.wait_ge(scored, S_ALL * u + S_CUM[i] + k + 1)
                    if k == 0 and QT * u + i >= 2:
                        dve.wait_ge(exped, 16 * u + 4 * i - 4)
                    nc.vector.tensor_reduce(nmax[:, i % 2, k * per:(k + 1) * per],
                                            score[S_BANK0[i] + k][:, 0:per * n].rearrange("p (h n) -> p h n", h=per),
                                            AX_X, ALU.max, negate=True).then_inc(maxed, 1)

            def normalise(u, i):
                dve.wait_ge(exped, 16 * u + 4 * (i + 1))
                nc.vector.reciprocal(rinv[:, i % 2, :], rsum[:, i % 2, :]).then_inc(inverted, 1)
                dve.wait_ge(inverted, QT * u + i + 1)
                for h in range(HPG):
                    pr = prob[i % 2][:, h, 0:(i + 1) * P]
                    last = nc.vector.tensor_scalar(pr, pr, rinv[:, i % 2, h:h + 1], None, ALU.mult)
                last.then_inc(normed, 1)

            def low(u, i, j):
                n = J_ALL * u + J_CUM[i] + j
                dve.wait_ge(pt_hi_done, n + 1)
                nc.vector.tensor_tensor(pt_lo[:, n % 2, :], ring[(RING[i] + j) % 2][:, :],
                                        pt_hi[:, n % 2, :].bitcast(F32), ALU.subtract).then_inc(ring_read, 1)

            def head_low(u, i):
                dve.wait_ge(c_hi_done, QT * u + i + 1)
                nc.vector.tensor_tensor(c_lo[:, i % 2, :], cbank[:, :], c_hi[:, i % 2, :].bitcast(F32),
                                        ALU.subtract).then_inc(c_ready, 1)

            def rotate(u, c):
                dve.wait_ge(x_read, NC * u + c + 1)
                n = 5 * u + c
                if n >= 2:
                    dve.wait_ge(p_ready, NC * u + c - 1)
                r = raw_p[:, c % 2, :]
                nc.vector.tensor_tensor(rot_a[:, c % 2, :], r, m.cos1[:, :], ALU.mult)
                nc.vector.tensor_tensor(rot_b[0:64, c % 2, :], raw_p[64:128, c % 2, :], m.sin1[64:128, :], ALU.mult)
                nc.vector.tensor_tensor(rot_b[64:128, c % 2, :], raw_p[0:64, c % 2, :], m.sin1[0:64, :],
                                        ALU.mult).then_inc(rotated, 1)

            def add_out(u, i):
                n = RING_ALL * u + RING[i] + i + 1
                dve.wait_ge(ringed, n + 1)
                xt = m.x[:, (u % 2) * QT + i, :]
                nc.vector.tensor_tensor(xt, ring[n % 2][:, :], xt, ALU.add).then_inc(ring_read, 1)

            for c in range(V):
                rotate(0, c)
            maxima(0, 0)
            normalise(0, 0)
            for u in range(2 * NG):
                more = u + 1 < 2 * NG
                for i in range(QT):
                    for j in range(min(2, i + 1)):
                        low(u, i, j)
                    if i < QT - 1:
                        maxima(u, i + 1)
                        if more:
                            rotate(u + 1, 2 * i)
                    for j in range(2, i + 1):
                        low(u, i, j)
                    head_low(u, i)
                    if i < QT - 1:
                        normalise(u, i + 1)
                        if more and 2 * i + 1 < V:
                            rotate(u + 1, 2 * i + 1)
                        add_out(u, i)
                    else:
                        if more:
                            maxima(u + 1, 0)
                        add_out(u, i)
                        if more:
                            normalise(u + 1, 0)

        @block.scalar
        def _(act):
            def exponentials(u, i, heads):
                per = HPG // S_BANKS[i]
                for h in heads:
                    act.wait_ge(maxed, S_ALL * u + S_CUM[i] + h // per + 1)
                    if h == 0 and QT * u + i >= 2:
                        s = QT * u + i - 2
                        act.wait_ge(ringed, RING_ALL * (s // QT) + RING[s % QT] + s % QT + 1)
                    n = (i + 1) * P
                    nc.scalar.activation(prob[i % 2][:, h, 0:n],
                                         score[S_BANK0[i] + h // per][:, (h % per) * n:(h % per + 1) * n], ACT.Exp,
                                         bias=nmax[:, i % 2, h:h + 1], accum_out=rsum[:, i % 2, h:h + 1],
                                         ).then_inc(exped, 1)

            def high(u, i, j):
                n = J_ALL * u + J_CUM[i] + j
                act.wait_ge(ringed, RING_ALL * u + RING[i] + j + 1)
                if n >= 2:
                    act.wait_ge(pt_used, n - 1)
                nc.scalar.activation(pt_hi[:, n % 2, :], ring[(RING[i] + j) % 2][:, :], ACT.Copy).then_inc(pt_hi_done, 1)

            def head_high(u, i):
                act.wait_ge(pt_used, J_ALL * u + J_CUM[i] + i + 1)
                if QT * u + i >= 2:
                    s = QT * u + i - 2
                    act.wait_ge(ringed, RING_ALL * (s // QT) + RING[s % QT] + s % QT + 2)
                nc.scalar.activation(c_hi[:, i % 2, :], cbank[:, :], ACT.Copy).then_inc(c_hi_done, 1)

            def read_out(u, c):
                act.wait_ge(x_made, NC * u + c + 1)
                if NC * u + c >= 2:
                    if c >= 2:
                        act.wait_ge(rotated, 5 * u + c - 1)
                    else:
                        act.wait_ge(p_ready, NC * u + c - 1)
                nc.scalar.activation(raw_p[:, c % 2, :], xbank[:, :], ACT.Copy,
                                     scale=scale if 1 <= c < V else 1.0).then_inc(x_read, 1)

            def part_high(u, c):
                if c < V:
                    act.wait_ge(summed, 5 * u + c + 1)
                    src = rot_a[:, c % 2, :]
                else:
                    act.wait_ge(x_read, NC * u + c + 1)
                    src = raw_p[:, c % 2, :]
                nc.scalar.activation(p_hi[:, u % 2, c, :], src, ACT.Copy).then_inc(p_hi_done, 1)

            def weights_high(g, c):
                slot, done, count = piece(g, c)
                act.wait_ge(done, count)
                if g >= 1:
                    act.wait_ge(x_made, NC * (2 * g - 1) + c + 1)
                nc.scalar.activation(w_hi[:, c, :, :], raw_w[:, slot, :].rearrange("p (k n) -> p k n", k=KT),
                                     ACT.Copy).then_inc(w_hi_done, 1)

            def out_weights_high(g):
                for h in range(HPG):
                    slot, done, count = piece(g, NC + h)
                    act.wait_ge(done, count)
                    if g >= 1:
                        act.wait_ge(ringed, RING_ALL * 2 * g)
                    nc.scalar.activation(wo_hi[:, h, :], raw_w[:, slot, :], ACT.Copy).then_inc(wo_hi_done, 1)

            for c in range(NC):
                weights_high(0, c)
                if c >= 1:
                    read_out(0, c - 1)
                if c >= 2:
                    part_high(0, c - 2)
            read_out(0, V)
            part_high(0, V - 1)
            part_high(0, V)
            exponentials(0, 0, range(HPG))
            for u in range(2 * NG):
                g, more = u // 2, u + 1 < 2 * NG
                split = u % 2 == 0 and g + 1 < NG
                for i in range(QT):
                    for j in range(min(2, i + 1)):
                        high(u, i, j)
                    if u % 2 == 0 and i == 0:
                        out_weights_high(g)
                    if i >= 1 and more:
                        part_high(u + 1, 2 * i - 1)
                    if i < QT - 1:
                        if more:
                            read_out(u + 1, 2 * i)
                        exponentials(u, i + 1, range(0, 2))
                    for j in range(2, i + 1):
                        high(u, i, j)
                    if i < QT - 1:
                        exponentials(u, i + 1, range(2, 4))
                    head_high(u, i)
                    if i < QT - 1:
                        if more:
                            part_high(u + 1, 2 * i)
                            read_out(u + 1, 2 * i + 1)
                    elif more:
                        exponentials(u + 1, 0, range(HPG))
                    if split and i >= 1:
                        weights_high(g + 1, 2 * i - 2)
                        weights_high(g + 1, 2 * i - 1)

        @block.gpsimd
        def _(pool):
            def part_sum(u, c):
                if c < V:
                    pool.wait_ge(rotated, 5 * u + c + 1)
                    nc.gpsimd.tensor_tensor(rot_a[:, c % 2, :], rot_a[:, c % 2, :], rot_b[:, c % 2, :],
                                            ALU.add).then_inc(summed, 1)

            def part_low(u, c):
                pool.wait_ge(p_hi_done, NC * u + c + 1)
                src = rot_a[:, c % 2, :] if c < V else raw_p[:, c % 2, :]
                nc.gpsimd.tensor_tensor(p_lo[:, u % 2, c, :], src, p_hi[:, u % 2, c, :].bitcast(F32),
                                        ALU.subtract).then_inc(p_ready, 1)

            def weights_low(g, c):
                pool.wait_ge(w_hi_done, NC * g + c + 1)
                nc.gpsimd.tensor_tensor(w_lo[:, c, :, :], raw_w[:, piece(g, c)[0], :].rearrange("p (k n) -> p k n", k=KT),
                                        w_hi[:, c, :, :].bitcast(F32), ALU.subtract).then_inc(w_ready, 1)

            def out_weights_low(g):
                for h in range(HPG):
                    pool.wait_ge(wo_hi_done, HPG * g + h + 1)
                    nc.gpsimd.tensor_tensor(wo_lo[:, h, :], raw_w[:, piece(g, NC + h)[0], :],
                                            wo_hi[:, h, :].bitcast(F32), ALU.subtract).then_inc(wo_ready, 1)

            for c in range(NC):
                weights_low(0, c)
                if c >= 2:
                    part_sum(0, c - 2)
                    part_low(0, c - 2)
            part_sum(0, V - 1)
            part_low(0, V - 1)
            part_low(0, V)
            for u in range(2 * NG):
                g, more = u // 2, u + 1 < 2 * NG
                split = u % 2 == 0 and g + 1 < NG
                for i in range(QT):
                    if u % 2 == 0 and i == 0:
                        out_weights_low(g)
                    if i >= 1 and more:
                        part_low(u + 1, 2 * i - 1)
                    if i < QT - 1 and more:
                        part_sum(u + 1, 2 * i)
                        part_low(u + 1, 2 * i)
                        part_sum(u + 1, 2 * i + 1)
                    if split and i >= 1:
                        weights_low(g + 1, 2 * i - 2)
                        weights_low(g + 1, 2 * i - 1)


def project0(nc, m, wqkv):
    NQ, NKV = NG * HPG, NG
    QW, KW = NQ * HD0, NKV * HD0
    W = QW + 2 * KW
    half = HD0 // 2
    w_v = wqkv.rearrange("(k p) n -> p k n", p=P)
    with ExitStack() as ctx:
        sb = lambda n, shape, dt=F32: ctx.enter_context(nc.sbuf_tensor(f"p0_{n}", shape, dt))
        ps = lambda n: ctx.enter_context(nc.psum_tensor(f"p0_{n}", [P, 512], F32))
        sem = lambda n: ctx.enter_context(nc.semaphore(f"p0_{n}"))
        raw_w = sb("raw_w", [P, 2, W])
        w_hi, w_lo = sb("w_hi", [P, KT, W], F32R), sb("w_lo", [P, KT, W], F32R)
        row, rot_a, rot_b = (sb(n, [P, 2, QW + KW]) for n in ("row", "rot_a", "rot_b"))
        qbank, kvbank = [ps("qbank0"), ps("qbank1")], [ps("kvbank0"), ps("kvbank1")]
        loaded = [sem("loaded0"), sem("loaded1")]
        w_hi_done, w_ready, zeroed, made, read, rotated, summed, hi_done, q_ready, k_ready = (sem(n) for n in (
            "w_hi_done", "w_ready", "zeroed", "made", "read", "rotated", "summed", "hi_done", "q_ready", "k_ready"))
        block = ctx.enter_context(nc.Block())

        @block.sync
        def _(sp):
            for k in range(KT):
                if k >= 2:
                    sp.wait_ge(w_ready, k - 1)
                sp.dma_start(raw_w[:, k % 2, :], w_v[:, k, :]).then_inc(loaded[k % 2], 16)

        @block.tensor
        def _(pe):
            for t in range(NT):
                if t >= 2:
                    pe.wait_ge(read, 3 * (t - 1))
                for bank, cols in ((qbank, slice(0, QW)), (kvbank, slice(QW, W))):
                    n = cols.stop - cols.start
                    for k in range(KT):
                        if t == 0:
                            pe.wait_ge(w_ready, k + 1)
                        h = slice(t * P, (t + 1) * P)
                        out = bank[t % 2][:, 0:n]
                        nc.tensor.matmul(out, m.h_hi[:, k, h], w_hi[:, k, cols], start=(k == 0), stop=False)
                        nc.tensor.matmul(out, m.h_hi[:, k, h], w_lo[:, k, cols], start=False, stop=False)
                        last = nc.tensor.matmul(out, m.h_lo[:, k, h], w_hi[:, k, cols], start=False, stop=(k == KT - 1))
                    last.then_inc(made, 1)

        @block.scalar
        def _(act):
            def high(t):
                act.wait_ge(summed, t + 1)
                r = rot_a[:, t % 2, :]
                nc.scalar.activation(m.q2[:, t, :, 0, :], r[:, 0:QW].rearrange("p (h n) -> p h n", n=HD0),
                                     ACT.Copy).then_inc(hi_done, 1)
                k3 = r[:, QW:QW + KW].rearrange("p (g n) -> p g n", n=HD0)
                for dup in range(2):
                    nc.scalar.activation(m.k2[:, t, :, 0, dup, :], k3, ACT.Copy).then_inc(hi_done, 1)

            for k in range(KT):
                act.wait_ge(loaded[k % 2], 16 * (k // 2 + 1))
                nc.scalar.activation(w_hi[:, k, :], raw_w[:, k % 2, :], ACT.Copy).then_inc(w_hi_done, 1)
            for t in range(NT):
                if t >= 2:
                    act.wait_ge(rotated, t - 1)
                act.wait_ge(made, 2 * t + 1)
                nc.scalar.activation(row[:, t % 2, 0:QW], qbank[t % 2][:, :], ACT.Copy,
                                     scale=float(HD0) ** -0.5).then_inc(read, 1)
                act.wait_ge(made, 2 * t + 2)
                nc.scalar.activation(row[:, t % 2, QW:QW + KW], kvbank[t % 2][:, 0:KW], ACT.Copy).then_inc(read, 1)
                if t == 0:
                    act.wait_ge(zeroed, 1)
                nc.scalar.activation(m.vpad[:, t, :, 48:48 + HD0],
                                     kvbank[t % 2][:, KW:2 * KW].rearrange("p (g n) -> p g n", n=HD0),
                                     ACT.Copy).then_inc(read, 1)
                if t >= 1:
                    high(t - 1)
            high(NT - 1)

        @block.vector
        def _(dve):
            def low(t):
                dve.wait_ge(hi_done, 3 * t + 3)
                nc.vector.tensor_tensor(m.q2[:, t, :, 1, :], rot_a[:, t % 2, 0:QW].rearrange("p (h n) -> p h n", n=HD0),
                                        m.q2[:, t, :, 0, :].bitcast(F32), ALU.subtract).then_inc(q_ready, 1)

            nc.vector.memset(m.vpad[:, :, :, :], 0.0).then_inc(zeroed, 1)
            for t in range(NT):
                dve.wait_ge(read, 3 * t + 2)
                if t >= 2:
                    dve.wait_ge(k_ready, 2 * (t - 1))
                    dve.wait_ge(q_ready, t - 1)
                table = lambda x, n: x[:, t % QT, :].unsqueeze(1).to_broadcast([P, n, half])
                heads = (QW + KW) // HD0
                nc.vector.tensor_tensor(rot_a[:, t % 2, :].rearrange("p (h n) -> p h n", n=half),
                                        row[:, t % 2, :].rearrange("p (h n) -> p h n", n=half),
                                        table(m.cos0, 2 * heads), ALU.mult)
                src = row[:, t % 2, :].rearrange("p (h s n) -> p h s n", s=2, n=half)
                dst = rot_b[:, t % 2, :].rearrange("p (h s n) -> p h s n", s=2, n=half)
                nc.vector.tensor_tensor(dst[:, :, 0, :], src[:, :, 1, :], table(m.nsin0, heads), ALU.mult)
                nc.vector.tensor_tensor(dst[:, :, 1, :], src[:, :, 0, :], table(m.sin0, heads),
                                        ALU.mult).then_inc(rotated, 1)
                if t >= 1:
                    low(t - 1)
            low(NT - 1)

        @block.gpsimd
        def _(pool):
            for k in range(KT):
                pool.wait_ge(w_hi_done, k + 1)
                nc.gpsimd.tensor_tensor(w_lo[:, k, :], raw_w[:, k % 2, :], w_hi[:, k, :].bitcast(F32),
                                        ALU.subtract).then_inc(w_ready, 1)
            for t in range(NT):
                pool.wait_ge(rotated, t + 1)
                nc.gpsimd.tensor_tensor(rot_a[:, t % 2, :], rot_a[:, t % 2, :], rot_b[:, t % 2, :],
                                        ALU.add).then_inc(summed, 1)
                pool.wait_ge(hi_done, 3 * t + 3)
                k3 = rot_a[:, t % 2, QW:QW + KW].rearrange("p (g n) -> p g n", n=HD0)
                for dup in range(2):
                    nc.gpsimd.tensor_tensor(m.k2[:, t, :, 1, dup, :], k3, m.k2[:, t, :, 0, 0, :].bitcast(F32),
                                            ALU.subtract).then_inc(k_ready, 1)


def attend0(nc, m, wo):
    wo_v = wo.rearrange("(k p) n -> p k n", p=P)
    HW = HPG * HD0
    S_BANK0 = [0, 2, 0, 0]
    S_BANKS = [2, 2, 4, 4]
    S_CUM = [0, 2, 4, 8]
    S_ALL = 12
    with ExitStack() as ctx:
        sb = lambda n, shape, dt=F32: ctx.enter_context(nc.sbuf_tensor(f"a0_{n}", shape, dt))
        ps = lambda n: ctx.enter_context(nc.psum_tensor(f"a0_{n}", [P, 512], F32))
        sem = lambda n: ctx.enter_context(nc.semaphore(f"a0_{n}"))
        raw_wo = sb("raw_wo", [P, KT, D])
        wo_hi, wo_lo = sb("wo_hi", [P, KT, D], F32R), sb("wo_lo", [P, KT, D], F32R)
        qk = sb("qk", [P, B, 3, T], F32R)
        wide = sb("wide", [P, 2, 3, P])
        prob = [sb("prob0", [P, HPG, 3 * P]), sb("prob1", [P, HPG, 4 * P])]
        pt = sb("pt", [P, 2, 512])
        c_hi, c_lo = sb("c_hi", [P, KT, NT * P], F32R), sb("c_lo", [P, KT, NT * P], F32R)
        nmax, rsum, rinv = sb("nmax", [P, 2, HPG]), sb("rsum", [P, 2, HPG]), sb("rinv", [P, 2, HPG])
        score = [ps(f"score{k}") for k in range(4)]
        ring = [ps("ring0"), ps("ring1")]
        cbank, xbank = ps("cbank"), ps("xbank")
        loaded = sem("loaded")
        scored, turned, pt_used, x_made = (sem(n) for n in ("scored", "turned", "pt_used", "x_made"))
        maxed, inverted, normed, pt_odd, c_ready, added = (
            sem(n) for n in ("maxed", "inverted", "normed", "pt_odd", "c_ready", "added"))
        exped, pt_even, c_hi_done, qk_ready, wo_hi_done = (
            sem(n) for n in ("exped", "pt_even", "c_hi_done", "qk_ready", "wo_hi_done"))
        spread, wo_ready = sem("spread"), sem("wo_ready")
        block = ctx.enter_context(nc.Block())

        @block.sync
        def _(sp):
            sp.dma_start(raw_wo[:, :, :], wo_v).then_inc(loaded, 16)

        @block.tensor
        def _(pe):
            def turn_qk(u, i):
                if QT * u + i >= 1:
                    pe.wait_ge(qk_ready, QT * u + i)
                pe.wait_ge(spread, QT * u + i + 1)
                for s in range(3):
                    last = nc.tensor.transpose(xbank[:, s * P:(s + 1) * P], wide[:, i % 2, s, :], m.ident[:, :])
                last.then_inc(x_made, 1)

            def scores(u, i):
                b, n = u % 2, (i + 1) * P
                pe.wait_ge(qk_ready, QT * u + i + 1)
                for h in range(HPG):
                    per = HPG // S_BANKS[i]
                    bank = S_BANK0[i] + h // per
                    before = 16 * u + [-3 + h // 2, -1 + h // 2, 2 + 2 * h, 9 + h][i]
                    if h % per == 0 and before > 0:
                        pe.wait_ge(exped, before)
                    out = score[bank][:, (h % per) * n:(h % per + 1) * n]
                    rows = slice(64 * (h // 2), 64 * (h // 2) + 64)
                    nc.tensor.matmul(out, qk[rows, b, 1 + h % 2, i * P:(i + 1) * P], qk[rows, b, 0, 0:n],
                                     start=True, stop=False)
                    last = nc.tensor.matmul(out[:, i * P:n], m.ident_b[:, :], m.mask_b[:, :], start=False, stop=True)
                    if h % per == per - 1:
                        last.then_inc(scored, 1)

            def turn(u, i, j):
                n = J_ALL * u + J_CUM[i] + j
                if j == 0:
                    pe.wait_ge(normed, QT * u + i + 1)
                if n >= 2:
                    pe.wait_ge((pt_even, pt_odd)[n % 2], n // 2)
                for h in range(HPG):
                    last = nc.tensor.transpose(ring[n % 2][:, h * P:(h + 1) * P],
                                               prob[i % 2][:, h, j * P:(j + 1) * P], m.ident[:, :])
                last.then_inc(turned, 1)

            def weigh(u, i, j):
                g, b, n = u // 2, u % 2, J_ALL * u + J_CUM[i] + j
                pe.wait_ge((pt_even, pt_odd)[n % 2], n // 2 + 1)
                if j == 0 and QT * u + i >= 1:
                    pe.wait_ge(c_ready, QT * u + i)
                rows = slice(HW * (g % 2), HW * (g % 2) + HW)
                for h in range(HPG):
                    last = nc.tensor.matmul(cbank[rows, 0:P], m.vpad[:, b * QT + j, g, 48 - HD0 * h:112 - HD0 * h],
                                            pt[:, n % 2, h * P:(h + 1) * P], start=(j == 0 and h == 0),
                                            stop=(j == i and h == HPG - 1))
                last.then_inc(pt_used, 1)

            for i in range(QT):
                turn_qk(0, i)
            scores(0, 0)
            for u in range(2 * NG):
                more = u + 1 < 2 * NG
                for i in range(QT):
                    for j in range(min(2, i + 1)):
                        turn(u, i, j)
                    if i < QT - 1:
                        scores(u, i + 1)
                    elif more:
                        scores(u + 1, 0)
                    if more and i < QT - 1:
                        turn_qk(u + 1, i)
                    for j in range(i + 1):
                        weigh(u, i, j)
                        if j + 2 <= i:
                            turn(u, i, j + 2)
                    if more and i == QT - 1:
                        turn_qk(u + 1, i)
            pe.wait_ge(wo_ready, KT)
            for t in range(NT):
                if t == 0:
                    pe.wait_ge(c_ready, QT * 2 * NG)
                if t >= 4:
                    pe.wait_ge(added, t - 3)
                for k in range(KT):
                    tok, out = slice(t * P, (t + 1) * P), score[t % 4][:, :]
                    nc.tensor.matmul(out, c_hi[:, k, tok], wo_hi[:, k, :], start=(k == 0), stop=False)
                    nc.tensor.matmul(out, c_hi[:, k, tok], wo_lo[:, k, :], start=False, stop=False)
                    last = nc.tensor.matmul(out, c_lo[:, k, tok], wo_hi[:, k, :], start=False, stop=(k == KT - 1))
                last.then_inc(scored, 1)

        def head_rows(u, i):
            g, t = u // 2, (u % 2) * QT + i
            return slice(HW * (g % 2), HW * (g % 2) + HW), g // 2, slice(t * P, (t + 1) * P)

        @block.vector
        def _(dve):
            def maxima(u, i):
                per, n = HPG // S_BANKS[i], (i + 1) * P
                for k in range(S_BANKS[i]):
                    dve.wait_ge(scored, S_ALL * u + S_CUM[i] + k + 1)
                    if k == 0 and QT * u + i >= 2:
                        dve.wait_ge(exped, 16 * u + 4 * i - 4)
                    nc.vector.tensor_reduce(nmax[:, i % 2, k * per:(k + 1) * per],
                                            score[S_BANK0[i] + k][:, 0:per * n].rearrange("p (h n) -> p h n", h=per),
                                            AX_X, ALU.max, negate=True).then_inc(maxed, 1)

            def normalise(u, i):
                dve.wait_ge(exped, 16 * u + 4 * (i + 1))
                nc.vector.reciprocal(rinv[:, i % 2, :], rsum[:, i % 2, :]).then_inc(inverted, 1)
                dve.wait_ge(inverted, QT * u + i + 1)
                for h in range(HPG):
                    pr = prob[i % 2][:, h, 0:(i + 1) * P]
                    last = nc.vector.tensor_scalar(pr, pr, rinv[:, i % 2, h:h + 1], None, ALU.mult)
                last.then_inc(normed, 1)

            def read_odd(u, i, j):
                n = J_ALL * u + J_CUM[i] + j
                if n % 2:
                    dve.wait_ge(turned, n + 1)
                    if n >= 2:
                        dve.wait_ge(pt_used, n - 1)
                    nc.vector.tensor_copy(pt[:, 1, :], ring[1][:, :]).then_inc(pt_odd, 1)

            def head_low(u, i):
                rows, k, tok = head_rows(u, i)
                dve.wait_ge(c_hi_done, QT * u + i + 1)
                nc.vector.tensor_tensor(c_lo[rows, k, tok], cbank[rows, 0:P], c_hi[rows, k, tok].bitcast(F32),
                                        ALU.subtract).then_inc(c_ready, 1)

            maxima(0, 0)
            normalise(0, 0)
            for u in range(2 * NG):
                more = u + 1 < 2 * NG
                for i in range(QT):
                    for j in range(min(2, i + 1)):
                        read_odd(u, i, j)
                    if i < QT - 1:
                        maxima(u, i + 1)
                    elif more:
                        maxima(u + 1, 0)
                    for j in range(2, i + 1):
                        read_odd(u, i, j)
                    head_low(u, i)
                    if i < QT - 1:
                        normalise(u, i + 1)
                    elif more:
                        normalise(u + 1, 0)
            for t in range(NT):
                dve.wait_ge(scored, S_ALL * 2 * NG + t + 1)
                nc.vector.tensor_tensor(m.x[:, t, :], score[t % 4][:, :], m.x[:, t, :], ALU.add).then_inc(added, 1)

        @block.scalar
        def _(act):
            def exponentials(u, i, heads):
                per = HPG // S_BANKS[i]
                for h in heads:
                    act.wait_ge(maxed, S_ALL * u + S_CUM[i] + h // per + 1)
                    if h == 0 and QT * u + i >= 2:
                        s = QT * u + i - 2
                        act.wait_ge(turned, J_ALL * (s // QT) + J_CUM[s % QT] + s % QT + 1)
                    n = (i + 1) * P
                    nc.scalar.activation(prob[i % 2][:, h, 0:n],
                                         score[S_BANK0[i] + h // per][:, (h % per) * n:(h % per + 1) * n], ACT.Exp,
                                         bias=nmax[:, i % 2, h:h + 1], accum_out=rsum[:, i % 2, h:h + 1],
                                         ).then_inc(exped, 1)

            def read_qk(u, i):
                act.wait_ge(x_made, QT * u + i + 1)
                nc.scalar.activation(qk[:, u % 2, :, i * P:(i + 1) * P],
                                     xbank[:, 0:3 * P].rearrange("p (s n) -> p s n", s=3), ACT.Copy).then_inc(qk_ready, 1)

            def read_even(u, i, j):
                n = J_ALL * u + J_CUM[i] + j
                if n % 2 == 0:
                    act.wait_ge(turned, n + 1)
                    if n >= 2:
                        act.wait_ge(pt_used, n - 1)
                    nc.scalar.activation(pt[:, 0, :], ring[0][:, :], ACT.Copy).then_inc(pt_even, 1)

            def head_high(u, i):
                rows, k, tok = head_rows(u, i)
                act.wait_ge(pt_used, J_ALL * u + J_CUM[i] + i + 1)
                nc.scalar.activation(c_hi[rows, k, tok], cbank[rows, 0:P], ACT.Copy).then_inc(c_hi_done, 1)

            for i in range(QT):
                read_qk(0, i)
            exponentials(0, 0, range(HPG))
            act.wait_ge(loaded, 16)
            for k in range(KT):
                nc.scalar.activation(wo_hi[:, k, :], raw_wo[:, k, :], ACT.Copy).then_inc(wo_hi_done, 1)
            for u in range(2 * NG):
                more = u + 1 < 2 * NG
                for i in range(QT):
                    for j in range(min(2, i + 1)):
                        read_even(u, i, j)
                    if i < QT - 1:
                        exponentials(u, i + 1, range(0, 2))
                        if more:
                            read_qk(u + 1, i)
                    for j in range(2, i + 1):
                        read_even(u, i, j)
                    if i < QT - 1:
                        exponentials(u, i + 1, range(2, 4))
                    head_high(u, i)
                    if i == QT - 1 and more:
                        exponentials(u + 1, 0, range(HPG))
                        read_qk(u + 1, i)

        @block.gpsimd
        def _(pool):
            for u in range(2 * NG):
                g, b = u // 2, u % 2
                for i in range(QT):
                    t = b * QT + i
                    if QT * u + i >= 2:
                        pool.wait_ge(x_made, QT * u + i - 1)
                    k = m.k2[:, t, g, :, :, :].bitcast(F32).rearrange("p s r n -> p (s r n)")
                    nc.gpsimd.tensor_copy(wide[:, i % 2, 0, :].rearrange("p (d n) -> p d n", d=2),
                                          k.unsqueeze(1).to_broadcast([P, 2, 4 * HD0]))
                    for a in range(2):
                        q = m.q2[:, t, HPG * g + a:HPG * g + HPG:2, :, :].bitcast(F32).rearrange("p h s n -> p h (s n)")
                        last = nc.gpsimd.tensor_copy(wide[:, i % 2, 1 + a, :].rearrange("p (h d n) -> p h d n", h=2, d=2),
                                                     q.unsqueeze(2).to_broadcast([P, 2, 2, 2 * HD0]))
                    last.then_inc(spread, 1)
                if u == 0:
                    for k in range(KT):
                        pool.wait_ge(wo_hi_done, k + 1)
                        nc.gpsimd.tensor_tensor(wo_lo[:, k, :], raw_wo[:, k, :], wo_hi[:, k, :].bitcast(F32),
                                                ALU.subtract).then_inc(wo_ready, 1)


def feed_forward0(nc, m, inp):
    FQ = FF // 4
    ROW = [(0, 128), (128, 128), (256, FQ - 256)]
    NR = len(ROW)
    S3 = 3 * R
    tiles = [(FQ * c + ROW[r][0], ROW[r][1]) for r in range(NR) for c in range(4)]
    NM = len(tiles)
    with ExitStack() as ctx:
        sb = lambda n, shape, dt=F32: ctx.enter_context(nc.sbuf_tensor(f"f0_{n}", shape, dt))
        ps = lambda n: ctx.enter_context(nc.psum_tensor(f"f0_{n}", [P, 512], F32))
        sem = lambda n: ctx.enter_context(nc.semaphore(f"f0_{n}"))
        w_raw, w_hi, w_lo = sb("w_raw", [P, 2 * FF]), sb("w_hi", [P, 2 * FF], F32R), sb("w_lo", [P, 2 * FF], F32R)
        d_raw, d_hi, d_lo = sb("d_raw", [P, NR, D]), sb("d_hi", [P, NR, D], F32R), sb("d_lo", [P, NR, D], F32R)
        a_raw, a_hi, a_lo = sb("a_raw", [P, KT, 64]), sb("a_hi", [P, KT, 64], F32R), sb("a_lo", [P, KT, 64], F32R)
        a2 = sb("a2", [P, NM, S3])
        b_raw, b_hi, b_lo = sb("b_raw", [64, FF]), sb("b_hi", [64, FF], F32R), sb("b_lo", [64, FF])
        b_st = sb("b_st", [64, FF], F32R)
        e_raw, e_hi, e_lo = sb("e_raw", [S3, D]), sb("e_hi", [S3, D], F32R), sb("e_lo", [S3, D])
        e_st = sb("e_st", [S3, D], F32R)
        pick = sb("pick", [64, 4])
        t_raw, t_hi, t_lo = sb("t_raw", [64, B, T]), sb("t_hi", [64, B, T], F32R), sb("t_lo", [64, B, T])
        t_st = sb("t_st", [64, B, T], F32R)
        s_raw, s_hi, s_lo = sb("s_raw", [S3, 2, T]), sb("s_hi", [S3, 2, T], F32R), sb("s_lo", [S3, 2, T])
        s_st = sb("s_st", [S3, 2, T], F32R)
        act_g, prod = sb("act_g", [P, 2, T]), sb("prod", [P, 3, T])
        quarters = sb("quarters", [P, 2, T])
        z_hi, z_lo = sb("z_hi", [P, NR, T], F32R), sb("z_lo", [P, NR, T], F32R)
        out = [ps(f"out{k}") for k in range(QT)]
        gbank, ubank, tbank = [ps("gbank0"), ps("gbank1")], ps("ubank"), ps("tbank")
        loaded_a, loaded_b, loaded_w, loaded_d = (sem(n) for n in ("loaded_a", "loaded_b", "loaded_w", "loaded_d"))
        s_hi_done, s_lo_done, stacked, chain = (sem(n) for n in ("split_hi", "split_lo", "stacked", "chain"))
        t_made, t_read, gated, upped, silued, prodded, summed, z_hi_done, z_ready = (sem(n) for n in (
            "t_made", "t_read", "gated", "upped", "silued", "prodded", "summed", "z_hi_done", "z_ready"))
        t2_made, t2_read, downed, added = (sem(n) for n in ("t2_made", "t2_read", "downed", "added"))
        block = ctx.enter_context(nc.Block())

        splits = [(a_raw[:, :, :], a_hi[:, :, :], a_lo[:, :, :])]
        splits += [(b_raw[:, :], b_hi[:, :], b_lo[:, :]), (e_raw[:, :], e_hi[:, :], e_lo[:, :])]
        NWS = 4
        wc = 2 * FF // NWS
        for k in (0, 2, 1, 3):
            splits.append(tuple(x[:, k * wc:(k + 1) * wc] for x in (w_raw, w_hi, w_lo)))
        splits.append((d_raw[:, 0:2, :], d_hi[:, 0:2, :], d_lo[:, 0:2, :]))
        wl = ROW[2][1]
        splits.append((d_raw[0:wl, 2, :], d_hi[0:wl, 2, :], d_lo[0:wl, 2, :]))
        ALL = len(splits)

        @block.sync
        def _(sp):
            sp.dma_start(a_raw[:, :, :], inp["L0_a13"].rearrange("(k p) n -> p k n", p=P)).then_inc(loaded_a, 16)
            sp.dma_start(b_raw[:, :], inp["L0_b13"]).then_inc(loaded_b, 16)
            sp.dma_start(e_raw[:, :], inp["L0_b2"]).then_inc(loaded_b, 16)
            sp.dma_start(pick[:, :], inp["c_pick"]).then_inc(loaded_b, 16)
            sp.dma_start(w_raw[:, :], inp["L0_w13_t"]).then_inc(loaded_w, 16)
            for r, (at, w) in enumerate(ROW):
                sp.dma_start(d_raw[0:w, r, :], inp["L0_w2_t"][at:at + w, :]).then_inc(loaded_d, 16)
            for n, (at, w) in enumerate(tiles):
                sp.dma_start(a2[0:w, n, :], inp["L0_a2"][at:at + w, :]).then_inc(loaded_d, 16)

        @block.scalar
        def _(act):
            for n, (raw, hi, _) in enumerate(splits):
                if n == 0:
                    act.wait_ge(loaded_a, 16)
                if n == 1:
                    act.wait_ge(loaded_b, 48)
                if n == 3:
                    act.wait_ge(loaded_w, 16)
                if n == ALL - 2:
                    act.wait_ge(loaded_d, 16 * (NR + NM))
                nc.scalar.activation(hi, raw, ACT.Copy).then_inc(s_hi_done, 1)

            def silu(b, n):
                w = tiles[n][1]
                k = NM * b + n
                act.wait_ge(gated, k + 1)
                if k >= 2:
                    act.wait_ge(prodded, k - 1)
                nc.scalar.activation(act_g[0:w, k % 2, :], gbank[k % 2][0:w, :], ACT.Silu).then_inc(silued, 1)

            def z_high(b, r):
                w = ROW[r][1]
                act.wait_ge(summed, 3 * (NR * b + r) + 3)
                if b:
                    act.wait_ge(downed, 1)
                nc.scalar.activation(z_hi[0:w, r, :], quarters[0:w, r % 2, :], ACT.Copy).then_inc(z_hi_done, 1)

            for b in range(B):
                for n in range(NM):
                    silu(b, n)
                    if n % 4 == 1 and n >= 4:
                        z_high(b, n // 4 - 1)
                z_high(b, NR - 1)

        @block.gpsimd
        def _(pool):
            for n, (raw, hi, lo) in enumerate(splits):
                pool.wait_ge(s_hi_done, n + 1)
                nc.gpsimd.tensor_tensor(lo, raw, hi.bitcast(F32), ALU.subtract).then_inc(s_lo_done, 1)

            def add_quarter(b, n):
                k, r, c, w = NM * b + n, n // 4, n % 4, tiles[n][1]
                z = NR * b + r
                pool.wait_ge(prodded, k + 1)
                q = quarters[0:w, r % 2, :]
                if c == 1:
                    if z >= 2:
                        pool.wait_ge(z_ready, z - 1)
                    nc.gpsimd.tensor_tensor(q, prod[0:w, (k - 1) % 3, :], prod[0:w, k % 3, :], ALU.add).then_inc(summed, 1)
                elif c:
                    pool.wait_ge(summed, 3 * z + c - 1)
                    nc.gpsimd.tensor_tensor(q, q, prod[0:w, k % 3, :], ALU.add).then_inc(summed, 1)

            def z_low(b, r):
                z, w = NR * b + r, ROW[r][1]
                pool.wait_ge(z_hi_done, z + 1)
                nc.gpsimd.tensor_tensor(z_lo[0:w, r, :], quarters[0:w, r % 2, :], z_hi[0:w, r, :].bitcast(F32),
                                        ALU.subtract).then_inc(z_ready, 1)

            for b in range(B):
                for n in range(NM):
                    add_quarter(b, n)
                    if n % 4 == 3:
                        z_low(b, n // 4)

        @block.vector
        def _(dve):
            steps = [0]

            def link(ins):
                steps[0] += 1
                ins.then_inc(chain, 1)
                dve.wait_ge(chain, steps[0])

            def stack(to, hi, lo, tmp, cols):
                n = tmp.shape[0]
                link(nc.vector.tensor_scalar(tmp, lo, pick[0:n, cols + 1:cols + 2], None, ALU.mult))
                return nc.vector.scalar_tensor_tensor(to, hi.bitcast(F32), pick[0:n, cols:cols + 1], tmp, ALU.mult, ALU.add)

            dve.wait_ge(s_lo_done, 3)
            stack(b_st[:, :], b_hi[:, :], b_lo[:, :], b_raw[:, :], 2).then_inc(stacked, 1)
            stack(e_st[:, :], e_hi[:, :], e_lo[:, :], e_raw[:, :], 2).then_inc(stacked, 1)

            def t_stack(b):
                dve.wait_ge(t_made, b + 1)
                link(nc.vector.tensor_scalar(t_raw[:, b, :], tbank[0:64, :], 0.5, None, ALU.mult))
                link(nc.vector.tensor_copy(t_hi[:, b, :], t_raw[:, b, :]))
                link(nc.vector.tensor_tensor(t_lo[:, b, :], t_raw[:, b, :], t_hi[:, b, :].bitcast(F32), ALU.subtract))
                stack(t_st[:, b, :], t_hi[:, b, :], t_lo[:, b, :], t_raw[:, b, :], 0).then_inc(t_read, 1)

            def t2_stack(b):
                dve.wait_ge(t2_made, NM * (b + 1))
                link(nc.vector.tensor_scalar(s_raw[:, b, :], tbank[0:S3, :], 0.5, None, ALU.mult))
                link(nc.vector.tensor_copy(s_hi[:, b, :], s_raw[:, b, :]))
                link(nc.vector.tensor_tensor(s_lo[:, b, :], s_raw[:, b, :], s_hi[:, b, :].bitcast(F32), ALU.subtract))
                stack(s_st[:, b, :], s_hi[:, b, :], s_lo[:, b, :], s_raw[:, b, :], 0).then_inc(t2_read, 1)

            def multiply(b, n):
                k, w = NM * b + n, tiles[n][1]
                dve.wait_ge(silued, k + 1)
                dve.wait_ge(upped, k + 1)
                if k >= 3:
                    dve.wait_ge(t2_made, k - 2)
                    j = k - 3
                    done = 3 * (j // 4) + max(j % 4, 1)
                    dve.wait_ge(summed, done)
                nc.vector.tensor_tensor(prod[0:w, k % 3, :], act_g[0:w, k % 2, :], ubank[0:w, :],
                                        ALU.mult).then_inc(prodded, 1)

            t_stack(0)
            t_stack(1)
            for b in range(B):
                for n in range(NM):
                    multiply(b, n)
                    if b and n == 0:
                        for t in range(QT):
                            dve.wait_ge(downed, t + 1)
                            nc.vector.tensor_tensor(m.x[:, t, :], out[t][:, :], m.x[:, t, :], ALU.add).then_inc(added, 1)
                t2_stack(b)
            for t in range(QT):
                dve.wait_ge(downed, QT + t + 1)
                nc.vector.tensor_tensor(m.x[:, QT + t, :], out[t][:, :], m.x[:, QT + t, :], ALU.add).then_inc(added, 1)

        @block.tensor
        def _(pe):
            def three(to, l_hi, l_lo, r_hi, r_lo, start, stop):
                nc.tensor.matmul(to, l_hi, r_hi, start=start, stop=False)
                nc.tensor.matmul(to, l_hi, r_lo, start=False, stop=False)
                return nc.tensor.matmul(to, l_lo, r_hi, start=False, stop=stop)

            pe.wait_ge(s_lo_done, 1)
            for b in range(B):
                if b:
                    pe.wait_ge(t_read, 1)
                tok = slice(b * T, (b + 1) * T)
                for k in range(KT):
                    last = three(tbank[0:64, :], a_hi[:, k, :], a_lo[:, k, :], m.h_hi[:, k, tok], m.h_lo[:, k, tok],
                                 k == 0, k == KT - 1)
                last.then_inc(t_made, 1)

            def up(b, n, second):
                at, w = tiles[n]
                k = NM * b + n
                bank = ubank if second else gbank[k % 2]
                tok = slice(b * T, (b + 1) * T)
                if second and k >= 1:
                    pe.wait_ge(prodded, k)
                if not second and k >= 2:
                    pe.wait_ge(silued, k - 1)
                cols = slice(FF * second + at, FF * second + at + w)
                three(bank[0:w, :], w_hi[:, cols], w_lo[:, cols], m.f_hi[:, tok], m.f_lo[:, tok], True, False)
                rows = slice(32 * second, 32 * second + S3)
                nc.tensor.matmul(bank[0:w, :], b_st[rows, at:at + w], t_st[rows, b, :], start=False,
                                 stop=True).then_inc(upped if second else gated, 1)

            def lora_down(b, n):
                k, w = NM * b + n, tiles[n][1]
                pe.wait_ge(prodded, k + 1)
                if n == 0 and b:
                    pe.wait_ge(t2_read, b)
                nc.tensor.matmul(tbank[0:S3, :], a2[0:w, n, :], prod[0:w, k % 3, :], start=(n == 0),
                                 stop=(n == NM - 1)).then_inc(t2_made, 1)

            def down(b, r):
                w = ROW[r][1]
                pe.wait_ge(z_ready, NR * b + r + 1)
                for t in range(QT):
                    if b and r == 0:
                        pe.wait_ge(added, t + 1)
                    tok = slice(t * P, (t + 1) * P)
                    three(out[t][:, :], z_hi[0:w, r, tok], z_lo[0:w, r, tok], d_hi[0:w, r, :], d_lo[0:w, r, :],
                          r == 0, False)

            pe.wait_ge(t_read, B)
            pe.wait_ge(stacked, 2)
            pe.wait_ge(s_lo_done, 3 + NWS)
            for b in range(B):
                for n in range(NM):
                    up(b, n, 0)
                    up(b, n, 1)
                    if n == 0 and b == 0:
                        pe.wait_ge(s_lo_done, ALL)
                    if n >= 1:
                        lora_down(b, n - 1)
                    if n % 4 == 2 and n >= 4:
                        down(b, n // 4 - 1)
                lora_down(b, NM - 1)
                down(b, NR - 1)
                pe.wait_ge(t2_read, b + 1)
                for t in range(QT):
                    nc.tensor.matmul(out[t][:, :], s_st[:, b, t * P:(t + 1) * P], e_st[:, :], start=False,
                                     stop=True).then_inc(downed, 1)


def feed_forward1(nc, m, inp):
    tiles = [(at, min(P, FF - at)) for at in range(0, FF, P)]
    NM = len(tiles)
    NRAW = 6
    gu_v = inp["L1_gate_up_t"].rearrange("(k p) n -> p k n", p=P)
    with ExitStack() as ctx:
        sb = lambda n, shape, dt=F32: ctx.enter_context(nc.sbuf_tensor(f"f1_{n}", shape, dt))
        ps = lambda n: ctx.enter_context(nc.psum_tensor(f"f1_{n}", [P, 512], F32))
        sem = lambda n: ctx.enter_context(nc.semaphore(f"f1_{n}"))
        raw = sb("raw", [P, NRAW, 512])
        w_hi, w_lo = sb("w_hi", [P, NRAW, 512], F32R), sb("w_lo", [P, NRAW, 512], F32R)
        act_g, prod = sb("act_g", [P, 2, T]), sb("prod", [P, 2, T])
        z_hi, z_lo = sb("z_hi", [P, 2, T], F32R), sb("z_lo", [P, 2, T], F32R)
        out = [ps(f"out{k}") for k in range(QT)]
        gbank, ubank = [ps("gbank0"), ps("gbank1")], [ps("ubank0"), ps("ubank1")]
        loaded = [sem(f"loaded{k}") for k in range(NRAW)]
        w_hi_done, w_ready, gated, upped, silued, prodded, z_hi_done, z_ready, downed, added = (sem(n) for n in (
            "w_hi_done", "w_ready", "gated", "upped", "silued", "prodded", "z_hi_done", "z_ready", "downed", "added"))
        block = ctx.enter_context(nc.Block())
        ALL = B * NM

        def piece(x, s, p):
            w = tiles[s % NM][1]
            slot = (3 * s + p) % NRAW
            if p == 2:
                return x[0:w, slot, :]
            return x[:, slot, 0:KT * w].rearrange("p (k n) -> p k n", k=KT)

        @block.sync
        def _(sp):
            for s in range(ALL):
                at, w = tiles[s % NM]
                for p in range(3):
                    n = 3 * s + p
                    if n >= NRAW:
                        sp.wait_ge(w_ready, n - NRAW + 1)
                    src = inp["L1_down_t"][at:at + w, :] if p == 2 else gu_v[:, :, FF * p + at:FF * p + at + w]
                    sp.dma_start(piece(raw, s, p), src).then_inc(loaded[n % NRAW], 16)

        @block.tensor
        def _(pe):
            def three(to, l_hi, l_lo, r_hi, r_lo, start, stop):
                nc.tensor.matmul(to, l_hi, r_hi, start=start, stop=False)
                nc.tensor.matmul(to, l_hi, r_lo, start=False, stop=False)
                return nc.tensor.matmul(to, l_lo, r_hi, start=False, stop=stop)

            def up(s, p):
                b, w = s // NM, tiles[s % NM][1]
                bank = (gbank, ubank)[p][s % 2]
                pe.wait_ge(w_ready, 3 * s + p + 1)
                if s >= 2:
                    pe.wait_ge((silued, prodded)[p], s - 1)
                hi, lo = piece(w_hi, s, p), piece(w_lo, s, p)
                for k in range(KT):
                    tok = slice(b * T, (b + 1) * T)
                    last = three(bank[0:w, :], hi[:, k, :], lo[:, k, :], m.h_hi[:, k, tok], m.h_lo[:, k, tok],
                                 k == 0, k == KT - 1)
                last.then_inc((gated, upped)[p], 1)

            def down(s):
                b, n, w = s // NM, s % NM, tiles[s % NM][1]
                pe.wait_ge(z_ready, s + 1)
                pe.wait_ge(w_ready, 3 * s + 3)
                hi, lo = piece(w_hi, s, 2), piece(w_lo, s, 2)
                for t in range(QT):
                    if b and n == 0:
                        pe.wait_ge(added, t + 1)
                    tok = slice(t * P, (t + 1) * P)
                    last = three(out[t][:, :], z_hi[0:w, s % 2, tok], z_lo[0:w, s % 2, tok], hi, lo, n == 0, n == NM - 1)
                last.then_inc(downed, 1)

            for s in range(ALL):
                up(s, 0)
                up(s, 1)
                if s >= 1:
                    down(s - 1)
            down(ALL - 1)

        @block.scalar
        def _(act):
            def weights_high(s, p):
                n = 3 * s + p
                act.wait_ge(loaded[n % NRAW], 16 * (n // NRAW + 1))
                if s >= 2:
                    act.wait_ge((gated, upped, downed)[p], s - 1)
                nc.scalar.activation(piece(w_hi, s, p), piece(raw, s, p), ACT.Copy).then_inc(w_hi_done, 1)

            for p in range(3):
                weights_high(0, p)
            for s in range(ALL):
                w = tiles[s % NM][1]
                if s + 1 < ALL:
                    weights_high(s + 1, 0)
                    weights_high(s + 1, 1)
                act.wait_ge(gated, s + 1)
                if s >= 2:
                    act.wait_ge(prodded, s - 1)
                nc.scalar.activation(act_g[0:w, s % 2, :], gbank[s % 2][0:w, :], ACT.Silu).then_inc(silued, 1)
                if s + 1 < ALL:
                    weights_high(s + 1, 2)
                act.wait_ge(prodded, s + 1)
                if s >= 2:
                    act.wait_ge(downed, s - 1)
                nc.scalar.activation(z_hi[0:w, s % 2, :], prod[0:w, s % 2, :], ACT.Copy).then_inc(z_hi_done, 1)

        @block.vector
        def _(dve):
            def add_out(b):
                for t in range(QT):
                    dve.wait_ge(downed, NM * (b + 1))
                    xt = m.x[:, QT * b + t, :]
                    nc.vector.tensor_tensor(xt, out[t][:, :], xt, ALU.add).then_inc(added, 1)

            for s in range(ALL):
                w = tiles[s % NM][1]
                dve.wait_ge(silued, s + 1)
                dve.wait_ge(upped, s + 1)
                if s >= 2:
                    dve.wait_ge(z_ready, s - 1)
                nc.vector.tensor_tensor(prod[0:w, s % 2, :], act_g[0:w, s % 2, :], ubank[s % 2][0:w, :],
                                        ALU.mult).then_inc(prodded, 1)
                dve.wait_ge(z_hi_done, s + 1)
                nc.vector.tensor_tensor(z_lo[0:w, s % 2, :], prod[0:w, s % 2, :], z_hi[0:w, s % 2, :].bitcast(F32),
                                        ALU.subtract).then_inc(z_ready, 1)
                if s == NM:
                    add_out(0)
            add_out(1)

        @block.gpsimd
        def _(pool):
            for s in range(ALL):
                for p in range(3):
                    pool.wait_ge(w_hi_done, 3 * s + p + 1)
                    nc.gpsimd.tensor_tensor(piece(w_lo, s, p), piece(raw, s, p), piece(w_hi, s, p).bitcast(F32),
                                            ALU.subtract).then_inc(w_ready, 1)


def program(nc, inp, out, phases=("attn0", "ffn0", "attn1", "ffn1")):
    with ExitStack() as ctx:
        sb = lambda n, shape, dt=F32: ctx.enter_context(nc.sbuf_tensor(n, shape, dt))
        sem = lambda n: ctx.enter_context(nc.semaphore(n))
        m = Memory()
        m.x = sb("x", [P, NT, D])
        m.ident, m.mask = sb("ident", [P, P]), sb("mask", [P, P])
        m.ident_b, m.mask_b = sb("ident_b", [P, P], BF16), sb("mask_b", [P, P], BF16)
        fetched, fetched0, fetched1, cast, stored = (sem(n) for n in ("fetched", "fetched0", "fetched1", "cast", "stored"))
        x_in = inp["L0_attn_x"].rearrange("b (t p) d -> p (b t) d", p=P)
        x_out = out.rearrange("b (t p) d -> p (b t) d", p=P)

        with nc.Block() as block:
            @block.sync
            def _(sp):
                sp.dma_start(m.ident[:, :], inp["c_ident"]).then_inc(fetched, 16)
                sp.dma_start(m.mask[:, :], inp["c_mask"]).then_inc(fetched, 16)
                sp.dma_start(m.x[:, :, :], x_in).then_inc(fetched, 16)

            @block.vector
            def _(dve):
                dve.wait_ge(fetched, 48)
                nc.vector.tensor_copy(m.ident_b[:, :], m.ident[:, :]).then_inc(cast, 1)
                nc.vector.tensor_copy(m.mask_b[:, :], m.mask[:, :]).then_inc(cast, 1)

        if "attn0" in phases:
            with ExitStack() as scope:
                ssb = lambda n, shape, dt=F32: scope.enter_context(nc.sbuf_tensor(n, shape, dt))
                m.q2 = ssb("q2", [P, NT, NG * HPG, 2, HD0], F32R)
                m.k2 = ssb("k2", [P, NT, NG, 2, 2, HD0], F32R)
                m.vpad = ssb("vpad", [P, NT, NG, 112])
                with ExitStack() as inner:
                    isb = lambda n, shape, dt=F32: inner.enter_context(nc.sbuf_tensor(n, shape, dt))
                    m.h_hi, m.h_lo = isb("h0_hi", [P, KT, NT * P], F32R), isb("h0_lo", [P, KT, NT * P], F32R)
                    m.cos0, m.sin0, m.nsin0 = (isb(n, [P, QT, HD0 // 2]) for n in ("cos0", "sin0", "nsin0"))
                    with nc.Block() as block:
                        @block.sync
                        def _(sp):
                            for to, of in ((m.cos0, "c_cos0"), (m.sin0, "c_sin0"), (m.nsin0, "c_nsin0")):
                                sp.dma_start(to[:, :, :], inp[of]).then_inc(fetched0, 16)
                            sp.wait_ge(fetched0, 48)
                    layer_norm(nc, m, "n0")
                    project0(nc, m, inp["L0_qkv"])
                attend0(nc, m, inp["L0_attn_Wo"])
        if "ffn0" in phases:
            with ExitStack() as scope:
                ssb = lambda n, shape, dt=F32: scope.enter_context(nc.sbuf_tensor(n, shape, dt))
                m.h_hi, m.h_lo = ssb("h2_hi", [P, KT, NT * P], F32R), ssb("h2_lo", [P, KT, NT * P], F32R)
                m.f_hi, m.f_lo = ssb("f_hi", [P, NT * P], F32R), ssb("f_lo", [P, NT * P], F32R)
                layer_norm(nc, m, "n1", folded=True)
                feed_forward0(nc, m, inp)
        if "attn1" in phases:
            with ExitStack() as scope:
                ssb = lambda n, shape, dt=F32: scope.enter_context(nc.sbuf_tensor(n, shape, dt))
                m.h_hi, m.h_lo = ssb("h1_hi", [P, KT, NT * P], F32R), ssb("h1_lo", [P, KT, NT * P], F32R)
                m.cos1, m.sin1 = ssb("cos1", [P, T]), ssb("sin1", [P, T])
                with nc.Block() as block:
                    @block.sync
                    def _(sp):
                        sp.dma_start(m.cos1[:, :], inp["c_cos1"]).then_inc(fetched1, 16)
                        sp.dma_start(m.sin1[:, :], inp["c_sin1"]).then_inc(fetched1, 16)
                        sp.wait_ge(fetched1, 32)
                layer_norm(nc, m, "n2")
                attention1(nc, m, inp["L1_attn_wq"], inp["L1_attn_wk"], inp["L1_attn_wv"], inp["L1_attn_wo"])
        if "ffn1" in phases:
            with ExitStack() as scope:
                ssb = lambda n, shape, dt=F32: scope.enter_context(nc.sbuf_tensor(n, shape, dt))
                m.h_hi, m.h_lo = ssb("h3_hi", [P, KT, NT * P], F32R), ssb("h3_lo", [P, KT, NT * P], F32R)
                layer_norm(nc, m, "n3")
                feed_forward1(nc, m, inp)

        with nc.Block() as block:
            @block.sync
            def _(sp):
                sp.dma_start(x_out, m.x[:, :, :]).then_inc(stored, 16)
                sp.wait_ge(stored, 16)


class Memory:
    pass


def laid_out(inputs):
    import numpy as np

    a = {n: np.asarray(v) for n, v in inputs.items()}
    same = ["L0_attn_x", "L0_attn_Wo", "L1_attn_wq", "L1_attn_wk", "L1_attn_wv", "L1_attn_wo"]
    out = {n: np.ascontiguousarray(a[n]) for n in same}
    out["L0_qkv"] = np.concatenate([a["L0_attn_Wq"], a["L0_attn_Wk"], a["L0_attn_Wv"]], axis=1)
    out["L1_gate_up_t"] = np.ascontiguousarray(a["L1_ffn_w_gate_up"].T)
    out["L1_down_t"] = np.ascontiguousarray(a["L1_ffn_w_down"].T)
    out["L0_w13_t"] = np.ascontiguousarray(np.concatenate([a["L0_ffn_w1q"], a["L0_ffn_w3q"]], axis=0).T)
    out["L0_w2_t"] = np.ascontiguousarray(a["L0_ffn_w2q"].T)

    def stack(first, second, axis):
        shape = list(first.shape)
        shape[axis] = 32 - 3 * R
        gap = np.zeros(shape, first.dtype)
        return np.concatenate([first] * 3 + [gap] + [second] * 3 + [gap], axis=axis)

    out["L0_a13"] = stack(a["L0_ffn_a1"].T, a["L0_ffn_a3"].T, 1)
    out["L0_b13"] = stack(a["L0_ffn_b1"].T, a["L0_ffn_b3"].T, 0)
    out["L0_a2"] = np.concatenate([a["L0_ffn_a2"].T] * 3, axis=1)
    out["L0_b2"] = np.concatenate([a["L0_ffn_b2"].T] * 3, axis=0)
    out.update(constants())
    return out


def constants():
    import numpy as np

    ident = np.eye(P, dtype=np.float32)
    key, query = np.arange(P)[None, :], np.arange(P)[:, None]
    mask = np.where(key > query, np.float32(-1e30), np.float32(0))
    one, lora = np.float32(1), np.arange(32) // R
    rows = np.stack([(lora == 0) | (lora == 2), lora == 1, lora <= 1, lora == 2], axis=1)
    pick = np.concatenate([rows, rows], axis=0) * one
    pos = np.arange(T, dtype=np.float32)
    inv0 = (np.float32(1) / np.float32(500000.0) ** (np.arange(0, HD0, 2, dtype=np.float32) / np.float32(HD0)))
    f0 = (pos[:, None] * inv0.astype(np.float32)[None, :]).astype(np.float32).reshape(QT, P, HD0 // 2).transpose(1, 0, 2)
    inv = 1.0 / 500000.0 ** (np.arange(0, HD1, 2, dtype=np.float64) / HD1)
    wavelen = 2.0 * np.pi / inv
    low_wl, high_wl = 1024 / 1.0, 1024 / 4.0
    smooth = (1024 / wavelen - 1.0) / (4.0 - 1.0)
    scaled = np.where(wavelen > low_wl, inv / 8.0, inv)
    mid = (wavelen <= low_wl) & (wavelen >= high_wl)
    scaled = np.where(mid, (1 - smooth) * inv / 8.0 + smooth * inv, scaled).astype(np.float32)
    f1 = (pos[:, None] * scaled[None, :]).T
    return {
        "c_ident": ident,
        "c_mask": mask,
        "c_pick": pick,
        "c_cos0": np.ascontiguousarray(np.cos(f0)),
        "c_sin0": np.ascontiguousarray(np.sin(f0)),
        "c_nsin0": np.ascontiguousarray(-np.sin(f0)),
        "c_cos1": np.concatenate([np.cos(f1), np.cos(f1)], axis=0),
        "c_sin1": np.concatenate([np.sin(f1), -np.sin(f1)], axis=0),
    }


def kernel(**inputs):
    import concourse.bacc as _bacc
    from concourse import mybir as _mybir
    from concourse.bass_utils import run_bass_kernel_spmd as _run

    nc = _bacc.Bacc("TRN2", target_bir_lowering=False, num_devices=1)
    arrays = laid_out(inputs)
    args = {}
    for name, a in arrays.items():
        args[name] = nc.dram_tensor(f"in_{name}", a.shape, _mybir.dt.from_np(a.dtype), kind="ExternalInput").ap()
    out = nc.dram_tensor("out_0", (B, T, D), _mybir.dt.float32, kind="ExternalOutput").ap()
    program(nc, args, out)
    r = _run(nc, [{f"in_{name}": a for name, a in arrays.items()}], core_ids=[0])
    return r.results[0]["out_0"]
```

```python
from contextlib import ExitStack

import concourse.bass as bass
from concourse import mybir

F32 = mybir.dt.float32
F32R = mybir.dt.float32r
BF16 = mybir.dt.bfloat16
ALU = mybir.AluOpType
ACT = mybir.ActivationFunctionType
AX_X = mybir.AxisListType.X

P = 128
B, T, D = 2, 512, 512
KT = D // P
NT = B * T // P
QT = T // P
NG, HPG = 8, 4
HD0, HD1 = 16, 128
FF = 1376
R = 2
EPS = 1e-5

J_CUM = [0, 1, 3, 6]
J_ALL = 10


def layer_norm(nc, m, name, folded=False):
    with ExitStack() as ctx:
        sb = lambda n, shape, dt=F32: ctx.enter_context(nc.sbuf_tensor(f"{name}_{n}", shape, dt))
        ps = lambda n: ctx.enter_context(nc.psum_tensor(f"{name}_{n}", [P, 512], F32))
        sem = lambda n: ctx.enter_context(nc.semaphore(f"{name}_{n}"))
        stats = sb("stats", [P, NT, 6])
        mv = sb("mv", [P, NT, 2])
        ve = sb("ve", [P, NT])
        sd = sb("sd", [P, NT])
        y0 = sb("y0", [P, NT])
        y1 = sb("y1", [P, NT])
        y2 = sb("y2", [P, NT])
        rstd = sb("rstd", [P, NT])
        row = sb("row", [P, 2, D])
        bank = [ps("bank0"), ps("bank1")]
        if folded:
            quarter = sb("quarter", [P, 2, P])
            fbank = [ps("fbank0"), ps("fbank1")]
            row_made, f_hi_done = sem("row_made"), sem("f_hi_done")
        moments, chain, root, row_ready = sem("moments"), sem("chain"), sem("root"), sem("row_ready")
        turned, hi_done, lo_done = sem("turned"), sem("hi_done"), sem("lo_done")

        block = ctx.enter_context(nc.Block())

        @block.vector
        def _(dve):
            steps = [0]

            def link(ins):
                steps[0] += 1
                ins.then_inc(chain, 1)
                dve.wait_ge(chain, steps[0])

            def low(t):
                dve.wait_ge(hi_done, t + 1)
                nc.vector.tensor_tensor(m.h_lo[:, :, t * P:(t + 1) * P],
                                        bank[t % 2][:, :].rearrange("p (k n) -> p k n", k=KT),
                                        m.h_hi[:, :, t * P:(t + 1) * P].bitcast(F32),
                                        ALU.subtract).then_inc(lo_done, 1)
                if folded:
                    dve.wait_ge(f_hi_done, t + 1)
                    nc.vector.tensor_tensor(m.f_lo[:, t * P:(t + 1) * P], fbank[t % 2][:, 0:P],
                                            m.f_hi[:, t * P:(t + 1) * P].bitcast(F32),
                                            ALU.subtract).then_inc(lo_done, 1)

            for t in range(NT):
                last = nc.vector.bn_stats(stats[:, t, :], m.x[:, t, :])
            link(last)
            for t in range(NT):
                last = nc.vector.bn_aggr(mv[:, t, :], stats[:, t, :])
            link(last)
            nc.vector.tensor_scalar(ve[:, :], mv[:, :, 1], EPS, None, ALU.add).then_inc(moments, 1)
            dve.wait_ge(root, 1)
            link(nc.vector.reciprocal(y0[:, :], sd[:, :]))
            link(nc.vector.tensor_tensor(y1[:, :], y0[:, :], y0[:, :], ALU.mult))
            link(nc.vector.tensor_tensor(y2[:, :], y1[:, :], ve[:, :], ALU.mult))
            link(nc.vector.tensor_scalar(y1[:, :], y2[:, :], -0.5, 1.5, ALU.mult, ALU.add))
            link(nc.vector.tensor_tensor(rstd[:, :], y0[:, :], y1[:, :], ALU.mult))
            for t in range(NT):
                if t >= 2:
                    dve.wait_ge(turned, t - 1)
                made = nc.vector.tensor_scalar(row[:, t % 2, :], m.x[:, t, :], mv[:, t, 0:1], rstd[:, t:t + 1],
                                               ALU.subtract, ALU.mult)
                if folded:
                    made.then_inc(row_made, 1)
                    dve.wait_ge(row_made, t + 1)
                    made = nc.vector.tensor_reduce(quarter[:, t % 2, :],
                                                   row[:, t % 2, :].rearrange("p (k n) -> p n k", k=KT), AX_X, ALU.add)
                made.then_inc(row_ready, 1)
                if t >= 1:
                    low(t - 1)
            low(NT - 1)

        @block.scalar
        def _(act):
            act.wait_ge(moments, 1)
            nc.scalar.activation(sd[:, :], ve[:, :], ACT.Sqrt).then_inc(root, 1)
            for t in range(NT):
                act.wait_ge(turned, t + 1)
                nc.scalar.activation(m.h_hi[:, :, t * P:(t + 1) * P],
                                     bank[t % 2][:, :].rearrange("p (k n) -> p k n", k=KT),
                                     ACT.Copy).then_inc(hi_done, 1)
                if folded:
                    nc.scalar.activation(m.f_hi[:, t * P:(t + 1) * P], fbank[t % 2][:, 0:P],
                                         ACT.Copy).then_inc(f_hi_done, 1)

        @block.tensor
        def _(pe):
            for t in range(NT):
                pe.wait_ge(row_ready, t + 1)
                if t >= 2:
                    pe.wait_ge(lo_done, (2 if folded else 1) * (t - 1))
                for k in range(KT):
                    last = nc.tensor.transpose(bank[t % 2][:, k * P:(k + 1) * P],
                                               row[:, t % 2, k * P:(k + 1) * P], m.ident[:, :])
                if folded:
                    last = nc.tensor.transpose(fbank[t % 2][:, 0:P], quarter[:, t % 2, :], m.ident[:, :])
                last.then_inc(turned, 1)


def attention1(nc, m, wq, wk, wv, wo):
    scale = float(HD1) ** -0.5
    RING = [J_CUM[i] + i for i in range(QT)]
    RING_ALL = J_ALL + QT
    S_BANK0 = [0, 1, 0, 0]
    S_BANKS = [1, 2, 4, 4]
    S_CUM = [0, 1, 3, 7]
    S_ALL = 11
    NC = 6
    V = NC - 1
    NX = NC + 1
    NRAW = 5

    wk_v = wk.rearrange("(k p) n -> p k n", p=P)
    wq_v = wq.rearrange("(k p) n -> p k n", p=P)
    wv_v = wv.rearrange("(k p) n -> p k n", p=P)
    wo_v = wo.rearrange("(h p) n -> h p n", p=P)

    with ExitStack() as ctx:
        sb = lambda n, shape, dt=F32: ctx.enter_context(nc.sbuf_tensor(f"a1_{n}", shape, dt))
        ps = lambda n: ctx.enter_context(nc.psum_tensor(f"a1_{n}", [P, 512], F32))
        sem = lambda n: ctx.enter_context(nc.semaphore(f"a1_{n}"))
        raw_w = sb("raw_w", [P, NRAW, 512])
        w_hi, w_lo = sb("w_hi", [P, NC, KT, P], F32R), sb("w_lo", [P, NC, KT, P], F32R)
        wo_hi, wo_lo = sb("wo_hi", [P, HPG, D], F32R), sb("wo_lo", [P, HPG, D], F32R)
        p_hi, p_lo = sb("p_hi", [P, B, NC, T], F32R), sb("p_lo", [P, B, NC, T], F32R)
        raw_p = sb("raw_p", [P, 2, T])
        rot_a, rot_b = sb("rot_a", [P, 2, T]), sb("rot_b", [P, 2, T])
        prob = [sb("prob0", [P, HPG, 3 * P]), sb("prob1", [P, HPG, 4 * P])]
        pt_hi, pt_lo = sb("pt_hi", [P, 2, 512], F32R), sb("pt_lo", [P, 2, 512], F32R)
        c_hi, c_lo = sb("c_hi", [P, 2, 512], F32R), sb("c_lo", [P, 2, 512], F32R)
        nmax, rsum, rinv = sb("nmax", [P, 2, HPG]), sb("rsum", [P, 2, HPG]), sb("rinv", [P, 2, HPG])
        score = [ps(f"score{k}") for k in range(4)]
        ring = [ps("ring0"), ps("ring1")]
        cbank, xbank = ps("cbank"), ps("xbank")

        loaded = [sem(f"loaded{k}") for k in range(NRAW)]
        scored, ringed, pt_used, x_made = (sem(n) for n in ("scored", "ringed", "pt_used", "x_made"))
        maxed, inverted, normed, ring_read, c_ready, rotated, v_ready = (
            sem(n) for n in ("maxed", "inverted", "normed", "ring_read", "c_ready", "rotated", "v_ready"))
        exped, pt_hi_done, c_hi_done, x_read, p_hi_done, v_hi_done, w_hi_done, wo_hi_done = (sem(n) for n in (
            "exped", "pt_hi_done", "c_hi_done", "x_read", "p_hi_done", "v_hi_done", "w_hi_done", "wo_hi_done"))
        summed, p_ready, w_ready, wo_ready = (sem(n) for n in ("summed", "p_ready", "w_ready", "wo_ready"))

        def piece(g, k):
            return k % NRAW, loaded[k % NRAW], 16 * (10 // NRAW * g + k // NRAW + 1)

        block = ctx.enter_context(nc.Block())

        @block.sync
        def _(sp):
            def load(g, k):
                slot, done, _ = piece(g, k)
                n = 10 * g + k - NRAW
                if n >= 0:
                    if n % 10 < NC:
                        sp.wait_ge(w_ready, NC * (n // 10) + n % 10 + 1)
                    else:
                        sp.wait_ge(wo_ready, HPG * (n // 10) + n % 10 - NC + 1)
                if k == 0:
                    src = wk_v[:, :, g * P:(g + 1) * P]
                elif k == V:
                    src = wv_v[:, :, g * P:(g + 1) * P]
                elif k < V:
                    src = wq_v[:, :, (HPG * g + k - 1) * P:(HPG * g + k) * P]
                else:
                    sp.dma_start(raw_w[:, slot, :], wo_v[HPG * g + k - NC]).then_inc(done, 16)
                    return
                sp.dma_start(raw_w[:, slot, :].rearrange("p (k n) -> p k n", k=KT), src).then_inc(done, 16)

            for g in range(NG):
                for k in range(NC + HPG):
                    load(g, k)

        @block.tensor
        def _(pe):
            def three(out, l_hi, l_lo, r_hi, r_lo, start, stop):
                nc.tensor.matmul(out, l_hi, r_hi, start=start, stop=False)
                nc.tensor.matmul(out, l_hi, r_lo, start=False, stop=False)
                return nc.tensor.matmul(out, l_lo, r_hi, start=False, stop=stop)

            def project(u, c, parts=range(KT)):
                g, b = u // 2, u % 2
                if 0 in parts:
                    pe.wait_ge(w_ready, NC * g + c + 1)
                    if c >= 1:
                        pe.wait_ge(x_read, NC * u + c)
                    elif u >= 1:
                        pe.wait_ge(v_ready, u)
                tok = slice(b * T, (b + 1) * T)
                for k in parts:
                    last = three(xbank[:, :], w_hi[:, c, k, :], w_lo[:, c, k, :], m.h_hi[:, k, tok], m.h_lo[:, k, tok],
                                 k == 0, k == KT - 1)
                if KT - 1 in parts:
                    last.then_inc(x_made, 1)

            def turn_v(u):
                pe.wait_ge(x_read, NC * (u + 1))
                for t in range(QT):
                    last = nc.tensor.transpose(xbank[:, t * P:(t + 1) * P], raw_p[:, V % 2, t * P:(t + 1) * P],
                                               m.ident[:, :])
                last.then_inc(x_made, 1)

            def scores(u, i, bank):
                b, n, per = u % 2, (i + 1) * P, HPG // S_BANKS[i]
                if i == 0:
                    pe.wait_ge(p_ready, 5 * (u + 1))
                before = 16 * u + [-3, -2 + bank, [4, 6, 8, 0][bank], 9 + bank][i]
                if before > 0:
                    pe.wait_ge(exped, before)
                for h in range(bank * per, (bank + 1) * per):
                    out = score[S_BANK0[i] + bank][:, (h % per) * n:(h % per + 1) * n]
                    q = slice(i * P, (i + 1) * P)
                    three(out, p_hi[:, b, 1 + h, q], p_lo[:, b, 1 + h, q], p_hi[:, b, 0, 0:n], p_lo[:, b, 0, 0:n],
                          True, False)
                    last = nc.tensor.matmul(out[:, i * P:n], m.ident_b[:, :], m.mask_b[:, :], start=False, stop=True)
                last.then_inc(scored, 1)

            def turn(u, i, j):
                n = RING_ALL * u + RING[i] + j
                if j == 0:
                    pe.wait_ge(normed, 2 * (QT * u + i + 1))
                if n >= 2:
                    pe.wait_ge(ring_read, n - 1)
                for h in range(HPG):
                    last = nc.tensor.transpose(ring[n % 2][:, h * P:(h + 1) * P],
                                               prob[i % 2][:, h, j * P:(j + 1) * P], m.ident[:, :])
                last.then_inc(ringed, 1)

            def weigh(u, i, j):
                n, b = J_ALL * u + J_CUM[i] + j, u % 2
                pe.wait_ge(ring_read, RING_ALL * u + RING[i] + j + 1)
                if j == 0:
                    if i == 0:
                        pe.wait_ge(v_ready, u + 1)
                    if QT * u + i >= 1:
                        pe.wait_ge(c_ready, QT * u + i)
                v = slice(j * P, (j + 1) * P)
                last = three(cbank[:, :], p_hi[:, b, V, v], p_lo[:, b, V, v], pt_hi[:, n % 2, :], pt_lo[:, n % 2, :],
                             j == 0, j == i)
                last.then_inc(pt_used, 1)

            def out_project(u, i):
                g, n = u // 2, RING_ALL * u + RING[i] + i + 1
                pe.wait_ge(c_ready, QT * u + i + 1)
                pe.wait_ge(ring_read, n - 1)
                for h in range(HPG):
                    if u % 2 == 0 and i == 0:
                        pe.wait_ge(wo_ready, HPG * g + h + 1)
                    last = three(ring[n % 2][:, :], c_hi[:, i % 2, h * P:(h + 1) * P], c_lo[:, i % 2, h * P:(h + 1) * P],
                                 wo_hi[:, h, :], wo_lo[:, h, :], h == 0, h == HPG - 1)
                last.then_inc(ringed, 1)

            for c in range(NC):
                project(0, c)
            scores(0, 0, 0)
            turn_v(0)
            for u in range(2 * NG):
                more = u + 1 < 2 * NG
                turn(u, 0, 0)
                scores(u, 1, 0)
                scores(u, 1, 1)
                if more:
                    project(u + 1, 0)
                weigh(u, 0, 0)
                if more:
                    project(u + 1, 1)
                out_project(u, 0)
                turn(u, 1, 0)
                scores(u, 2, 0)
                turn(u, 1, 1)
                if more:
                    project(u + 1, 2)
                weigh(u, 1, 0)
                scores(u, 2, 1)
                weigh(u, 1, 1)
                scores(u, 2, 2)
                scores(u, 2, 3)
                if more:
                    project(u + 1, 3)
                out_project(u, 1)
                turn(u, 2, 0)
                scores(u, 3, 0)
                turn(u, 2, 1)
                weigh(u, 2, 0)
                turn(u, 2, 2)
                scores(u, 3, 1)
                weigh(u, 2, 1)
                scores(u, 3, 2)
                weigh(u, 2, 2)
                scores(u, 3, 3)
                if more:
                    project(u + 1, 4)
                out_project(u, 2)
                turn(u, 3, 0)
                if more:
                    project(u + 1, V, [0])
                turn(u, 3, 1)
                weigh(u, 3, 0)
                turn(u, 3, 2)
                if more:
                    project(u + 1, V, [1])
                weigh(u, 3, 1)
                turn(u, 3, 3)
                if more:
                    scores(u + 1, 0, 0)
                weigh(u, 3, 2)
                weigh(u, 3, 3)
                if more:
                    project(u + 1, V, [2, 3])
                out_project(u, 3)
                if more:
                    turn_v(u + 1)

        @block.vector
        def _(dve):
            def maxima(u, i, banks):
                per, n = HPG // S_BANKS[i], (i + 1) * P
                for k in banks:
                    dve.wait_ge(scored, S_ALL * u + S_CUM[i] + k + 1)
                    if k == 0 and QT * u + i >= 2:
                        dve.wait_ge(exped, 16 * u + 4 * i - 4)
                    nc.vector.tensor_reduce(nmax[:, i % 2, k * per:(k + 1) * per],
                                            score[S_BANK0[i] + k][:, 0:per * n].rearrange("p (h n) -> p h n", h=per),
                                            AX_X, ALU.max, negate=True).then_inc(maxed, 1)

            def normalise(u, i):
                for pair in range(2):
                    dve.wait_ge(exped, 16 * u + 4 * i + 2 * (pair + 1))
                    heads = slice(2 * pair, 2 * pair + 2)
                    nc.vector.reciprocal(rinv[:, i % 2, heads], rsum[:, i % 2, heads]).then_inc(inverted, 1)
                    dve.wait_ge(inverted, 2 * (QT * u + i) + pair + 1)
                    for h in (2 * pair, 2 * pair + 1):
                        pr = prob[i % 2][:, h, 0:(i + 1) * P]
                        last = nc.vector.tensor_scalar(pr, pr, rinv[:, i % 2, h:h + 1], None, ALU.mult)
                    last.then_inc(normed, 1)

            def low(u, i, j):
                n = J_ALL * u + J_CUM[i] + j
                dve.wait_ge(pt_hi_done, n + 1)
                nc.vector.tensor_tensor(pt_lo[:, n % 2, :], ring[(RING[i] + j) % 2][:, :],
                                        pt_hi[:, n % 2, :].bitcast(F32), ALU.subtract).then_inc(ring_read, 1)

            def head_low(u, i):
                dve.wait_ge(c_hi_done, QT * u + i + 1)
                nc.vector.tensor_tensor(c_lo[:, i % 2, :], cbank[:, :], c_hi[:, i % 2, :].bitcast(F32),
                                        ALU.subtract).then_inc(c_ready, 1)

            def rotate(u, c):
                dve.wait_ge(x_read, NC * u + c + 1)
                n = 5 * u + c
                if n >= 2:
                    dve.wait_ge(p_ready, 5 * u + (c - 1 if c >= 2 else -c))
                r = raw_p[:, c % 2, :]
                nc.vector.tensor_tensor(rot_a[:, c % 2, :], r, m.cos1[:, :], ALU.mult)
                nc.vector.tensor_tensor(rot_b[0:64, c % 2, :], raw_p[64:128, c % 2, :], m.sin1[64:128, :], ALU.mult)
                nc.vector.tensor_tensor(rot_b[64:128, c % 2, :], raw_p[0:64, c % 2, :], m.sin1[0:64, :],
                                        ALU.mult).then_inc(rotated, 1)

            def v_low(u):
                dve.wait_ge(v_hi_done, u + 1)
                nc.vector.tensor_tensor(p_lo[:, u % 2, V, :], xbank[:, :], p_hi[:, u % 2, V, :].bitcast(F32),
                                        ALU.subtract).then_inc(v_ready, 1)

            def add_out(u, i):
                n = RING_ALL * u + RING[i] + i + 1
                dve.wait_ge(ringed, n + 1)
                xt = m.x[:, (u % 2) * QT + i, :]
                nc.vector.tensor_tensor(xt, ring[n % 2][:, :], xt, ALU.add).then_inc(ring_read, 1)

            for c in range(V):
                rotate(0, c)
            maxima(0, 0, [0])
            normalise(0, 0)
            v_low(0)
            for u in range(2 * NG):
                more = u + 1 < 2 * NG
                low(u, 0, 0)
                maxima(u, 1, [0, 1])
                normalise(u, 1)
                head_low(u, 0)
                if more:
                    rotate(u + 1, 0)
                    rotate(u + 1, 1)
                add_out(u, 0)
                low(u, 1, 0)
                maxima(u, 2, [0])
                low(u, 1, 1)
                maxima(u, 2, [1])
                if more:
                    rotate(u + 1, 2)
                head_low(u, 1)
                maxima(u, 2, [2, 3])
                normalise(u, 2)
                if more:
                    rotate(u + 1, 3)
                add_out(u, 1)
                low(u, 2, 0)
                maxima(u, 3, [0])
                low(u, 2, 1)
                low(u, 2, 2)
                maxima(u, 3, [1, 2])
                head_low(u, 2)
                maxima(u, 3, [3])
                normalise(u, 3)
                if more:
                    rotate(u + 1, 4)
                add_out(u, 2)
                for j in range(QT):
                    low(u, 3, j)
                if more:
                    maxima(u + 1, 0, [0])
                head_low(u, 3)
                if more:
                    normalise(u + 1, 0)
                add_out(u, 3)
                if more:
                    v_low(u + 1)

        @block.scalar
        def _(act):
            def exponentials(u, i, heads):
                per = HPG // S_BANKS[i]
                for h in heads:
                    act.wait_ge(maxed, S_ALL * u + S_CUM[i] + h // per + 1)
                    if h == 0 and QT * u + i >= 2:
                        s = QT * u + i - 2
                        act.wait_ge(ringed, RING_ALL * (s // QT) + RING[s % QT] + s % QT + 1)
                    n = (i + 1) * P
                    nc.scalar.activation(prob[i % 2][:, h, 0:n],
                                         score[S_BANK0[i] + h // per][:, (h % per) * n:(h % per + 1) * n], ACT.Exp,
                                         bias=nmax[:, i % 2, h:h + 1], accum_out=rsum[:, i % 2, h:h + 1],
                                         ).then_inc(exped, 1)

            def high(u, i, j):
                n = J_ALL * u + J_CUM[i] + j
                act.wait_ge(ringed, RING_ALL * u + RING[i] + j + 1)
                if n >= 2:
                    act.wait_ge(pt_used, n - 1)
                nc.scalar.activation(pt_hi[:, n % 2, :], ring[(RING[i] + j) % 2][:, :], ACT.Copy).then_inc(pt_hi_done, 1)

            def head_high(u, i):
                act.wait_ge(pt_used, J_ALL * u + J_CUM[i] + i + 1)
                if QT * u + i >= 2:
                    s = QT * u + i - 2
                    act.wait_ge(ringed, RING_ALL * (s // QT) + RING[s % QT] + s % QT + 2)
                nc.scalar.activation(c_hi[:, i % 2, :], cbank[:, :], ACT.Copy).then_inc(c_hi_done, 1)

            def read_out(u, c):
                act.wait_ge(x_made, NX * u + c + 1)
                if c >= 2:
                    act.wait_ge(rotated, 5 * u + c - 1)
                elif u >= 1:
                    act.wait_ge((rotated, x_made)[c], (5 * u, NX * u)[c])
                nc.scalar.activation(raw_p[:, c % 2, :], xbank[:, :], ACT.Copy,
                                     scale=scale if 1 <= c < V else 1.0).then_inc(x_read, 1)

            def part_high(u, c):
                act.wait_ge(summed, 5 * u + c + 1)
                nc.scalar.activation(p_hi[:, u % 2, c, :], rot_a[:, c % 2, :], ACT.Copy).then_inc(p_hi_done, 1)

            def v_high(u):
                act.wait_ge(x_made, NX * (u + 1))
                nc.scalar.activation(p_hi[:, u % 2, V, :], xbank[:, :], ACT.Copy).then_inc(v_hi_done, 1)

            def weights_high(g, c):
                slot, done, count = piece(g, c)
                act.wait_ge(done, count)
                if g >= 1:
                    act.wait_ge(x_made, NX * (2 * g - 1) + c + 1)
                nc.scalar.activation(w_hi[:, c, :, :], raw_w[:, slot, :].rearrange("p (k n) -> p k n", k=KT),
                                     ACT.Copy).then_inc(w_hi_done, 1)

            def out_weights_high(u, heads):
                if u % 2:
                    return
                g = u // 2
                for h in heads:
                    slot, done, count = piece(g, NC + h)
                    act.wait_ge(done, count)
                    if g >= 1:
                        act.wait_ge(ringed, RING_ALL * 2 * g)
                    nc.scalar.activation(wo_hi[:, h, :], raw_w[:, slot, :], ACT.Copy).then_inc(wo_hi_done, 1)

            for c in range(NC):
                weights_high(0, c)
                if c >= 1:
                    read_out(0, c - 1)
                if c >= 2:
                    part_high(0, c - 2)
            read_out(0, V)
            part_high(0, V - 1)
            exponentials(0, 0, range(HPG))
            out_weights_high(0, [0])
            v_high(0)
            for u in range(2 * NG):
                g, more = u // 2, u + 1 < 2 * NG
                split = u % 2 == 0 and g + 1 < NG
                high(u, 0, 0)
                out_weights_high(u, [1])
                exponentials(u, 1, range(HPG))
                out_weights_high(u, [2])
                if more:
                    read_out(u + 1, 0)
                out_weights_high(u, [3])
                head_high(u, 0)
                if more:
                    read_out(u + 1, 1)
                    part_high(u + 1, 0)
                high(u, 1, 0)
                high(u, 1, 1)
                exponentials(u, 2, [0])
                if more:
                    part_high(u + 1, 1)
                    read_out(u + 1, 2)
                exponentials(u, 2, [1])
                head_high(u, 1)
                exponentials(u, 2, [2, 3])
                if more:
                    part_high(u + 1, 2)
                    read_out(u + 1, 3)
                if split:
                    weights_high(g + 1, 0)
                    weights_high(g + 1, 1)
                high(u, 2, 0)
                high(u, 2, 1)
                if more:
                    part_high(u + 1, 3)
                exponentials(u, 3, [0])
                high(u, 2, 2)
                exponentials(u, 3, [1, 2])
                head_high(u, 2)
                exponentials(u, 3, [3])
                if more:
                    read_out(u + 1, 4)
                if split:
                    weights_high(g + 1, 2)
                    weights_high(g + 1, 3)
                high(u, 3, 0)
                high(u, 3, 1)
                if more:
                    part_high(u + 1, 4)
                high(u, 3, 2)
                high(u, 3, 3)
                if more:
                    exponentials(u + 1, 0, range(HPG))
                head_high(u, 3)
                if more:
                    read_out(u + 1, V)
                if split:
                    weights_high(g + 1, 4)
                    weights_high(g + 1, 5)
                if more:
                    out_weights_high(u + 1, [0])
                    v_high(u + 1)

        @block.gpsimd
        def _(pool):
            def part_sum(u, c):
                pool.wait_ge(rotated, 5 * u + c + 1)
                nc.gpsimd.tensor_tensor(rot_a[:, c % 2, :], rot_a[:, c % 2, :], rot_b[:, c % 2, :],
                                        ALU.add).then_inc(summed, 1)

            def part_low(u, c):
                pool.wait_ge(p_hi_done, 5 * u + c + 1)
                nc.gpsimd.tensor_tensor(p_lo[:, u % 2, c, :], rot_a[:, c % 2, :], p_hi[:, u % 2, c, :].bitcast(F32),
                                        ALU.subtract).then_inc(p_ready, 1)

            def weights_low(g, c):
                pool.wait_ge(w_hi_done, NC * g + c + 1)
                nc.gpsimd.tensor_tensor(w_lo[:, c, :, :], raw_w[:, piece(g, c)[0], :].rearrange("p (k n) -> p k n", k=KT),
                                        w_hi[:, c, :, :].bitcast(F32), ALU.subtract).then_inc(w_ready, 1)

            def out_weights_low(g):
                for h in range(HPG):
                    pool.wait_ge(wo_hi_done, HPG * g + h + 1)
                    nc.gpsimd.tensor_tensor(wo_lo[:, h, :], raw_w[:, piece(g, NC + h)[0], :],
                                            wo_hi[:, h, :].bitcast(F32), ALU.subtract).then_inc(wo_ready, 1)

            for c in range(NC):
                weights_low(0, c)
                if c >= 2:
                    part_sum(0, c - 2)
                    part_low(0, c - 2)
            part_sum(0, V - 1)
            part_low(0, V - 1)
            for u in range(2 * NG):
                g, more = u // 2, u + 1 < 2 * NG
                split = u % 2 == 0 and g + 1 < NG
                if u % 2 == 0:
                    out_weights_low(g)
                for c in range(V):
                    if more:
                        part_sum(u + 1, c)
                        part_low(u + 1, c)
                    if split and c >= 2:
                        weights_low(g + 1, 2 * (c - 2))
                        weights_low(g + 1, 2 * (c - 2) + 1)


def project0(nc, m, wqkv):
    NQ, NKV = NG * HPG, NG
    QW, KW = NQ * HD0, NKV * HD0
    W = QW + 2 * KW
    half = HD0 // 2
    w_v = wqkv.rearrange("(k p) n -> p k n", p=P)

    def twice(x):
        n = x.shape[1] // HD0
        return x.rearrange("p (h n) -> p h n", n=HD0).unsqueeze(2).to_broadcast([P, n, 2, HD0])

    with ExitStack() as ctx:
        sb = lambda n, shape, dt=F32: ctx.enter_context(nc.sbuf_tensor(f"p0_{n}", shape, dt))
        ps = lambda n: ctx.enter_context(nc.psum_tensor(f"p0_{n}", [P, 512], F32))
        sem = lambda n: ctx.enter_context(nc.semaphore(f"p0_{n}"))
        raw_w = sb("raw_w", [P, 2, W])
        w_hi, w_lo = sb("w_hi", [P, KT, W], F32R), sb("w_lo", [P, KT, W], F32R)
        row, rot_a, rot_b = (sb(n, [P, 2, QW + KW]) for n in ("row", "rot_a", "rot_b"))
        qbank, kvbank = [ps("qbank0"), ps("qbank1")], [ps("kvbank0"), ps("kvbank1")]
        loaded = [sem("loaded0"), sem("loaded1")]
        w_hi_done, w_ready, v_ready, made, read, rotated, summed, hi_done, q_ready, k_ready = (sem(n) for n in (
            "w_hi_done", "w_ready", "v_ready", "made", "read", "rotated", "summed", "hi_done", "q_ready", "k_ready"))
        block = ctx.enter_context(nc.Block())

        @block.sync
        def _(sp):
            for k in range(KT):
                if k >= 2:
                    sp.wait_ge(w_ready, k - 1)
                sp.dma_start(raw_w[:, k % 2, :], w_v[:, k, :]).then_inc(loaded[k % 2], 16)

        @block.tensor
        def _(pe):
            for t in range(NT):
                if t >= 2:
                    pe.wait_ge(read, 3 * (t - 1))
                    pe.wait_ge(v_ready, t)
                for bank, cols in ((qbank, slice(0, QW)), (kvbank, slice(QW, W))):
                    n = cols.stop - cols.start
                    for k in range(KT):
                        if t == 0:
                            pe.wait_ge(w_ready, k + 1)
                        h = slice(t * P, (t + 1) * P)
                        out = bank[t % 2][:, 0:n]
                        nc.tensor.matmul(out, m.h_hi[:, k, h], w_hi[:, k, cols], start=(k == 0), stop=False)
                        nc.tensor.matmul(out, m.h_hi[:, k, h], w_lo[:, k, cols], start=False, stop=False)
                        last = nc.tensor.matmul(out, m.h_lo[:, k, h], w_hi[:, k, cols], start=False, stop=(k == KT - 1))
                    last.then_inc(made, 1)

        @block.scalar
        def _(act):
            def high(t):
                act.wait_ge(summed, t + 1)
                r = rot_a[:, t % 2, :]
                nc.scalar.activation(m.q2[:, t, :, 0:4:2, :], twice(r[:, 0:QW]), ACT.Copy).then_inc(hi_done, 1)
                nc.scalar.activation(m.k2[:, t, :, 0:2, :], twice(r[:, QW:QW + KW]), ACT.Copy).then_inc(hi_done, 1)

            for k in range(KT):
                act.wait_ge(loaded[k % 2], 16 * (k // 2 + 1))
                nc.scalar.activation(w_hi[:, k, :], raw_w[:, k % 2, :], ACT.Copy).then_inc(w_hi_done, 1)
            for t in range(NT):
                if t >= 2:
                    act.wait_ge(rotated, t - 1)
                act.wait_ge(made, 2 * t + 1)
                nc.scalar.activation(row[:, t % 2, 0:QW], qbank[t % 2][:, :], ACT.Copy,
                                     scale=float(HD0) ** -0.5).then_inc(read, 1)
                act.wait_ge(made, 2 * t + 2)
                nc.scalar.activation(row[:, t % 2, QW:QW + KW], kvbank[t % 2][:, 0:KW], ACT.Copy).then_inc(read, 1)
                nc.scalar.activation(m.vw[:, t, :, :, 0:HD0], twice(kvbank[t % 2][:, KW:2 * KW]), ACT.Copy).then_inc(read, 1)
                if t >= 1:
                    high(t - 1)
            high(NT - 1)

        @block.vector
        def _(dve):
            def low(t):
                dve.wait_ge(hi_done, 2 * t + 2)
                nc.vector.tensor_tensor(m.q2[:, t, :, 1:4:2, :], twice(rot_a[:, t % 2, 0:QW]),
                                        m.q2[:, t, :, 0:4:2, :].bitcast(F32), ALU.subtract).then_inc(q_ready, 1)

            for t in range(NT):
                nc.vector.memset(m.vw[:, t, :, :, HD0:HD0 + 1].bitcast(F32), 1.0)
            nc.vector.memset(m.vw[:, :, :, 1, HD0 + 1:2 * HD0 + 1].bitcast(F32), 0.0).then_inc(v_ready, 1)
            for t in range(NT):
                dve.wait_ge(read, 3 * t + 3)
                nc.vector.tensor_tensor(m.vw[:, t, :, 0, HD0 + 1:2 * HD0 + 1],
                                        kvbank[t % 2][:, KW:2 * KW].rearrange("p (g n) -> p g n", n=HD0),
                                        m.vw[:, t, :, 0, 0:HD0].bitcast(F32), ALU.subtract).then_inc(v_ready, 1)
                if t >= 2:
                    dve.wait_ge(k_ready, t - 1)
                    dve.wait_ge(q_ready, t - 1)
                table = lambda x, n: x[:, t % QT, :].unsqueeze(1).to_broadcast([P, n, half])
                heads = (QW + KW) // HD0
                nc.vector.tensor_tensor(rot_a[:, t % 2, :].rearrange("p (h n) -> p h n", n=half),
                                        row[:, t % 2, :].rearrange("p (h n) -> p h n", n=half),
                                        table(m.cos0, 2 * heads), ALU.mult)
                src = row[:, t % 2, :].rearrange("p (h s n) -> p h s n", s=2, n=half)
                dst = rot_b[:, t % 2, :].rearrange("p (h s n) -> p h s n", s=2, n=half)
                nc.vector.tensor_tensor(dst[:, :, 0, :], src[:, :, 1, :], table(m.nsin0, heads), ALU.mult)
                nc.vector.tensor_tensor(dst[:, :, 1, :], src[:, :, 0, :], table(m.sin0, heads),
                                        ALU.mult).then_inc(rotated, 1)
                if t >= 1:
                    low(t - 1)
            low(NT - 1)

        @block.gpsimd
        def _(pool):
            for k in range(KT):
                pool.wait_ge(w_hi_done, k + 1)
                nc.gpsimd.tensor_tensor(w_lo[:, k, :], raw_w[:, k % 2, :], w_hi[:, k, :].bitcast(F32),
                                        ALU.subtract).then_inc(w_ready, 1)
            for t in range(NT):
                pool.wait_ge(rotated, t + 1)
                nc.gpsimd.tensor_tensor(rot_a[:, t % 2, :], rot_a[:, t % 2, :], rot_b[:, t % 2, :],
                                        ALU.add).then_inc(summed, 1)
                pool.wait_ge(hi_done, 2 * t + 2)
                nc.gpsimd.tensor_tensor(m.k2[:, t, :, 2:4, :], twice(rot_a[:, t % 2, QW:QW + KW]),
                                        m.k2[:, t, :, 0:2, :].bitcast(F32), ALU.subtract).then_inc(k_ready, 1)


def attend0(nc, m, wo):
    wo_v = wo.rearrange("(k p) n -> p k n", p=P)
    TICKS = J_ALL
    S_BANKS = [1, 2, 4, 4]
    S_CUM = [0, 1, 3, 7]
    S_ALL = 11
    NS = 3
    TU = 1 + QT
    NE, NP = 3, 5
    TURN = {1: (1, 0), 2: (1, 1), 4: (1, 2), 5: (1, 3), 7: (1, 4)}
    SCORE = {4: [(1, 0, 0)], 6: [(1, 1, 0), (1, 1, 1)], 7: [(1, 2, 0)], 8: [(1, 2, 1), (1, 2, 2)],
             9: [(1, 2, 3)], 0: [(0, 3, 0), (0, 3, 1)], 1: [(0, 3, 2)], 2: [(0, 3, 3)]}
    SHIFT = {6: (1, 0), 8: (1, 1), 0: (0, 2), 3: (0, 3)}
    AHEAD = 2
    BEHIND = 2
    LAST = [J_CUM[i] + i + BEHIND for i in range(QT)]
    END = {k % TICKS: (-(k // TICKS), i) for i, k in enumerate(LAST)}
    BACK = {(k + 2) % TICKS: (-((k + 2) // TICKS), i) for i, k in enumerate(LAST)}
    V1 = HD0 + 1
    VW = HD0 + V1
    S64 = slice(64, 64 + 2 * HPG)

    def pair(mm):
        k = mm % TICKS
        i = max(i for i in range(QT) if J_CUM[i] <= k)
        return mm // TICKS, i, k - J_CUM[i]

    def planned(table, u, k):
        if k not in table:
            return []
        entries = table[k] if isinstance(table[k], list) else [table[k]]
        return [(u + e[0],) + e[1:] for e in entries if 0 <= u + e[0] < 2 * NG]

    ticks = [(u, k) for u in range(-1, 2 * NG + 1) for k in range(TICKS)]

    with ExitStack() as ctx:
        sb = lambda n, shape, dt=F32: ctx.enter_context(nc.sbuf_tensor(f"a0_{n}", shape, dt))
        ps = lambda n: ctx.enter_context(nc.psum_tensor(f"a0_{n}", [P, 512], F32))
        sem = lambda n: ctx.enter_context(nc.semaphore(f"a0_{n}"))
        raw_wo = sb("raw_wo", [P, KT, D])
        wo_hi, wo_lo = sb("wo_hi", [P, KT, D], F32R), sb("wo_lo", [P, KT, D], F32R)
        k_rows = sb("k_rows", [P, B, T], F32R)
        q_rows = sb("q_rows", [P, QT, HPG, P], F32R)
        nmax = sb("nmax", [P, QT, HPG])
        split = sb("split", [P, P])
        prob = sb("prob", [P, NE, 512])
        p_hi, p_lo = sb("p_hi", [P, NP, 512], F32R), sb("p_lo", [P, NP, 512], F32R)
        head_t = sb("head_t", [P, 2, 512])
        rsum, head_sum = sb("rsum", [P, 2, HPG]), sb("head_sum", [P, 2, HPG, HD0])
        head = sb("head", [P, NT, NG * HPG, HD0])
        c_hi, c_lo = sb("c_hi", [P, 2, KT, P], F32R), sb("c_lo", [P, 2, KT, P], F32R)
        score = [ps(f"score{k}") for k in range(NS)]
        turned = [ps("turned0"), ps("turned1")]
        qkbank, hbank, cbank = ps("qkbank"), ps("hbank"), ps("cbank")
        loaded, ones_set, split_set = sem("loaded"), sem("ones_set"), sem("split_set")
        qk_turned, scored, t_scored, weighed, shifted, backed = (sem(n) for n in (
            "qk_turned", "scored", "t_scored", "weighed", "shifted", "backed"))
        maxed, parted, max_rows, c_read, divided, head_ready = (sem(n) for n in (
            "maxed", "parted", "max_rows", "c_read", "divided", "head_ready"))
        qk_read, exped, p_hi_done, p_ready = (sem(n) for n in ("qk_read", "exped", "p_hi_done", "p_ready"))
        wo_hi_done, wo_ready, c_turned, c_hi_done, c_ready, projected, added = (sem(n) for n in (
            "wo_hi_done", "wo_ready", "c_turned", "c_hi_done", "c_ready", "projected", "added"))
        block = ctx.enter_context(nc.Block())

        @block.sync
        def _(sp):
            sp.dma_start(raw_wo[:, :, :], wo_v).then_inc(loaded, 16)

        @block.tensor
        def _(pe):
            count = {"turned": 0, "shifted": 0}

            def wait_qkbank():
                if count["turned"]:
                    pe.wait_ge(qk_read, count["turned"])
                if count["shifted"]:
                    pe.wait_ge(max_rows, count["shifted"])

            def turn_qk(u, s):
                wait_qkbank()
                for r in range(QT):
                    g, b = u // 2, u % 2
                    if s == 0:
                        x = m.k2[:, b * QT + r, g, :, :]
                    else:
                        x = m.q2[:, b * QT + s - 1, HPG * g + r, :, :]
                    last = nc.tensor.transpose(qkbank[0:64, r * P:(r + 1) * P],
                                               x.bitcast(F32).rearrange("p s n -> p (s n)"), m.ident[:, :])
                last.then_inc(qk_turned, 1)
                count["turned"] += 1

            def scores(u, i, bank):
                per, n, e = HPG // S_BANKS[i], (i + 1) * P, S_ALL * u + S_CUM[i] + bank
                pe.wait_ge(qk_read, TU * u + i + 2)
                if e >= NS:
                    pe.wait_ge(maxed, e - NS + 1)
                out = score[e % NS]
                for h in range(per):
                    nc.tensor.matmul(out[:, h * n:(h + 1) * n], q_rows[0:64, i, bank * per + h, :],
                                     k_rows[0:64, u % 2, 0:n], start=(h == 0), stop=False)
                diagonal = out[:, 0:per * n].rearrange("p (h n) -> p h n", h=per)[:, :, i * P:n]
                nc.tensor.matmul(diagonal, m.ident_b[:, :], m.mask_b[:, :].unsqueeze(1).to_broadcast([P, per, P]),
                                 start=False, stop=True).then_inc(scored, 1)

            def turned_scores(mm):
                u, i, j = pair(mm)
                if j == 0:
                    pe.wait_ge(max_rows, QT * u + i + 1)
                if mm == 0:
                    pe.wait_ge(ones_set, 1)
                if mm >= 2:
                    pe.wait_ge(exped, mm - 1)
                out = turned[mm % 2][:, :].rearrange("p (h n) -> p h n", h=HPG)
                last = nc.tensor.matmul(out, k_rows[0:S64.stop, u % 2, j * P:(j + 1) * P], q_rows[0:S64.stop, i, :, :],
                                        start=True, stop=(j < i))
                if j == i:
                    last = nc.tensor.matmul(out, m.ident_b[:, :], m.mask_t_b[:, :].unsqueeze(1).to_broadcast([P, HPG, P]),
                                            start=False, stop=True)
                last.then_inc(t_scored, 1)

            def weigh(mm):
                u, i, j = pair(mm)
                pe.wait_ge(p_ready, mm + 1)
                if j == 0 and QT * u + i >= 1:
                    pe.wait_ge(c_read, QT * u + i)
                v = m.vw[:, (u % 2) * QT + j, u // 2, :, :]
                nc.tensor.matmul(cbank[0:VW, :], v[:, 0, :], p_hi[:, mm % NP, :], start=(j == 0), stop=False)
                nc.tensor.matmul(cbank[0:VW, :], v[:, 1, :], p_lo[:, mm % NP, :], start=False,
                                 stop=(j == i)).then_inc(weighed, 1)

            def shift_maxima(u, i):
                pe.wait_ge(parted, 2 * (QT * u + i + 1))
                wait_qkbank()
                nc.tensor.transpose(qkbank[:, 0:P], split[:, :], m.ident[:, :]).then_inc(shifted, 1)
                count["shifted"] += 1

            def turn_back(u, i):
                n = QT * u + i
                pe.wait_ge(c_read, n + 1)
                if n >= 1:
                    pe.wait_ge(divided, 3 * n)
                for h in range(HPG):
                    last = nc.tensor.transpose(hbank[:, h * VW:(h + 1) * VW], head_t[0:VW, n % 2, h * P:(h + 1) * P],
                                               m.ident[0:VW, 0:VW])
                last.then_inc(backed, 1)

            for u, k in ticks:
                mm = TICKS * u + k
                for step in planned(BACK, u, k):
                    turn_back(*step)
                for item in planned(SCORE, u, k):
                    scores(*item)
                if 0 <= mm - BEHIND < TICKS * 2 * NG:
                    weigh(mm - BEHIND)
                for step in planned(SHIFT, u, k):
                    shift_maxima(*step)
                if 0 <= mm + AHEAD < TICKS * 2 * NG:
                    turned_scores(mm + AHEAD)
                for item in planned(TURN, u, k):
                    turn_qk(*item)

            def turn_tile(t):
                pe.wait_ge(head_ready, QT * 2 * NG)
                if t >= 2:
                    pe.wait_ge(c_ready, t - 1)
                for k in range(KT):
                    heads = slice(k * P // HD0, (k + 1) * P // HD0)
                    last = nc.tensor.transpose(turned[t % 2][:, k * P:(k + 1) * P],
                                               head[:, t, heads, :].rearrange("p h n -> p (h n)"), m.ident[:, :])
                last.then_inc(c_turned, 1)

            turn_tile(0)
            for t in range(NT):
                if t + 1 < NT:
                    turn_tile(t + 1)
                pe.wait_ge(c_ready, t + 1)
                if t == 0:
                    pe.wait_ge(wo_ready, KT)
                    pe.wait_ge(maxed, S_ALL * 2 * NG)
                if t >= NS:
                    pe.wait_ge(added, t - NS + 1)
                for k in range(KT):
                    out = score[t % NS][:, :]
                    nc.tensor.matmul(out, c_hi[:, t % 2, k, :], wo_hi[:, k, :], start=(k == 0), stop=False)
                    nc.tensor.matmul(out, c_hi[:, t % 2, k, :], wo_lo[:, k, :], start=False, stop=False)
                    last = nc.tensor.matmul(out, c_lo[:, t % 2, k, :], wo_hi[:, k, :], start=False, stop=(k == KT - 1))
                last.then_inc(projected, 1)

        @block.vector
        def _(dve):
            def maxima(u, i, bank):
                per, n, e = HPG // S_BANKS[i], (i + 1) * P, S_ALL * u + S_CUM[i] + bank
                dve.wait_ge(scored, e + 1)
                nc.vector.tensor_reduce(nmax[:, i, bank * per:(bank + 1) * per],
                                        score[e % NS][:, 0:per * n].rearrange("p (h n) -> p h n", h=per),
                                        AX_X, ALU.max, negate=True).then_inc(maxed, 1)

            def part_maxima(u, i):
                n = QT * u + i
                hi, lo = slice(64, 64 + HPG), slice(64 + HPG, 64 + 2 * HPG)
                dve.wait_ge(maxed, S_ALL * u + S_CUM[i] + S_BANKS[i])
                if n == 0:
                    dve.wait_ge(split_set, 1)
                else:
                    dve.wait_ge(shifted, n)
                nc.vector.tensor_copy(split[:, hi].bitcast(F32R), nmax[:, i, :]).then_inc(parted, 1)
                dve.wait_ge(parted, 2 * n + 1)
                nc.vector.tensor_tensor(split[:, lo], nmax[:, i, :], split[:, hi], ALU.subtract).then_inc(parted, 1)

            def spread_maxima(u, i):
                n = QT * u + i
                dve.wait_ge(shifted, n + 1)
                if u >= 1:
                    dve.wait_ge(t_scored, TICKS * (u - 1) + J_CUM[i] + i + 1)
                nc.vector.tensor_tensor(q_rows[S64, i, :, :],
                                        qkbank[S64, 0:P].unsqueeze(1).to_broadcast([2 * HPG, HPG, P]),
                                        m.own[S64, :].unsqueeze(2).to_broadcast([2 * HPG, HPG, P]),
                                        ALU.mult).then_inc(max_rows, 1)

            def read_heads(u, i):
                n = QT * u + i
                dve.wait_ge(weighed, TICKS * u + J_CUM[i] + i + 1)
                if n >= 2:
                    dve.wait_ge(backed, n - 1)
                nc.vector.tensor_copy(head_t[0:VW, n % 2, :], cbank[0:VW, :]).then_inc(c_read, 1)

            def head_view():
                return hbank[:, 0:HPG * VW].rearrange("p (h n) -> p h n", h=HPG)

            def take_sums(u, i):
                n = QT * u + i
                dve.wait_ge(backed, n + 1)
                nc.vector.reciprocal(rsum[:, n % 2, :], head_view()[:, :, HD0]).then_inc(divided, 1)
                nc.vector.tensor_copy(head_sum[:, n % 2, :, :], head_view()[:, :, V1:VW]).then_inc(divided, 1)

            def add_parts(u, i):
                n = QT * u + i
                dve.wait_ge(divided, 3 * n + 2)
                nc.vector.tensor_tensor(head_sum[:, n % 2, :, :], head_view()[:, :, 0:HD0], head_sum[:, n % 2, :, :],
                                        ALU.add).then_inc(divided, 1)

            def divide(u, i):
                g, t, n = u // 2, (u % 2) * QT + i, QT * u + i
                dve.wait_ge(divided, 3 * n + 3)
                nc.vector.tensor_tensor(head[:, t, HPG * g:HPG * (g + 1), :], head_sum[:, n % 2, :, :],
                                        rsum[:, n % 2, :].unsqueeze(2).to_broadcast([P, HPG, HD0]),
                                        ALU.mult).then_inc(head_ready, 1)

            nc.vector.memset(split[:, :], 0.0).then_inc(split_set, 1)
            for u, k in ticks:
                for step in planned(BACK, u, k):
                    take_sums(*step)
                for step in planned(SHIFT, u, k):
                    part_maxima(*step)
                for item in planned(SCORE, u, k):
                    maxima(*item)
                for step in planned(END, u, k):
                    read_heads(*step)
                for step in planned(BACK, u, k):
                    add_parts(*step)
                for step in planned(BACK, u, k):
                    divide(*step)
                for step in planned(SHIFT, u, k):
                    spread_maxima(*step)

            def low(t):
                dve.wait_ge(c_hi_done, t + 1)
                nc.vector.tensor_tensor(c_lo[:, t % 2, :, :], turned[t % 2][:, :].rearrange("p (k n) -> p k n", k=KT),
                                        c_hi[:, t % 2, :, :].bitcast(F32), ALU.subtract).then_inc(c_ready, 1)

            low(0)
            for t in range(NT):
                if t + 1 < NT:
                    low(t + 1)
                dve.wait_ge(projected, t + 1)
                nc.vector.tensor_tensor(m.x[:, t, :], score[t % NS][:, :], m.x[:, t, :], ALU.add).then_inc(added, 1)

        @block.scalar
        def _(act):
            def read_qk(u, s):
                act.wait_ge(qk_turned, TU * u + s + 1)
                if s == 0:
                    if u >= 2:
                        act.wait_ge(t_scored, TICKS * (u - 1))
                    to = k_rows[0:64, u % 2, :]
                    src = qkbank[0:64, :]
                else:
                    if u >= 1:
                        act.wait_ge(t_scored, TICKS * (u - 1) + J_CUM[s - 1] + s)
                    to = q_rows[0:64, s - 1, :, :]
                    src = qkbank[0:64, :].rearrange("p (h n) -> p h n", h=HPG)
                nc.scalar.activation(to, src, ACT.Copy).then_inc(qk_read, 1)

            def exponentials(mm):
                act.wait_ge(t_scored, mm + 1)
                if mm >= NE:
                    act.wait_ge(p_ready, mm - NE + 1)
                nc.scalar.activation(prob[:, mm % NE, :], turned[mm % 2][:, :], ACT.Exp).then_inc(exped, 1)

            def high(mm):
                act.wait_ge(exped, mm + 1)
                if mm >= NP:
                    act.wait_ge(weighed, mm - NP + 1)
                nc.scalar.activation(p_hi[:, mm % NP, :], prob[:, mm % NE, :], ACT.Copy).then_inc(p_hi_done, 1)

            for u, k in ticks:
                mm = TICKS * u + k
                if 0 <= mm + AHEAD < TICKS * 2 * NG:
                    exponentials(mm + AHEAD)
                for item in planned(TURN, u, k):
                    read_qk(*item)
                if 0 <= mm + AHEAD < TICKS * 2 * NG:
                    high(mm + AHEAD)
                if u == 0 and k < KT:
                    act.wait_ge(loaded, 16)
                    nc.scalar.activation(wo_hi[:, k, :], raw_wo[:, k, :], ACT.Copy).then_inc(wo_hi_done, 1)
            for t in range(NT):
                act.wait_ge(c_turned, t + 1)
                if t >= 2:
                    act.wait_ge(projected, t - 1)
                nc.scalar.activation(c_hi[:, t % 2, :, :], turned[t % 2][:, :].rearrange("p (k n) -> p k n", k=KT),
                                     ACT.Copy).then_inc(c_hi_done, 1)

        @block.gpsimd
        def _(pool):
            nc.gpsimd.memset(k_rows[S64, :, :].bitcast(F32), 1.0).then_inc(ones_set, 1)
            for mm in range(TICKS * 2 * NG):
                pool.wait_ge(p_hi_done, mm + 1)
                if mm >= NP:
                    pool.wait_ge(weighed, mm - NP + 1)
                nc.gpsimd.tensor_tensor(p_lo[:, mm % NP, :], prob[:, mm % NE, :], p_hi[:, mm % NP, :].bitcast(F32),
                                        ALU.subtract).then_inc(p_ready, 1)
                if 2 <= mm < 2 + KT:
                    k = mm - 2
                    pool.wait_ge(wo_hi_done, k + 1)
                    nc.gpsimd.tensor_tensor(wo_lo[:, k, :], raw_wo[:, k, :], wo_hi[:, k, :].bitcast(F32),
                                            ALU.subtract).then_inc(wo_ready, 1)


def feed_forward0(nc, m, inp):
    FQ = FF // 4
    ROW = [(0, 128), (128, 128), (256, FQ - 256)]
    NR = len(ROW)
    S3 = 3 * R
    tiles = [(FQ * c + ROW[r][0], ROW[r][1]) for r in range(NR) for c in range(4)]
    NM = len(tiles)
    with ExitStack() as ctx:
        sb = lambda n, shape, dt=F32: ctx.enter_context(nc.sbuf_tensor(f"f0_{n}", shape, dt))
        ps = lambda n: ctx.enter_context(nc.psum_tensor(f"f0_{n}", [P, 512], F32))
        sem = lambda n: ctx.enter_context(nc.semaphore(f"f0_{n}"))
        w_raw, w_hi, w_lo = sb("w_raw", [P, 2 * FF]), sb("w_hi", [P, 2 * FF], F32R), sb("w_lo", [P, 2 * FF], F32R)
        d_raw, d_hi, d_lo = sb("d_raw", [P, NR, D]), sb("d_hi", [P, NR, D], F32R), sb("d_lo", [P, NR, D], F32R)
        a_raw, a_hi, a_lo = sb("a_raw", [P, KT, 64]), sb("a_hi", [P, KT, 64], F32R), sb("a_lo", [P, KT, 64], F32R)
        a2 = sb("a2", [P, NM, S3])
        b_raw, b_hi, b_lo = sb("b_raw", [64, FF]), sb("b_hi", [64, FF], F32R), sb("b_lo", [64, FF])
        b_st = sb("b_st", [64, FF], F32R)
        e_raw, e_hi, e_lo = sb("e_raw", [S3, D]), sb("e_hi", [S3, D], F32R), sb("e_lo", [S3, D])
        e_st = sb("e_st", [S3, D], F32R)
        pick = sb("pick", [64, 4])
        t_raw, t_hi, t_lo = sb("t_raw", [64, B, T]), sb("t_hi", [64, B, T], F32R), sb("t_lo", [64, B, T])
        t_st = sb("t_st", [64, B, T], F32R)
        s_raw, s_hi, s_lo = sb("s_raw", [S3, 2, T]), sb("s_hi", [S3, 2, T], F32R), sb("s_lo", [S3, 2, T])
        s_st = sb("s_st", [S3, 2, T], F32R)
        act_g, prod = sb("act_g", [P, 2, T]), sb("prod", [P, 3, T])
        quarters = sb("quarters", [P, 2, T])
        z_hi, z_lo = sb("z_hi", [P, NR, T], F32R), sb("z_lo", [P, NR, T], F32R)
        out = [ps(f"out{k}") for k in range(QT)]
        gbank, ubank, tbank = [ps("gbank0"), ps("gbank1")], ps("ubank"), ps("tbank")
        loaded_a, loaded_b, loaded_w, loaded_d = (sem(n) for n in ("loaded_a", "loaded_b", "loaded_w", "loaded_d"))
        s_hi_done, s_lo_done, stacked, chain = (sem(n) for n in ("split_hi", "split_lo", "stacked", "chain"))
        t_made, t_read, gated, upped, silued, prodded, summed, z_hi_done, z_ready = (sem(n) for n in (
            "t_made", "t_read", "gated", "upped", "silued", "prodded", "summed", "z_hi_done", "z_ready"))
        t2_made, t2_read, downed, added = (sem(n) for n in ("t2_made", "t2_read", "downed", "added"))
        block = ctx.enter_context(nc.Block())

        splits = [(a_raw[:, :, :], a_hi[:, :, :], a_lo[:, :, :])]
        splits += [(b_raw[:, :], b_hi[:, :], b_lo[:, :]), (e_raw[:, :], e_hi[:, :], e_lo[:, :])]
        NWS = 4
        wc = 2 * FF // NWS
        for k in (0, 2, 1, 3):
            splits.append(tuple(x[:, k * wc:(k + 1) * wc] for x in (w_raw, w_hi, w_lo)))
        splits.append((d_raw[:, 0:2, :], d_hi[:, 0:2, :], d_lo[:, 0:2, :]))
        wl = ROW[2][1]
        splits.append((d_raw[0:wl, 2, :], d_hi[0:wl, 2, :], d_lo[0:wl, 2, :]))
        ALL = len(splits)

        @block.sync
        def _(sp):
            sp.dma_start(a_raw[:, :, :], inp["L0_a13"].rearrange("(k p) n -> p k n", p=P)).then_inc(loaded_a, 16)
            sp.dma_start(b_raw[:, :], inp["L0_b13"]).then_inc(loaded_b, 16)
            sp.dma_start(e_raw[:, :], inp["L0_b2"]).then_inc(loaded_b, 16)
            sp.dma_start(pick[:, :], inp["c_pick"]).then_inc(loaded_b, 16)
            sp.dma_start(w_raw[:, :], inp["L0_w13_t"]).then_inc(loaded_w, 16)
            for r, (at, w) in enumerate(ROW):
                sp.dma_start(d_raw[0:w, r, :], inp["L0_w2_t"][at:at + w, :]).then_inc(loaded_d, 16)
            for n, (at, w) in enumerate(tiles):
                sp.dma_start(a2[0:w, n, :], inp["L0_a2"][at:at + w, :]).then_inc(loaded_d, 16)

        @block.scalar
        def _(act):
            for n, (raw, hi, _) in enumerate(splits):
                if n == 0:
                    act.wait_ge(loaded_a, 16)
                if n == 1:
                    act.wait_ge(loaded_b, 48)
                if n == 3:
                    act.wait_ge(loaded_w, 16)
                if n == ALL - 2:
                    act.wait_ge(loaded_d, 16 * (NR + NM))
                nc.scalar.activation(hi, raw, ACT.Copy).then_inc(s_hi_done, 1)

            def silu(b, n):
                w = tiles[n][1]
                k = NM * b + n
                act.wait_ge(gated, k + 1)
                if k >= 2:
                    act.wait_ge(prodded, k - 1)
                nc.scalar.activation(act_g[0:w, k % 2, :], gbank[k % 2][0:w, :], ACT.Silu).then_inc(silued, 1)

            def z_high(b, r):
                w = ROW[r][1]
                act.wait_ge(summed, 3 * (NR * b + r) + 3)
                if b:
                    act.wait_ge(downed, 1)
                nc.scalar.activation(z_hi[0:w, r, :], quarters[0:w, r % 2, :], ACT.Copy).then_inc(z_hi_done, 1)

            for b in range(B):
                for n in range(NM):
                    silu(b, n)
                    if n % 4 == 1 and n >= 4:
                        z_high(b, n // 4 - 1)
                z_high(b, NR - 1)

        @block.gpsimd
        def _(pool):
            for n, (raw, hi, lo) in enumerate(splits):
                pool.wait_ge(s_hi_done, n + 1)
                nc.gpsimd.tensor_tensor(lo, raw, hi.bitcast(F32), ALU.subtract).then_inc(s_lo_done, 1)

            def add_quarter(b, n):
                k, r, c, w = NM * b + n, n // 4, n % 4, tiles[n][1]
                z = NR * b + r
                pool.wait_ge(prodded, k + 1)
                q = quarters[0:w, r % 2, :]
                if c == 1:
                    if z >= 2:
                        pool.wait_ge(z_ready, z - 1)
                    nc.gpsimd.tensor_tensor(q, prod[0:w, (k - 1) % 3, :], prod[0:w, k % 3, :], ALU.add).then_inc(summed, 1)
                elif c:
                    pool.wait_ge(summed, 3 * z + c - 1)
                    nc.gpsimd.tensor_tensor(q, q, prod[0:w, k % 3, :], ALU.add).then_inc(summed, 1)

            def z_low(b, r):
                z, w = NR * b + r, ROW[r][1]
                pool.wait_ge(z_hi_done, z + 1)
                nc.gpsimd.tensor_tensor(z_lo[0:w, r, :], quarters[0:w, r % 2, :], z_hi[0:w, r, :].bitcast(F32),
                                        ALU.subtract).then_inc(z_ready, 1)

            for b in range(B):
                for n in range(NM):
                    add_quarter(b, n)
                    if n % 4 == 3:
                        z_low(b, n // 4)

        @block.vector
        def _(dve):
            steps = [0]

            def link(ins):
                steps[0] += 1
                ins.then_inc(chain, 1)
                dve.wait_ge(chain, steps[0])

            def stack(to, hi, lo, tmp, cols):
                n = tmp.shape[0]
                link(nc.vector.tensor_scalar(tmp, lo, pick[0:n, cols + 1:cols + 2], None, ALU.mult))
                return nc.vector.scalar_tensor_tensor(to, hi.bitcast(F32), pick[0:n, cols:cols + 1], tmp, ALU.mult, ALU.add)

            dve.wait_ge(s_lo_done, 3)
            stack(b_st[:, :], b_hi[:, :], b_lo[:, :], b_raw[:, :], 2).then_inc(stacked, 1)
            stack(e_st[:, :], e_hi[:, :], e_lo[:, :], e_raw[:, :], 2).then_inc(stacked, 1)

            def t_stack(b):
                dve.wait_ge(t_made, b + 1)
                link(nc.vector.tensor_scalar(t_raw[:, b, :], tbank[0:64, :], 0.5, None, ALU.mult))
                link(nc.vector.tensor_copy(t_hi[:, b, :], t_raw[:, b, :]))
                link(nc.vector.tensor_tensor(t_lo[:, b, :], t_raw[:, b, :], t_hi[:, b, :].bitcast(F32), ALU.subtract))
                stack(t_st[:, b, :], t_hi[:, b, :], t_lo[:, b, :], t_raw[:, b, :], 0).then_inc(t_read, 1)

            def t2_stack(b):
                dve.wait_ge(t2_made, NM * (b + 1))
                link(nc.vector.tensor_scalar(s_raw[:, b, :], tbank[0:S3, :], 0.5, None, ALU.mult))
                link(nc.vector.tensor_copy(s_hi[:, b, :], s_raw[:, b, :]))
                link(nc.vector.tensor_tensor(s_lo[:, b, :], s_raw[:, b, :], s_hi[:, b, :].bitcast(F32), ALU.subtract))
                stack(s_st[:, b, :], s_hi[:, b, :], s_lo[:, b, :], s_raw[:, b, :], 0).then_inc(t2_read, 1)

            def multiply(b, n):
                k, w = NM * b + n, tiles[n][1]
                dve.wait_ge(silued, k + 1)
                dve.wait_ge(upped, k + 1)
                if k >= 3:
                    dve.wait_ge(t2_made, k - 2)
                    j = k - 3
                    done = 3 * (j // 4) + max(j % 4, 1)
                    dve.wait_ge(summed, done)
                nc.vector.tensor_tensor(prod[0:w, k % 3, :], act_g[0:w, k % 2, :], ubank[0:w, :],
                                        ALU.mult).then_inc(prodded, 1)

            t_stack(0)
            t_stack(1)
            for b in range(B):
                for n in range(NM):
                    multiply(b, n)
                    if b and n == 0:
                        for t in range(QT):
                            dve.wait_ge(downed, t + 1)
                            nc.vector.tensor_tensor(m.x[:, t, :], out[t][:, :], m.x[:, t, :], ALU.add).then_inc(added, 1)
                t2_stack(b)
            for t in range(QT):
                dve.wait_ge(downed, QT + t + 1)
                nc.vector.tensor_tensor(m.x[:, QT + t, :], out[t][:, :], m.x[:, QT + t, :], ALU.add).then_inc(added, 1)

        @block.tensor
        def _(pe):
            def three(to, l_hi, l_lo, r_hi, r_lo, start, stop):
                nc.tensor.matmul(to, l_hi, r_hi, start=start, stop=False)
                nc.tensor.matmul(to, l_hi, r_lo, start=False, stop=False)
                return nc.tensor.matmul(to, l_lo, r_hi, start=False, stop=stop)

            pe.wait_ge(s_lo_done, 1)
            for b in range(B):
                if b:
                    pe.wait_ge(t_read, 1)
                tok = slice(b * T, (b + 1) * T)
                for k in range(KT):
                    last = three(tbank[0:64, :], a_hi[:, k, :], a_lo[:, k, :], m.h_hi[:, k, tok], m.h_lo[:, k, tok],
                                 k == 0, k == KT - 1)
                last.then_inc(t_made, 1)

            def up(b, n, second):
                at, w = tiles[n]
                k = NM * b + n
                bank = ubank if second else gbank[k % 2]
                tok = slice(b * T, (b + 1) * T)
                if second and k >= 1:
                    pe.wait_ge(prodded, k)
                if not second and k >= 2:
                    pe.wait_ge(silued, k - 1)
                cols = slice(FF * second + at, FF * second + at + w)
                three(bank[0:w, :], w_hi[:, cols], w_lo[:, cols], m.f_hi[:, tok], m.f_lo[:, tok], True, False)
                rows = slice(32 * second, 32 * second + S3)
                nc.tensor.matmul(bank[0:w, :], b_st[rows, at:at + w], t_st[rows, b, :], start=False,
                                 stop=True).then_inc(upped if second else gated, 1)

            def lora_down(b, n):
                k, w = NM * b + n, tiles[n][1]
                pe.wait_ge(prodded, k + 1)
                if n == 0 and b:
                    pe.wait_ge(t2_read, b)
                nc.tensor.matmul(tbank[0:S3, :], a2[0:w, n, :], prod[0:w, k % 3, :], start=(n == 0),
                                 stop=(n == NM - 1)).then_inc(t2_made, 1)

            def down(b, r):
                w = ROW[r][1]
                pe.wait_ge(z_ready, NR * b + r + 1)
                for t in range(QT):
                    if b and r == 0:
                        pe.wait_ge(added, t + 1)
                    tok = slice(t * P, (t + 1) * P)
                    three(out[t][:, :], z_hi[0:w, r, tok], z_lo[0:w, r, tok], d_hi[0:w, r, :], d_lo[0:w, r, :],
                          r == 0, False)

            pe.wait_ge(t_read, B)
            pe.wait_ge(stacked, 2)
            pe.wait_ge(s_lo_done, 3 + NWS)
            for b in range(B):
                for n in range(NM):
                    up(b, n, 0)
                    up(b, n, 1)
                    if n == 0 and b == 0:
                        pe.wait_ge(s_lo_done, ALL)
                    if n >= 1:
                        lora_down(b, n - 1)
                    if n % 4 == 2 and n >= 4:
                        down(b, n // 4 - 1)
                lora_down(b, NM - 1)
                down(b, NR - 1)
                pe.wait_ge(t2_read, b + 1)
                for t in range(QT):
                    nc.tensor.matmul(out[t][:, :], s_st[:, b, t * P:(t + 1) * P], e_st[:, :], start=False,
                                     stop=True).then_inc(downed, 1)


def feed_forward1(nc, m, inp):
    tiles = [(at, min(P, FF - at)) for at in range(0, FF, P)]
    NM = len(tiles)
    NRAW = 6
    gu_v = inp["L1_gate_up_t"].rearrange("(k p) n -> p k n", p=P)
    with ExitStack() as ctx:
        sb = lambda n, shape, dt=F32: ctx.enter_context(nc.sbuf_tensor(f"f1_{n}", shape, dt))
        ps = lambda n: ctx.enter_context(nc.psum_tensor(f"f1_{n}", [P, 512], F32))
        sem = lambda n: ctx.enter_context(nc.semaphore(f"f1_{n}"))
        raw = sb("raw", [P, NRAW, 512])
        w_hi, w_lo = sb("w_hi", [P, NRAW, 512], F32R), sb("w_lo", [P, NRAW, 512], F32R)
        act_g, prod = sb("act_g", [P, 2, T]), sb("prod", [P, 2, T])
        z_hi, z_lo = sb("z_hi", [P, 2, T], F32R), sb("z_lo", [P, 2, T], F32R)
        out = [ps(f"out{k}") for k in range(QT)]
        gbank, ubank = [ps("gbank0"), ps("gbank1")], [ps("ubank0"), ps("ubank1")]
        loaded = [sem(f"loaded{k}") for k in range(NRAW)]
        w_hi_done, w_ready, gated, upped, silued, prodded, z_hi_done, z_ready, downed, added = (sem(n) for n in (
            "w_hi_done", "w_ready", "gated", "upped", "silued", "prodded", "z_hi_done", "z_ready", "downed", "added"))
        block = ctx.enter_context(nc.Block())
        ALL = B * NM

        def piece(x, s, p):
            w = tiles[s % NM][1]
            slot = (3 * s + p) % NRAW
            if p == 2:
                return x[0:w, slot, :]
            return x[:, slot, 0:KT * w].rearrange("p (k n) -> p k n", k=KT)

        @block.sync
        def _(sp):
            for s in range(ALL):
                at, w = tiles[s % NM]
                for p in range(3):
                    n = 3 * s + p
                    if n >= NRAW:
                        sp.wait_ge(w_ready, n - NRAW + 1)
                    src = inp["L1_down_t"][at:at + w, :] if p == 2 else gu_v[:, :, FF * p + at:FF * p + at + w]
                    sp.dma_start(piece(raw, s, p), src).then_inc(loaded[n % NRAW], 16)

        @block.tensor
        def _(pe):
            def three(to, l_hi, l_lo, r_hi, r_lo, start, stop):
                nc.tensor.matmul(to, l_hi, r_hi, start=start, stop=False)
                nc.tensor.matmul(to, l_hi, r_lo, start=False, stop=False)
                return nc.tensor.matmul(to, l_lo, r_hi, start=False, stop=stop)

            def up(s, p):
                b, w = s // NM, tiles[s % NM][1]
                bank = (gbank, ubank)[p][s % 2]
                pe.wait_ge(w_ready, 3 * s + p + 1)
                if s >= 2:
                    pe.wait_ge((silued, prodded)[p], s - 1)
                hi, lo = piece(w_hi, s, p), piece(w_lo, s, p)
                for k in range(KT):
                    tok = slice(b * T, (b + 1) * T)
                    last = three(bank[0:w, :], hi[:, k, :], lo[:, k, :], m.h_hi[:, k, tok], m.h_lo[:, k, tok],
                                 k == 0, k == KT - 1)
                last.then_inc((gated, upped)[p], 1)

            def down(s):
                b, n, w = s // NM, s % NM, tiles[s % NM][1]
                pe.wait_ge(z_ready, s + 1)
                pe.wait_ge(w_ready, 3 * s + 3)
                hi, lo = piece(w_hi, s, 2), piece(w_lo, s, 2)
                for t in range(QT):
                    if b and n == 0:
                        pe.wait_ge(added, t + 1)
                    tok = slice(t * P, (t + 1) * P)
                    last = three(out[t][:, :], z_hi[0:w, s % 2, tok], z_lo[0:w, s % 2, tok], hi, lo, n == 0, n == NM - 1)
                last.then_inc(downed, 1)

            for s in range(ALL):
                up(s, 0)
                up(s, 1)
                if s >= 1:
                    down(s - 1)
            down(ALL - 1)

        @block.scalar
        def _(act):
            def weights_high(s, p):
                n = 3 * s + p
                act.wait_ge(loaded[n % NRAW], 16 * (n // NRAW + 1))
                if s >= 2:
                    act.wait_ge((gated, upped, downed)[p], s - 1)
                nc.scalar.activation(piece(w_hi, s, p), piece(raw, s, p), ACT.Copy).then_inc(w_hi_done, 1)

            for p in range(3):
                weights_high(0, p)
            for s in range(ALL):
                w = tiles[s % NM][1]
                if s + 1 < ALL:
                    weights_high(s + 1, 0)
                    weights_high(s + 1, 1)
                act.wait_ge(gated, s + 1)
                if s >= 2:
                    act.wait_ge(prodded, s - 1)
                nc.scalar.activation(act_g[0:w, s % 2, :], gbank[s % 2][0:w, :], ACT.Silu).then_inc(silued, 1)
                if s + 1 < ALL:
                    weights_high(s + 1, 2)
                act.wait_ge(prodded, s + 1)
                if s >= 2:
                    act.wait_ge(downed, s - 1)
                nc.scalar.activation(z_hi[0:w, s % 2, :], prod[0:w, s % 2, :], ACT.Copy).then_inc(z_hi_done, 1)

        @block.vector
        def _(dve):
            def add_out(b):
                for t in range(QT):
                    dve.wait_ge(downed, NM * (b + 1))
                    xt = m.x[:, QT * b + t, :]
                    nc.vector.tensor_tensor(xt, out[t][:, :], xt, ALU.add).then_inc(added, 1)

            for s in range(ALL):
                w = tiles[s % NM][1]
                dve.wait_ge(silued, s + 1)
                dve.wait_ge(upped, s + 1)
                if s >= 2:
                    dve.wait_ge(z_ready, s - 1)
                nc.vector.tensor_tensor(prod[0:w, s % 2, :], act_g[0:w, s % 2, :], ubank[s % 2][0:w, :],
                                        ALU.mult).then_inc(prodded, 1)
                dve.wait_ge(z_hi_done, s + 1)
                nc.vector.tensor_tensor(z_lo[0:w, s % 2, :], prod[0:w, s % 2, :], z_hi[0:w, s % 2, :].bitcast(F32),
                                        ALU.subtract).then_inc(z_ready, 1)
                if s == NM:
                    add_out(0)
            add_out(1)

        @block.gpsimd
        def _(pool):
            for s in range(ALL):
                for p in range(3):
                    pool.wait_ge(w_hi_done, 3 * s + p + 1)
                    nc.gpsimd.tensor_tensor(piece(w_lo, s, p), piece(raw, s, p), piece(w_hi, s, p).bitcast(F32),
                                            ALU.subtract).then_inc(w_ready, 1)


def program(nc, inp, out, phases=("attn0", "ffn0", "attn1", "ffn1")):
    with ExitStack() as ctx:
        sb = lambda n, shape, dt=F32: ctx.enter_context(nc.sbuf_tensor(n, shape, dt))
        sem = lambda n: ctx.enter_context(nc.semaphore(n))
        m = Memory()
        m.x = sb("x", [P, NT, D])
        m.ident, m.mask = sb("ident", [P, P]), sb("mask", [P, P])
        m.mask_t, m.own = sb("mask_t", [P, P]), sb("own", [P, HPG])
        m.ident_b, m.mask_b, m.mask_t_b = (sb(n, [P, P], BF16) for n in ("ident_b", "mask_b", "mask_t_b"))
        fetched, fetched0, fetched1, cast, stored = (sem(n) for n in ("fetched", "fetched0", "fetched1", "cast", "stored"))
        x_in = inp["L0_attn_x"].rearrange("b (t p) d -> p (b t) d", p=P)
        x_out = out.rearrange("b (t p) d -> p (b t) d", p=P)

        with nc.Block() as block:
            @block.sync
            def _(sp):
                sp.dma_start(m.ident[:, :], inp["c_ident"]).then_inc(fetched, 16)
                sp.dma_start(m.mask[:, :], inp["c_mask"]).then_inc(fetched, 16)
                sp.dma_start(m.mask_t[:, :], inp["c_mask_t"]).then_inc(fetched, 16)
                sp.dma_start(m.own[:, :], inp["c_own"]).then_inc(fetched, 16)
                sp.dma_start(m.x[:, :, :], x_in).then_inc(fetched, 16)

            @block.vector
            def _(dve):
                dve.wait_ge(fetched, 80)
                nc.vector.tensor_copy(m.ident_b[:, :], m.ident[:, :]).then_inc(cast, 1)
                nc.vector.tensor_copy(m.mask_b[:, :], m.mask[:, :]).then_inc(cast, 1)
                nc.vector.tensor_copy(m.mask_t_b[:, :], m.mask_t[:, :]).then_inc(cast, 1)

        if "attn0" in phases:
            with ExitStack() as scope:
                ssb = lambda n, shape, dt=F32: scope.enter_context(nc.sbuf_tensor(n, shape, dt))
                m.q2 = ssb("q2", [P, NT, NG * HPG, 4, HD0], F32R)
                m.k2 = ssb("k2", [P, NT, NG, 4, HD0], F32R)
                m.vw = ssb("vw", [P, NT, NG, 2, 2 * HD0 + 1], F32R)
                with ExitStack() as inner:
                    isb = lambda n, shape, dt=F32: inner.enter_context(nc.sbuf_tensor(n, shape, dt))
                    m.h_hi, m.h_lo = isb("h0_hi", [P, KT, NT * P], F32R), isb("h0_lo", [P, KT, NT * P], F32R)
                    m.cos0, m.sin0, m.nsin0 = (isb(n, [P, QT, HD0 // 2]) for n in ("cos0", "sin0", "nsin0"))
                    with nc.Block() as block:
                        @block.sync
                        def _(sp):
                            for to, of in ((m.cos0, "c_cos0"), (m.sin0, "c_sin0"), (m.nsin0, "c_nsin0")):
                                sp.dma_start(to[:, :, :], inp[of]).then_inc(fetched0, 16)
                            sp.wait_ge(fetched0, 48)
                    layer_norm(nc, m, "n0")
                    project0(nc, m, inp["L0_qkv"])
                attend0(nc, m, inp["L0_attn_Wo"])
        if "ffn0" in phases:
            with ExitStack() as scope:
                ssb = lambda n, shape, dt=F32: scope.enter_context(nc.sbuf_tensor(n, shape, dt))
                m.h_hi, m.h_lo = ssb("h2_hi", [P, KT, NT * P], F32R), ssb("h2_lo", [P, KT, NT * P], F32R)
                m.f_hi, m.f_lo = ssb("f_hi", [P, NT * P], F32R), ssb("f_lo", [P, NT * P], F32R)
                layer_norm(nc, m, "n1", folded=True)
                feed_forward0(nc, m, inp)
        if "attn1" in phases:
            with ExitStack() as scope:
                ssb = lambda n, shape, dt=F32: scope.enter_context(nc.sbuf_tensor(n, shape, dt))
                m.h_hi, m.h_lo = ssb("h1_hi", [P, KT, NT * P], F32R), ssb("h1_lo", [P, KT, NT * P], F32R)
                m.cos1, m.sin1 = ssb("cos1", [P, T]), ssb("sin1", [P, T])
                with nc.Block() as block:
                    @block.sync
                    def _(sp):
                        sp.dma_start(m.cos1[:, :], inp["c_cos1"]).then_inc(fetched1, 16)
                        sp.dma_start(m.sin1[:, :], inp["c_sin1"]).then_inc(fetched1, 16)
                        sp.wait_ge(fetched1, 32)
                layer_norm(nc, m, "n2")
                attention1(nc, m, inp["L1_attn_wq"], inp["L1_attn_wk"], inp["L1_attn_wv"], inp["L1_attn_wo"])
        if "ffn1" in phases:
            with ExitStack() as scope:
                ssb = lambda n, shape, dt=F32: scope.enter_context(nc.sbuf_tensor(n, shape, dt))
                m.h_hi, m.h_lo = ssb("h3_hi", [P, KT, NT * P], F32R), ssb("h3_lo", [P, KT, NT * P], F32R)
                layer_norm(nc, m, "n3")
                feed_forward1(nc, m, inp)

        with nc.Block() as block:
            @block.sync
            def _(sp):
                sp.dma_start(x_out, m.x[:, :, :]).then_inc(stored, 16)
                sp.wait_ge(stored, 16)


class Memory:
    pass


def laid_out(inputs):
    import numpy as np

    a = {n: np.asarray(v) for n, v in inputs.items()}
    same = ["L0_attn_x", "L0_attn_Wo", "L1_attn_wq", "L1_attn_wk", "L1_attn_wv", "L1_attn_wo"]
    out = {n: np.ascontiguousarray(a[n]) for n in same}
    out["L0_qkv"] = np.concatenate([a["L0_attn_Wq"], a["L0_attn_Wk"], a["L0_attn_Wv"]], axis=1)
    out["L1_gate_up_t"] = np.ascontiguousarray(a["L1_ffn_w_gate_up"].T)
    out["L1_down_t"] = np.ascontiguousarray(a["L1_ffn_w_down"].T)
    out["L0_w13_t"] = np.ascontiguousarray(np.concatenate([a["L0_ffn_w1q"], a["L0_ffn_w3q"]], axis=0).T)
    out["L0_w2_t"] = np.ascontiguousarray(a["L0_ffn_w2q"].T)

    def stack(first, second, axis):
        shape = list(first.shape)
        shape[axis] = 32 - 3 * R
        gap = np.zeros(shape, first.dtype)
        return np.concatenate([first] * 3 + [gap] + [second] * 3 + [gap], axis=axis)

    out["L0_a13"] = stack(a["L0_ffn_a1"].T, a["L0_ffn_a3"].T, 1)
    out["L0_b13"] = stack(a["L0_ffn_b1"].T, a["L0_ffn_b3"].T, 0)
    out["L0_a2"] = np.concatenate([a["L0_ffn_a2"].T] * 3, axis=1)
    out["L0_b2"] = np.concatenate([a["L0_ffn_b2"].T] * 3, axis=0)
    out.update(constants())
    return out


def constants():
    import numpy as np

    ident = np.eye(P, dtype=np.float32)
    key, query = np.arange(P)[None, :], np.arange(P)[:, None]
    mask = np.where(key > query, np.float32(-1e30), np.float32(0))
    row, h = np.arange(P)[:, None], np.arange(HPG)[None, :]
    own = ((row == 64 + h) | (row == 64 + HPG + h)).astype(np.float32)
    one, lora = np.float32(1), np.arange(32) // R
    rows = np.stack([(lora == 0) | (lora == 2), lora == 1, lora <= 1, lora == 2], axis=1)
    pick = np.concatenate([rows, rows], axis=0) * one
    pos = np.arange(T, dtype=np.float32)
    inv0 = (np.float32(1) / np.float32(500000.0) ** (np.arange(0, HD0, 2, dtype=np.float32) / np.float32(HD0)))
    f0 = (pos[:, None] * inv0.astype(np.float32)[None, :]).astype(np.float32).reshape(QT, P, HD0 // 2).transpose(1, 0, 2)
    inv = 1.0 / 500000.0 ** (np.arange(0, HD1, 2, dtype=np.float64) / HD1)
    wavelen = 2.0 * np.pi / inv
    low_wl, high_wl = 1024 / 1.0, 1024 / 4.0
    smooth = (1024 / wavelen - 1.0) / (4.0 - 1.0)
    scaled = np.where(wavelen > low_wl, inv / 8.0, inv)
    mid = (wavelen <= low_wl) & (wavelen >= high_wl)
    scaled = np.where(mid, (1 - smooth) * inv / 8.0 + smooth * inv, scaled).astype(np.float32)
    f1 = (pos[:, None] * scaled[None, :]).T
    return {
        "c_ident": ident,
        "c_mask": mask,
        "c_mask_t": np.ascontiguousarray(mask.T),
        "c_own": own,
        "c_pick": pick,
        "c_cos0": np.ascontiguousarray(np.cos(f0)),
        "c_sin0": np.ascontiguousarray(np.sin(f0)),
        "c_nsin0": np.ascontiguousarray(-np.sin(f0)),
        "c_cos1": np.concatenate([np.cos(f1), np.cos(f1)], axis=0),
        "c_sin1": np.concatenate([np.sin(f1), -np.sin(f1)], axis=0),
    }


def kernel(**inputs):
    import concourse.bacc as _bacc
    from concourse import mybir as _mybir
    from concourse.bass_utils import run_bass_kernel_spmd as _run

    nc = _bacc.Bacc("TRN2", target_bir_lowering=False, num_devices=1)
    arrays = laid_out(inputs)
    args = {}
    for name, a in arrays.items():
        args[name] = nc.dram_tensor(f"in_{name}", a.shape, _mybir.dt.from_np(a.dtype), kind="ExternalInput").ap()
    out = nc.dram_tensor("out_0", (B, T, D), _mybir.dt.float32, kind="ExternalOutput").ap()
    program(nc, args, out)
    r = _run(nc, [{f"in_{name}": a for name, a in arrays.items()}], core_ids=[0])
    return r.results[0]["out_0"]
```

```python
from contextlib import ExitStack

import concourse.bass as bass
from concourse import mybir

F32 = mybir.dt.float32
F32R = mybir.dt.float32r
BF16 = mybir.dt.bfloat16
ALU = mybir.AluOpType
ACT = mybir.ActivationFunctionType
AX_X = mybir.AxisListType.X

P = 128
B, T, D = 2, 512, 512
KT = D // P
NT = B * T // P
QT = T // P
NG, HPG = 8, 4
HD0, HD1 = 16, 128
FF = 1376
R = 2
EPS = 1e-5
FF_TILES = [(at, min(P, FF - at)) for at in range(0, FF, P)]

J_CUM = [0, 1, 3, 6]
J_ALL = 10


class LayerNorm:

    RING = 3

    def __init__(self, nc, m, ctx, name, banks, folded=False, fresh=False, stats=False, first=0, count=NT, ring=RING,
                 row=None):
        sb = lambda n, shape: ctx.enter_context(nc.sbuf_tensor(f"{name}_{n}", shape, F32))
        sem = lambda n: ctx.enter_context(nc.semaphore(f"{name}_{n}"))
        self.nc, self.m, self.folded, self.fresh = nc, m, folded, fresh
        self.first, self.count, self.ring = first, count, ring
        self.mv = sb("mv", [P, NT, 2])
        self.ve, self.sd, self.y0, self.y1, self.y2, self.rstd = (
            sb(n, [P, NT]) for n in ("ve", "sd", "y0", "y1", "y2", "rstd"))
        self.row = row or sb("row", [P, ring, D])
        self.bank = banks[0:ring]
        if folded:
            self.quarter = sb("quarter", [P, ring, P])
            self.fbank = banks[ring:]
            self.row_made, self.f_hi_done = sem("row_made"), sem("f_hi_done")
        self.chain, self.root, self.row_ready = sem("chain"), sem("root"), sem("row_ready")
        self.stats, self.steps = stats or fresh, 0
        self.moments = 3 if self.stats else 2
        self.turned, self.hi_done, self.lo_done = sem("turned"), sem("hi_done"), sem("lo_done")
        self.per_tile = 2 if folded else 1

    def link(self, dve, ins):
        self.steps += 1
        ins.then_inc(self.chain, 1)
        dve.wait_ge(self.chain, self.steps)

    def mine(self, x):
        return x[:, self.first:self.first + self.count]

    def scales(self, dve):
        self.variances(dve)
        self.inverses(dve)

    def variances(self, dve):
        nc, m = self.nc, self.m
        if self.stats:
            for t in self.all_tiles():
                if self.fresh:
                    dve.wait_ge(m.x_loaded[t // 2], 16)
                last = nc.vector.bn_stats(m.stats[:, t, :], m.x[:, t, :])
            self.link(dve, last)
        for t in self.all_tiles():
            last = nc.vector.bn_aggr(self.mv[:, t, :], m.stats[:, t, :])
        self.link(dve, last)
        self.link(dve, nc.vector.tensor_scalar(self.mine(self.ve), self.mine(self.mv[:, :, 1]), EPS, None, ALU.add))
        assert self.steps == self.moments

    def inverses(self, dve):
        nc = self.nc
        ve, sd, y0, y1, y2, rstd = (self.mine(x) for x in (self.ve, self.sd, self.y0, self.y1, self.y2, self.rstd))
        dve.wait_ge(self.root, 1)
        self.link(dve, nc.vector.reciprocal(y0, sd))
        self.link(dve, nc.vector.tensor_tensor(y1, y0, y0, ALU.mult))
        self.link(dve, nc.vector.tensor_tensor(y2, y1, ve, ALU.mult))
        self.link(dve, nc.vector.tensor_scalar(y1, y2, -0.5, 1.5, ALU.mult, ALU.add))
        self.link(dve, nc.vector.tensor_tensor(rstd, y0, y1, ALU.mult))

    def all_tiles(self):
        return range(self.first, self.first + self.count)

    def tokens(self, t):
        return slice((self.first + t) * P, (self.first + t + 1) * P)

    def parts(self, dve):
        self.scales(dve)
        self.rows(dve, 0)
        self.rows(dve, 1)
        for t in range(self.count):
            if t + 2 < self.count:
                self.rows(dve, t + 2)
            self.low(dve, t)

    def rows(self, dve, t):
        nc, m = self.nc, self.m
        n = self.ring
        if t >= n:
            dve.wait_ge(self.turned, t - n + 1)
        x = self.first + t
        made = nc.vector.tensor_scalar(self.row[:, t % self.ring, :], m.x[:, x, :], self.mv[:, x, 0:1],
                                       self.rstd[:, x:x + 1], ALU.subtract, ALU.mult)
        if self.folded:
            made.then_inc(self.row_made, 1)
            dve.wait_ge(self.row_made, t + 1)
            made = nc.vector.tensor_reduce(self.quarter[:, t % self.ring, :],
                                           self.row[:, t % self.ring, :].rearrange("p (k n) -> p n k", k=KT), AX_X, ALU.add)
        made.then_inc(self.row_ready, 1)

    def low(self, dve, t):
        nc, m = self.nc, self.m
        dve.wait_ge(self.hi_done, t + 1)
        nc.vector.tensor_tensor(m.h_lo[:, :, self.tokens(t)],
                                self.bank[t % self.ring][:, :].rearrange("p (k n) -> p k n", k=KT),
                                m.h_hi[:, :, self.tokens(t)].bitcast(F32), ALU.subtract).then_inc(self.lo_done, 1)
        if self.folded:
            dve.wait_ge(self.f_hi_done, t + 1)
            nc.vector.tensor_tensor(m.f_lo[:, self.tokens(t)], self.fbank[t % self.ring][:, 0:P],
                                    m.f_hi[:, self.tokens(t)].bitcast(F32), ALU.subtract).then_inc(self.lo_done, 1)

    def roots(self, act):
        act.wait_ge(self.chain, self.moments)
        self.nc.scalar.activation(self.mine(self.sd), self.mine(self.ve), ACT.Sqrt).then_inc(self.root, 1)

    def high(self, act, t):
        nc, m = self.nc, self.m
        act.wait_ge(self.turned, t + 1)
        nc.scalar.activation(m.h_hi[:, :, self.tokens(t)],
                             self.bank[t % self.ring][:, :].rearrange("p (k n) -> p k n", k=KT), ACT.Copy).then_inc(self.hi_done, 1)
        if self.folded:
            nc.scalar.activation(m.f_hi[:, self.tokens(t)], self.fbank[t % self.ring][:, 0:P],
                                 ACT.Copy).then_inc(self.f_hi_done, 1)

    def turn(self, pe, t):
        nc, m = self.nc, self.m
        if t == 0:
            pe.wait_ge(m.fetched, m.fetched_all)
        pe.wait_ge(self.row_ready, t + 1)
        n = self.ring
        if t >= n:
            self.wait(pe, t - n + 1)
        for k in range(KT):
            last = nc.tensor.transpose(self.bank[t % self.ring][:, k * P:(k + 1) * P],
                                       self.row[:, t % self.ring, k * P:(k + 1) * P], m.ident[:, :])
        if self.folded:
            last = nc.tensor.transpose(self.fbank[t % self.ring][:, 0:P], self.quarter[:, t % self.ring, :], m.ident[:, :])
        last.then_inc(self.turned, 1)

    def wait(self, pe, tiles):
        pe.wait_ge(self.lo_done, self.per_tile * tiles)


NRAW = 6
NRAW_A = 5


def load_attention_piece(sp, m, inp, g, k):
    slot = k % NRAW_A
    if k > HPG + 1:
        h = HPG * g + k - HPG - 2
        sp.dma_start(m.raw[:, slot, :], inp["L1_attn_wo"][h * P:(h + 1) * P, :]).then_inc(m.loaded[slot], 16)
        return
    name, col = ("L1_attn_wk", g) if k == 0 else ("L1_attn_wv", g) if k > HPG else ("L1_attn_wq", HPG * g + k - 1)
    src = inp[name].rearrange("(k p) n -> p k n", p=P)[:, :, col * P:(col + 1) * P]
    sp.dma_start(m.raw[:, slot, :].rearrange("p (k n) -> p k n", k=KT), src).then_inc(m.loaded[slot], 16)


def feed_forward_piece(x, s, p):
    w = FF_TILES[s % len(FF_TILES)][1]
    slot = (3 * s + p) % NRAW
    if p == 2:
        return x[0:w, slot, :]
    return x[:, slot, 0:KT * w].rearrange("p (k n) -> p k n", k=KT)


def load_feed_forward_piece(sp, m, inp, s, p):
    at, w = FF_TILES[s % len(FF_TILES)]
    if p == 2:
        src = inp["L1_down_t"][at:at + w, :]
    else:
        src = inp["L1_gate_up_t"].rearrange("(k p) n -> p k n", p=P)[:, :, FF * p + at:FF * p + at + w]
    sp.dma_start(feed_forward_piece(m.raw, s, p), src).then_inc(m.loaded[(3 * s + p) % NRAW], 16)


def attention1(nc, m, inp, fresh, ahead):
    scale = float(HD1) ** -0.5
    RING = [J_CUM[i] + i for i in range(QT)]
    RING_ALL = J_ALL + QT
    S_BANK0 = [0, 1, 0, 0]
    S_BANKS = [1, 2, 4, 4]
    S_CUM = [0, 1, 3, 7]
    S_ALL = 11
    NC = 6
    V = NC - 1
    NX = NC + 1

    with ExitStack() as ctx:
        sb = lambda n, shape, dt=F32: ctx.enter_context(nc.sbuf_tensor(f"a1_{n}", shape, dt))
        ps = lambda n: ctx.enter_context(nc.psum_tensor(f"a1_{n}", [P, 512], F32))
        sem = lambda n: ctx.enter_context(nc.semaphore(f"a1_{n}"))
        w_hi, w_lo = sb("w_hi", [P, NC, KT, P], F32R), sb("w_lo", [P, NC, KT, P], F32R)
        wo_hi, wo_lo = sb("wo_hi", [P, HPG, D], F32R), sb("wo_lo", [P, HPG, D], F32R)
        p_hi, p_lo = sb("p_hi", [P, B, NC, T], F32R), sb("p_lo", [P, B, NC, T], F32R)
        raw_p = sb("raw_p", [P, 2, T])
        rot_a, rot_b = sb("rot_a", [P, 2, T]), sb("rot_b", [P, 2, T])
        prob = [sb("prob0", [P, HPG, 3 * P]), sb("prob1", [P, HPG, 4 * P])]
        pt_hi, pt_lo = sb("pt_hi", [P, 2, 512], F32R), sb("pt_lo", [P, 2, 512], F32R)
        c_hi, c_lo = sb("c_hi", [P, 2, 512], F32R), sb("c_lo", [P, 2, 512], F32R)
        nmax, rsum, rinv = sb("nmax", [P, 2, HPG]), sb("rsum", [P, 2, HPG]), sb("rinv", [P, 2, HPG])
        score = [ps(f"score{k}") for k in range(4)]
        ring = [ps("ring0"), ps("ring1")]
        cbank, xbank = ps("cbank"), ps("xbank")
        done = 0 if fresh else QT
        ln = LayerNorm(nc, m, ctx, "n2", score, fresh=fresh, stats=True, first=done, count=NT - done)
        next_ln = LayerNorm(nc, m, ctx, "n3a", [xbank], count=QT, ring=1, row=ln.row)

        tables, stats_made = sem("tables"), sem("stats_made")
        scored, ringed, pt_used, x_made = (sem(n) for n in ("scored", "ringed", "pt_used", "x_made"))
        maxed, inverted, normed, ring_read, c_ready, rotated, v_ready = (
            sem(n) for n in ("maxed", "inverted", "normed", "ring_read", "c_ready", "rotated", "v_ready"))
        exped, pt_hi_done, c_hi_done, x_read, p_hi_done, v_hi_done, w_hi_done, wo_hi_done = (sem(n) for n in (
            "exped", "pt_hi_done", "c_hi_done", "x_read", "p_hi_done", "v_hi_done", "w_hi_done", "wo_hi_done"))
        summed, p_ready, w_ready, wo_ready = (sem(n) for n in ("summed", "p_ready", "w_ready", "wo_ready"))

        def piece(g, k):
            return k % NRAW_A, m.loaded[k % NRAW_A], 16 * (10 // NRAW_A * g + k // NRAW_A + 1)

        def projected(u, c):
            return cbank if u == 0 and c % 2 else xbank

        block = ctx.enter_context(nc.Block())

        @block.sync
        def _(sp):
            def load(g, k):
                n = 10 * g + k - NRAW_A
                if n >= 0:
                    if n % 10 < NC:
                        sp.wait_ge(w_ready, NC * (n // 10) + n % 10 + 1)
                    else:
                        sp.wait_ge(wo_ready, HPG * (n // 10) + n % 10 - NC + 1)
                load_attention_piece(sp, m, inp, g, k)

            for g in range(NG):
                for k in range(NC + HPG):
                    if g or k >= NRAW_A or fresh:
                        load(g, k)
                    if g == 0 and k == NRAW_A - 1:
                        sp.dma_start(m.cos1[:, :], m.cos1_in).then_inc(tables, 16)
                        sp.dma_start(m.sin1[:, :], m.sin1_in).then_inc(tables, 16)
            if ahead:
                sp.wait_ge(w_ready, NC * NG)
                sp.wait_ge(wo_ready, HPG * NG)
                for n in range(NRAW):
                    load_feed_forward_piece(sp, m, inp, n // 3, n % 3)
            m.loads_before = [10 // NRAW_A * NG] * NRAW_A + [0]

        @block.tensor
        def _(pe):
            def three(out, l_hi, l_lo, r_hi, r_lo, start, stop):
                nc.tensor.matmul(out, l_hi, r_hi, start=start, stop=False)
                nc.tensor.matmul(out, l_hi, r_lo, start=False, stop=False)
                return nc.tensor.matmul(out, l_lo, r_hi, start=False, stop=stop)

            def project(u, c, parts=range(KT)):
                g, b = u // 2, u % 2
                bank = projected(u, c)
                if 0 in parts:
                    pe.wait_ge(w_ready, NC * g + c + 1)
                    if u == 0 and c >= 2:
                        pe.wait_ge(x_read, c - 1)
                    elif u >= 1 and c >= 1:
                        pe.wait_ge(x_read, NC * u + c)
                    elif u >= 1:
                        pe.wait_ge(v_ready, u)
                tok = slice(b * T, (b + 1) * T)
                for k in parts:
                    last = three(bank[:, :], w_hi[:, c, k, :], w_lo[:, c, k, :], m.h_hi[:, k, tok], m.h_lo[:, k, tok],
                                 k == 0, k == KT - 1)
                if KT - 1 in parts:
                    last.then_inc(x_made, 1)

            def turn_v(u):
                pe.wait_ge(x_read, NC * (u + 1))
                for t in range(QT):
                    last = nc.tensor.transpose(xbank[:, t * P:(t + 1) * P], raw_p[:, V % 2, t * P:(t + 1) * P],
                                               m.ident[:, :])
                last.then_inc(x_made, 1)

            def scores(u, i, bank):
                b, n, per = u % 2, (i + 1) * P, HPG // S_BANKS[i]
                if i == 0:
                    pe.wait_ge(p_ready, 5 * (u + 1))
                before = 16 * u + [-3, -2 + bank, [4, 6, 8, 0][bank], 9 + bank][i]
                if before > 0:
                    pe.wait_ge(exped, before)
                out, q = score[S_BANK0[i] + bank], slice(i * P, (i + 1) * P)
                for h in range(per):
                    c = 1 + bank * per + h
                    three(out[:, h * n:(h + 1) * n], p_hi[:, b, c, q], p_lo[:, b, c, q], p_hi[:, b, 0, 0:n],
                          p_lo[:, b, 0, 0:n], h == 0, False)
                diagonal = out[:, 0:per * n].rearrange("p (h n) -> p h n", h=per)[:, :, i * P:n]
                nc.tensor.matmul(diagonal, m.ident_b[:, :], m.mask_b[:, :].unsqueeze(1).to_broadcast([P, per, P]),
                                 start=False, stop=True).then_inc(scored, 1)

            def turn(u, i, j):
                n = RING_ALL * u + RING[i] + j
                if j == 0:
                    pe.wait_ge(normed, 2 * (QT * u + i + 1))
                if n >= 2:
                    pe.wait_ge(ring_read, n - 1)
                for h in range(HPG):
                    last = nc.tensor.transpose(ring[n % 2][:, h * P:(h + 1) * P],
                                               prob[i % 2][:, h, j * P:(j + 1) * P], m.ident[:, :])
                last.then_inc(ringed, 1)

            def weigh(u, i, j):
                n, b = J_ALL * u + J_CUM[i] + j, u % 2
                pe.wait_ge(ring_read, RING_ALL * u + RING[i] + j + 1)
                if j == 0:
                    if i == 0:
                        pe.wait_ge(v_ready, u + 1)
                    if QT * u + i >= 1:
                        pe.wait_ge(c_ready, QT * u + i)
                v = slice(j * P, (j + 1) * P)
                last = three(cbank[:, :], p_hi[:, b, V, v], p_lo[:, b, V, v], pt_hi[:, n % 2, :], pt_lo[:, n % 2, :],
                             j == 0, j == i)
                last.then_inc(pt_used, 1)

            def out_project(u, i):
                g, n = u // 2, RING_ALL * u + RING[i] + i + 1
                pe.wait_ge(c_ready, QT * u + i + 1)
                pe.wait_ge(ring_read, n - 1)
                for h in range(HPG):
                    if u % 2 == 0 and i == 0:
                        pe.wait_ge(wo_ready, HPG * g + h + 1)
                    last = three(ring[n % 2][:, :], c_hi[:, i % 2, h * P:(h + 1) * P], c_lo[:, i % 2, h * P:(h + 1) * P],
                                 wo_hi[:, h, :], wo_lo[:, h, :], h == 0, h == HPG - 1)
                last.then_inc(ringed, 1)

            early = 0 if done else QT + 2
            for t in range(early):
                ln.turn(pe, t)
            if not done:
                ln.wait(pe, QT)
            for c in range(NC):
                project(0, c)
                if c == 0:
                    for t in range(early, ln.count):
                        ln.turn(pe, t)
            ln.wait(pe, ln.count)
            scores(0, 0, 0)
            turn_v(0)
            for u in range(2 * NG):
                more = u + 1 < 2 * NG
                turn(u, 0, 0)
                scores(u, 1, 0)
                scores(u, 1, 1)
                if more:
                    project(u + 1, 0)
                weigh(u, 0, 0)
                if more:
                    project(u + 1, 1)
                out_project(u, 0)
                turn(u, 1, 0)
                scores(u, 2, 0)
                turn(u, 1, 1)
                if more:
                    project(u + 1, 2)
                if ahead and not more:
                    pe.wait_ge(v_ready, u + 1)
                    next_ln.turn(pe, 0)
                scores(u, 2, 1)
                weigh(u, 1, 0)
                scores(u, 2, 2)
                weigh(u, 1, 1)
                scores(u, 2, 3)
                if more:
                    project(u + 1, 3)
                if ahead and not more:
                    next_ln.turn(pe, 1)
                out_project(u, 1)
                turn(u, 2, 0)
                scores(u, 3, 0)
                turn(u, 2, 1)
                scores(u, 3, 1)
                turn(u, 2, 2)
                weigh(u, 2, 0)
                weigh(u, 2, 1)
                scores(u, 3, 2)
                weigh(u, 2, 2)
                scores(u, 3, 3)
                if more:
                    project(u + 1, 4)
                if ahead and not more:
                    next_ln.turn(pe, 2)
                out_project(u, 2)
                turn(u, 3, 0)
                if more:
                    project(u + 1, V, [0])
                if ahead and not more:
                    next_ln.turn(pe, 3)
                turn(u, 3, 1)
                if more:
                    project(u + 1, V, [1])
                turn(u, 3, 2)
                weigh(u, 3, 0)
                weigh(u, 3, 1)
                turn(u, 3, 3)
                if more:
                    scores(u + 1, 0, 0)
                weigh(u, 3, 2)
                weigh(u, 3, 3)
                if more:
                    project(u + 1, V, [2, 3])
                out_project(u, 3)
                if more:
                    turn_v(u + 1)

        @block.vector
        def _(dve):
            def maxima(u, i, banks):
                per, n = HPG // S_BANKS[i], (i + 1) * P
                for k in banks:
                    dve.wait_ge(scored, S_ALL * u + S_CUM[i] + k + 1)
                    if k == 0 and QT * u + i >= 2:
                        dve.wait_ge(exped, 16 * u + 4 * i - 4)
                    nc.vector.tensor_reduce(nmax[:, i % 2, k * per:(k + 1) * per],
                                            score[S_BANK0[i] + k][:, 0:per * n].rearrange("p (h n) -> p h n", h=per),
                                            AX_X, ALU.max, negate=True).then_inc(maxed, 1)

            def normalise(u, i):
                for pair in range(2):
                    dve.wait_ge(exped, 16 * u + 4 * i + 2 * (pair + 1))
                    heads = slice(2 * pair, 2 * pair + 2)
                    nc.vector.reciprocal(rinv[:, i % 2, heads], rsum[:, i % 2, heads]).then_inc(inverted, 1)
                    dve.wait_ge(inverted, 2 * (QT * u + i) + pair + 1)
                    for h in (2 * pair, 2 * pair + 1):
                        pr = prob[i % 2][:, h, 0:(i + 1) * P]
                        last = nc.vector.tensor_scalar(pr, pr, rinv[:, i % 2, h:h + 1], None, ALU.mult)
                    last.then_inc(normed, 1)

            def low(u, i, j):
                n = J_ALL * u + J_CUM[i] + j
                dve.wait_ge(pt_hi_done, n + 1)
                nc.vector.tensor_tensor(pt_lo[:, n % 2, :], ring[(RING[i] + j) % 2][:, :],
                                        pt_hi[:, n % 2, :].bitcast(F32), ALU.subtract).then_inc(ring_read, 1)

            def head_low(u, i):
                dve.wait_ge(c_hi_done, QT * u + i + 1)
                nc.vector.tensor_tensor(c_lo[:, i % 2, :], cbank[:, :], c_hi[:, i % 2, :].bitcast(F32),
                                        ALU.subtract).then_inc(c_ready, 1)

            def rotate(u, c):
                dve.wait_ge(x_read, NC * u + c + 1)
                n = 5 * u + c
                if n >= 2:
                    dve.wait_ge(p_ready, 5 * u + (c - 1 if c >= 2 else -c))
                r = raw_p[:, c % 2, :]
                nc.vector.tensor_tensor(rot_a[:, c % 2, :], r, m.cos1[:, :], ALU.mult)
                nc.vector.tensor_tensor(rot_b[0:64, c % 2, :], raw_p[64:128, c % 2, :], m.sin1[64:128, :], ALU.mult)
                nc.vector.tensor_tensor(rot_b[64:128, c % 2, :], raw_p[0:64, c % 2, :], m.sin1[0:64, :],
                                        ALU.mult).then_inc(rotated, 1)

            def v_low(u):
                dve.wait_ge(v_hi_done, u + 1)
                nc.vector.tensor_tensor(p_lo[:, u % 2, V, :], xbank[:, :], p_hi[:, u % 2, V, :].bitcast(F32),
                                        ALU.subtract).then_inc(v_ready, 1)

            def add_out(u, i):
                n = RING_ALL * u + RING[i] + i + 1
                dve.wait_ge(ringed, n + 1)
                xt = m.x[:, (u % 2) * QT + i, :]
                nc.vector.tensor_tensor(xt, ring[n % 2][:, :], xt, ALU.add).then_inc(ring_read, 1)
                if u == 2 * NG - 2:
                    dve.wait_ge(ring_read, n + 1)
                    nc.vector.bn_stats(m.stats[:, (u % 2) * QT + i, :], xt).then_inc(stats_made, 1)

            ln.parts(dve)
            dve.wait_ge(tables, 32)
            for c in range(V):
                rotate(0, c)
                dve.wait_ge(rotated, c + 1)
                nc.vector.tensor_tensor(rot_a[:, c % 2, :], rot_a[:, c % 2, :], rot_b[:, c % 2, :],
                                        ALU.add).then_inc(summed, 1)
            maxima(0, 0, [0])
            normalise(0, 0)
            v_low(0)
            for u in range(2 * NG):
                more = u + 1 < 2 * NG
                low(u, 0, 0)
                maxima(u, 1, [0, 1])
                normalise(u, 1)
                head_low(u, 0)
                if more:
                    rotate(u + 1, 0)
                    rotate(u + 1, 1)
                if ahead and not more:
                    dve.wait_ge(stats_made, QT)
                    next_ln.scales(dve)
                    next_ln.rows(dve, 0)
                add_out(u, 0)
                low(u, 1, 0)
                maxima(u, 2, [0])
                low(u, 1, 1)
                maxima(u, 2, [1])
                if ahead and not more:
                    next_ln.low(dve, 0)
                if more:
                    rotate(u + 1, 2)
                head_low(u, 1)
                maxima(u, 2, [2, 3])
                if ahead and not more:
                    next_ln.rows(dve, 1)
                normalise(u, 2)
                if more:
                    rotate(u + 1, 3)
                if ahead and not more:
                    next_ln.low(dve, 1)
                    next_ln.rows(dve, 2)
                add_out(u, 1)
                low(u, 2, 0)
                maxima(u, 3, [0])
                low(u, 2, 1)
                low(u, 2, 2)
                maxima(u, 3, [1, 2])
                head_low(u, 2)
                maxima(u, 3, [3])
                normalise(u, 3)
                if more:
                    rotate(u + 1, 4)
                if ahead and not more:
                    next_ln.low(dve, 2)
                    next_ln.rows(dve, 3)
                add_out(u, 2)
                low(u, 3, 0)
                low(u, 3, 1)
                if ahead and not more:
                    next_ln.low(dve, 3)
                low(u, 3, 2)
                low(u, 3, 3)
                if more:
                    maxima(u + 1, 0, [0])
                head_low(u, 3)
                if more:
                    normalise(u + 1, 0)
                add_out(u, 3)
                if more:
                    v_low(u + 1)

        @block.scalar
        def _(act):
            def exponentials(u, i, heads):
                per = HPG // S_BANKS[i]
                for h in heads:
                    act.wait_ge(maxed, S_ALL * u + S_CUM[i] + h // per + 1)
                    if h == 0 and QT * u + i >= 2:
                        s = QT * u + i - 2
                        act.wait_ge(ringed, RING_ALL * (s // QT) + RING[s % QT] + s % QT + 1)
                    n = (i + 1) * P
                    nc.scalar.activation(prob[i % 2][:, h, 0:n],
                                         score[S_BANK0[i] + h // per][:, (h % per) * n:(h % per + 1) * n], ACT.Exp,
                                         bias=nmax[:, i % 2, h:h + 1], accum_out=rsum[:, i % 2, h:h + 1],
                                         ).then_inc(exped, 1)

            def high(u, i, j):
                n = J_ALL * u + J_CUM[i] + j
                act.wait_ge(ringed, RING_ALL * u + RING[i] + j + 1)
                if n >= 2:
                    act.wait_ge(pt_used, n - 1)
                nc.scalar.activation(pt_hi[:, n % 2, :], ring[(RING[i] + j) % 2][:, :], ACT.Copy).then_inc(pt_hi_done, 1)

            def head_high(u, i):
                act.wait_ge(pt_used, J_ALL * u + J_CUM[i] + i + 1)
                if QT * u + i >= 2:
                    s = QT * u + i - 2
                    act.wait_ge(ringed, RING_ALL * (s // QT) + RING[s % QT] + s % QT + 2)
                nc.scalar.activation(c_hi[:, i % 2, :], cbank[:, :], ACT.Copy).then_inc(c_hi_done, 1)

            def read_out(u, c):
                act.wait_ge(x_made, NX * u + c + 1)
                if c >= 2:
                    act.wait_ge(rotated, 5 * u + c - 1)
                elif u >= 1:
                    act.wait_ge((rotated, x_made)[c], (5 * u, NX * u)[c])
                nc.scalar.activation(raw_p[:, c % 2, :], projected(u, c)[:, :], ACT.Copy,
                                     scale=scale if 1 <= c < V else 1.0).then_inc(x_read, 1)

            def part_high(u, c):
                act.wait_ge(summed, 5 * u + c + 1)
                nc.scalar.activation(p_hi[:, u % 2, c, :], rot_a[:, c % 2, :], ACT.Copy).then_inc(p_hi_done, 1)

            def v_high(u):
                act.wait_ge(x_made, NX * (u + 1))
                nc.scalar.activation(p_hi[:, u % 2, V, :], xbank[:, :], ACT.Copy).then_inc(v_hi_done, 1)

            def weights_high(g, c):
                slot, done, count = piece(g, c)
                act.wait_ge(done, count)
                if g >= 1:
                    act.wait_ge(x_made, NX * (2 * g - 1) + c + 1)
                nc.scalar.activation(w_hi[:, c, :, :], m.raw[:, slot, :].rearrange("p (k n) -> p k n", k=KT),
                                     ACT.Copy).then_inc(w_hi_done, 1)

            def out_weights_high(u, heads):
                if u % 2:
                    return
                g = u // 2
                for h in heads:
                    slot, done, count = piece(g, NC + h)
                    act.wait_ge(done, count)
                    if g >= 1:
                        act.wait_ge(ringed, RING_ALL * 2 * g)
                    nc.scalar.activation(wo_hi[:, h, :], m.raw[:, slot, :], ACT.Copy).then_inc(wo_hi_done, 1)

            if not done:
                ln.roots(act)
            for c in range(2):
                weights_high(0, c)
            if done:
                ln.roots(act)
            for t in range(ln.count):
                ln.high(act, t)
                if t + 2 < NC:
                    weights_high(0, t + 2)
            for c in range(NC):
                read_out(0, c)
                if c >= 1:
                    part_high(0, c - 1)
            exponentials(0, 0, range(HPG))
            out_weights_high(0, [0])
            v_high(0)
            for u in range(2 * NG):
                g, more = u // 2, u + 1 < 2 * NG
                split = u % 2 == 0 and g + 1 < NG
                high(u, 0, 0)
                out_weights_high(u, [1])
                out_weights_high(u, [2])
                exponentials(u, 1, range(HPG))
                if more:
                    read_out(u + 1, 0)
                out_weights_high(u, [3])
                head_high(u, 0)
                if more:
                    read_out(u + 1, 1)
                    part_high(u + 1, 0)
                if ahead and not more:
                    next_ln.roots(act)
                high(u, 1, 0)
                high(u, 1, 1)
                exponentials(u, 2, [0])
                if more:
                    part_high(u + 1, 1)
                    read_out(u + 1, 2)
                exponentials(u, 2, [1])
                if ahead and not more:
                    next_ln.high(act, 0)
                head_high(u, 1)
                exponentials(u, 2, [2, 3])
                if more:
                    part_high(u + 1, 2)
                    read_out(u + 1, 3)
                if ahead and not more:
                    next_ln.high(act, 1)
                if split:
                    weights_high(g + 1, 0)
                    weights_high(g + 1, 1)
                high(u, 2, 0)
                high(u, 2, 1)
                if more:
                    part_high(u + 1, 3)
                high(u, 2, 2)
                exponentials(u, 3, [0])
                head_high(u, 2)
                exponentials(u, 3, [1, 2])
                exponentials(u, 3, [3])
                if split:
                    weights_high(g + 1, 2)
                if more:
                    read_out(u + 1, 4)
                if ahead and not more:
                    next_ln.high(act, 2)
                if split:
                    weights_high(g + 1, 3)
                high(u, 3, 0)
                high(u, 3, 1)
                if more:
                    part_high(u + 1, 4)
                if ahead and not more:
                    next_ln.high(act, 3)
                high(u, 3, 2)
                high(u, 3, 3)
                head_high(u, 3)
                if more:
                    exponentials(u + 1, 0, [0, 1])
                    exponentials(u + 1, 0, [2, 3])
                if split:
                    weights_high(g + 1, 4)
                if more:
                    read_out(u + 1, V)
                if split:
                    weights_high(g + 1, 5)
                if more:
                    out_weights_high(u + 1, [0])
                    v_high(u + 1)

        @block.gpsimd
        def _(pool):
            def part_sum(u, c):
                pool.wait_ge(rotated, 5 * u + c + 1)
                nc.gpsimd.tensor_tensor(rot_a[:, c % 2, :], rot_a[:, c % 2, :], rot_b[:, c % 2, :],
                                        ALU.add).then_inc(summed, 1)

            def part_low(u, c):
                pool.wait_ge(p_hi_done, 5 * u + c + 1)
                nc.gpsimd.tensor_tensor(p_lo[:, u % 2, c, :], rot_a[:, c % 2, :], p_hi[:, u % 2, c, :].bitcast(F32),
                                        ALU.subtract).then_inc(p_ready, 1)

            def weights_low(g, c):
                pool.wait_ge(w_hi_done, NC * g + c + 1)
                nc.gpsimd.tensor_tensor(w_lo[:, c, :, :], m.raw[:, piece(g, c)[0], :].rearrange("p (k n) -> p k n", k=KT),
                                        w_hi[:, c, :, :].bitcast(F32), ALU.subtract).then_inc(w_ready, 1)

            def out_weights_low(g):
                for h in range(HPG):
                    pool.wait_ge(wo_hi_done, HPG * g + h + 1)
                    nc.gpsimd.tensor_tensor(wo_lo[:, h, :], m.raw[:, piece(g, NC + h)[0], :],
                                            wo_hi[:, h, :].bitcast(F32), ALU.subtract).then_inc(wo_ready, 1)

            for c in range(NC):
                weights_low(0, c)
            for c in range(V):
                part_low(0, c)
            for u in range(2 * NG):
                g, more = u // 2, u + 1 < 2 * NG
                split = u % 2 == 0 and g + 1 < NG
                if u % 2 == 0:
                    out_weights_low(g)
                for c in range(V):
                    if more:
                        part_sum(u + 1, c)
                        part_low(u + 1, c)
                    if split and c >= 2:
                        weights_low(g + 1, 2 * (c - 2))
                        weights_low(g + 1, 2 * (c - 2) + 1)


def project0(nc, m, wqkv, fresh):
    NQ, NKV = NG * HPG, NG
    QW, KW = NQ * HD0, NKV * HD0
    W = QW + 2 * KW
    half = HD0 // 2
    w_v = wqkv.rearrange("(k p) n -> p k n", p=P)

    def twice(x):
        n = x.shape[1] // HD0
        return x.rearrange("p (h n) -> p h n", n=HD0).unsqueeze(2).to_broadcast([P, n, 2, HD0])

    with ExitStack() as ctx:
        sb = lambda n, shape, dt=F32: ctx.enter_context(nc.sbuf_tensor(f"p0_{n}", shape, dt))
        ps = lambda n: ctx.enter_context(nc.psum_tensor(f"p0_{n}", [P, 512], F32))
        sem = lambda n: ctx.enter_context(nc.semaphore(f"p0_{n}"))
        raw_w = sb("raw_w", [P, KT, W])
        w_hi, w_lo = sb("w_hi", [P, KT, W], F32R), sb("w_lo", [P, KT, W], F32R)
        row, rot_a, rot_b = (sb(n, [P, 2, QW + KW]) for n in ("row", "rot_a", "rot_b"))
        qbank, kvbank = [ps("qbank0"), ps("qbank1")], [ps("kvbank0"), ps("kvbank1")]
        ln = LayerNorm(nc, m, ctx, "n0", [ps(f"turned{k}") for k in range(LayerNorm.RING)], fresh=fresh)
        loaded, tables = [sem(f"loaded{k}") for k in range(KT)], sem("tables")
        w_hi_done, w_ready, v_ready, made, read, rotated, summed, hi_done, q_ready, k_ready = (sem(n) for n in (
            "w_hi_done", "w_ready", "v_ready", "made", "read", "rotated", "summed", "hi_done", "q_ready", "k_ready"))
        block = ctx.enter_context(nc.Block())

        @block.sync
        def _(sp):
            for k in range(KT):
                sp.dma_start(raw_w[:, k, :], w_v[:, k, :]).then_inc(loaded[k], 16)
            for to, of in m.tables0:
                sp.dma_start(to[:, :, :], of).then_inc(tables, 16)

        @block.tensor
        def _(pe):
            ln.turn(pe, 0)
            ln.turn(pe, 1)
            for t in range(NT):
                if t + 2 < NT:
                    ln.turn(pe, t + 2)
                ln.wait(pe, t + 1)
                if t >= 2:
                    pe.wait_ge(read, 3 * (t - 1))
                    pe.wait_ge(v_ready, t)
                for bank, cols in ((qbank, slice(0, QW)), (kvbank, slice(QW, W))):
                    n = cols.stop - cols.start
                    for k in range(KT):
                        if t == 0:
                            pe.wait_ge(w_ready, k + 1)
                        h = slice(t * P, (t + 1) * P)
                        out = bank[t % 2][:, 0:n]
                        nc.tensor.matmul(out, m.h_hi[:, k, h], w_hi[:, k, cols], start=(k == 0), stop=False)
                        nc.tensor.matmul(out, m.h_hi[:, k, h], w_lo[:, k, cols], start=False, stop=False)
                        last = nc.tensor.matmul(out, m.h_lo[:, k, h], w_hi[:, k, cols], start=False, stop=(k == KT - 1))
                    last.then_inc(made, 1)

        @block.scalar
        def _(act):
            def high(t):
                act.wait_ge(summed, t + 1)
                r = rot_a[:, t % 2, :]
                nc.scalar.activation(m.q2[:, t, :, 0:4:2, :], twice(r[:, 0:QW]), ACT.Copy).then_inc(hi_done, 1)
                nc.scalar.activation(m.k2[:, t, :, 0:2, :], twice(r[:, QW:QW + KW]), ACT.Copy).then_inc(hi_done, 1)

            for k in range(KT):
                act.wait_ge(loaded[k], 16)
                nc.scalar.activation(w_hi[:, k, :], raw_w[:, k, :], ACT.Copy).then_inc(w_hi_done, 1)
                if k == 0:
                    ln.roots(act)
            ln.high(act, 0)
            for t in range(NT):
                if t + 1 < NT:
                    ln.high(act, t + 1)
                if t >= 2:
                    act.wait_ge(rotated, t - 1)
                act.wait_ge(made, 2 * t + 1)
                nc.scalar.activation(row[:, t % 2, 0:QW], qbank[t % 2][:, :], ACT.Copy,
                                     scale=float(HD0) ** -0.5).then_inc(read, 1)
                act.wait_ge(made, 2 * t + 2)
                nc.scalar.activation(row[:, t % 2, QW:QW + KW], kvbank[t % 2][:, 0:KW], ACT.Copy).then_inc(read, 1)
                nc.scalar.activation(m.vw[:, t, :, :, 0:HD0], twice(kvbank[t % 2][:, KW:2 * KW]), ACT.Copy).then_inc(read, 1)
                if t >= 1:
                    high(t - 1)
            high(NT - 1)

        @block.vector
        def _(dve):
            def low(t):
                dve.wait_ge(hi_done, 2 * t + 2)
                nc.vector.tensor_tensor(m.q2[:, t, :, 1:4:2, :], twice(rot_a[:, t % 2, 0:QW]),
                                        m.q2[:, t, :, 0:4:2, :].bitcast(F32), ALU.subtract).then_inc(q_ready, 1)

            for t in range(NT):
                nc.vector.memset(m.vw[:, t, :, :, HD0:HD0 + 1].bitcast(F32), 1.0)
            nc.vector.memset(m.vw[:, :, :, 1, HD0 + 1:2 * HD0 + 1].bitcast(F32), 0.0).then_inc(v_ready, 1)
            ln.scales(dve)
            for t in range(3):
                ln.rows(dve, t)
            ln.low(dve, 0)
            dve.wait_ge(tables, 16 * len(m.tables0))
            for t in range(NT):
                if t + 3 < NT:
                    ln.rows(dve, t + 3)
                if t + 1 < NT:
                    ln.low(dve, t + 1)
                dve.wait_ge(read, 3 * t + 3)
                nc.vector.tensor_tensor(m.vw[:, t, :, 0, HD0 + 1:2 * HD0 + 1],
                                        kvbank[t % 2][:, KW:2 * KW].rearrange("p (g n) -> p g n", n=HD0),
                                        m.vw[:, t, :, 0, 0:HD0].bitcast(F32), ALU.subtract).then_inc(v_ready, 1)
                if t >= 2:
                    dve.wait_ge(k_ready, t - 1)
                    dve.wait_ge(q_ready, t - 1)
                table = lambda x, n: x[:, t % QT, :].unsqueeze(1).to_broadcast([P, n, half])
                heads = (QW + KW) // HD0
                nc.vector.tensor_tensor(rot_a[:, t % 2, :].rearrange("p (h n) -> p h n", n=half),
                                        row[:, t % 2, :].rearrange("p (h n) -> p h n", n=half),
                                        table(m.cos0, 2 * heads), ALU.mult)
                src = row[:, t % 2, :].rearrange("p (h s n) -> p h s n", s=2, n=half)
                dst = rot_b[:, t % 2, :].rearrange("p (h s n) -> p h s n", s=2, n=half)
                nc.vector.tensor_tensor(dst[:, :, 0, :], src[:, :, 1, :], table(m.nsin0, heads), ALU.mult)
                nc.vector.tensor_tensor(dst[:, :, 1, :], src[:, :, 0, :], table(m.sin0, heads),
                                        ALU.mult).then_inc(rotated, 1)
                if t >= 1:
                    low(t - 1)
            low(NT - 1)

        @block.gpsimd
        def _(pool):
            for k in range(KT):
                pool.wait_ge(w_hi_done, k + 1)
                nc.gpsimd.tensor_tensor(w_lo[:, k, :], raw_w[:, k, :], w_hi[:, k, :].bitcast(F32),
                                        ALU.subtract).then_inc(w_ready, 1)
            for t in range(NT):
                pool.wait_ge(rotated, t + 1)
                nc.gpsimd.tensor_tensor(rot_a[:, t % 2, :], rot_a[:, t % 2, :], rot_b[:, t % 2, :],
                                        ALU.add).then_inc(summed, 1)
                pool.wait_ge(hi_done, 2 * t + 2)
                nc.gpsimd.tensor_tensor(m.k2[:, t, :, 2:4, :], twice(rot_a[:, t % 2, QW:QW + KW]),
                                        m.k2[:, t, :, 0:2, :].bitcast(F32), ALU.subtract).then_inc(k_ready, 1)


def attend0(nc, m, wo):
    wo_v = wo.rearrange("(k p) n -> p k n", p=P)
    TICKS = J_ALL
    S_BANKS = [1, 2, 4, 4]
    S_CUM = [0, 1, 3, 7]
    S_ALL = 11
    NS = 3
    TU = 1 + QT
    NE, NP = 3, 5
    TURN = {1: (1, 0), 2: (1, 1), 4: (1, 2), 5: (1, 3), 7: (1, 4)}
    SCORE = {5: [(1, 0, 0)], 6: [(1, 1, 0), (1, 1, 1)], 7: [(1, 2, 0), (1, 2, 1)], 8: [(1, 2, 2), (1, 2, 3)],
             9: [(1, 3, 0), (1, 3, 1)], 1: [(0, 3, 2)], 2: [(0, 3, 3)]}
    SHIFT = {6: (1, 0), 8: (1, 1), 9: (1, 2), 3: (0, 3)}
    AHEAD = 2
    BEHIND = 2
    LAST = [J_CUM[i] + i + BEHIND for i in range(QT)]
    END = {k % TICKS: (-(k // TICKS), i) for i, k in enumerate(LAST)}
    BACK = {(k + 2) % TICKS: (-((k + 2) // TICKS), i) for i, k in enumerate(LAST)}
    V1 = HD0 + 1
    VW = HD0 + V1
    S64 = slice(64, 64 + 2 * HPG)

    def pair(mm):
        k = mm % TICKS
        i = max(i for i in range(QT) if J_CUM[i] <= k)
        return mm // TICKS, i, k - J_CUM[i]

    def planned(table, u, k):
        if k not in table:
            return []
        entries = table[k] if isinstance(table[k], list) else [table[k]]
        return [(u + e[0],) + e[1:] for e in entries if 0 <= u + e[0] < 2 * NG]

    ticks = [(u, k) for u in range(-1, 2 * NG + 1) for k in range(TICKS)]
    DRAIN = ticks.index((2 * NG, BEHIND))

    with ExitStack() as ctx:
        sb = lambda n, shape, dt=F32: ctx.enter_context(nc.sbuf_tensor(f"a0_{n}", shape, dt))
        ps = lambda n: ctx.enter_context(nc.psum_tensor(f"a0_{n}", [P, 512], F32))
        sem = lambda n: ctx.enter_context(nc.semaphore(f"a0_{n}"))
        raw_wo = sb("raw_wo", [P, KT, D])
        wo_hi, wo_lo = sb("wo_hi", [P, KT, D], F32R), sb("wo_lo", [P, KT, D], F32R)
        k_rows = sb("k_rows", [P, B, T], F32R)
        q_rows = sb("q_rows", [P, QT, HPG, P], F32R)
        nmax = sb("nmax", [P, QT, HPG])
        split = sb("split", [P, P])
        prob = sb("prob", [P, NE, 512])
        p_hi, p_lo = sb("p_hi", [P, NP, 512], F32R), sb("p_lo", [P, NP, 512], F32R)
        head_t = sb("head_t", [P, 2, 512])
        rsum, head_sum = sb("rsum", [P, 2, HPG]), sb("head_sum", [P, 2, HPG, HD0])
        head = sb("head", [P, NT, NG * HPG, HD0])
        c_hi, c_lo = sb("c_hi", [P, 2, KT, P], F32R), sb("c_lo", [P, 2, KT, P], F32R)
        score = [ps(f"score{k}") for k in range(NS)]
        turned = [ps("turned0"), ps("turned1")]
        qkbank, hbank, cbank = ps("qkbank"), ps("hbank"), ps("cbank")
        loaded, ones_set, split_set = sem("loaded"), sem("ones_set"), sem("split_set")
        qk_turned, scored, t_scored, weighed, shifted, backed = (sem(n) for n in (
            "qk_turned", "scored", "t_scored", "weighed", "shifted", "backed"))
        maxed, parted, max_rows, c_read, divided, head_ready = (sem(n) for n in (
            "maxed", "parted", "max_rows", "c_read", "divided", "head_ready"))
        qk_read, exped, p_hi_done, p_ready = (sem(n) for n in ("qk_read", "exped", "p_hi_done", "p_ready"))
        wo_hi_done, wo_ready, c_turned, c_hi_done, c_ready, projected, added = (sem(n) for n in (
            "wo_hi_done", "wo_ready", "c_turned", "c_hi_done", "c_ready", "projected", "added"))
        block = ctx.enter_context(nc.Block())

        @block.sync
        def _(sp):
            sp.dma_start(raw_wo[:, :, :], wo_v).then_inc(loaded, 16)

        @block.tensor
        def _(pe):
            count = {"turned": 0, "shifted": 0}

            def wait_qkbank():
                if count["turned"]:
                    pe.wait_ge(qk_read, count["turned"])
                if count["shifted"]:
                    pe.wait_ge(max_rows, count["shifted"])

            def turn_qk(u, s):
                wait_qkbank()
                for r in range(QT):
                    g, b = u // 2, u % 2
                    if s == 0:
                        x = m.k2[:, b * QT + r, g, :, :]
                    else:
                        x = m.q2[:, b * QT + s - 1, HPG * g + r, :, :]
                    last = nc.tensor.transpose(qkbank[0:64, r * P:(r + 1) * P],
                                               x.bitcast(F32).rearrange("p s n -> p (s n)"), m.ident[:, :])
                last.then_inc(qk_turned, 1)
                count["turned"] += 1

            def scores(u, i, bank):
                per, n, e = HPG // S_BANKS[i], (i + 1) * P, S_ALL * u + S_CUM[i] + bank
                pe.wait_ge(qk_read, TU * u + i + 2)
                if e >= NS:
                    pe.wait_ge(maxed, e - NS + 1)
                out = score[e % NS]
                for h in range(per):
                    nc.tensor.matmul(out[:, h * n:(h + 1) * n], q_rows[0:64, i, bank * per + h, :],
                                     k_rows[0:64, u % 2, 0:n], start=(h == 0), stop=False)
                diagonal = out[:, 0:per * n].rearrange("p (h n) -> p h n", h=per)[:, :, i * P:n]
                nc.tensor.matmul(diagonal, m.ident_b[:, :], m.mask_b[:, :].unsqueeze(1).to_broadcast([P, per, P]),
                                 start=False, stop=True).then_inc(scored, 1)

            def turned_scores(mm):
                u, i, j = pair(mm)
                if j == 0:
                    pe.wait_ge(max_rows, QT * u + i + 1)
                if mm == 0:
                    pe.wait_ge(ones_set, 1)
                if mm >= 2:
                    pe.wait_ge(exped, mm - 1)
                out = turned[mm % 2][:, :].rearrange("p (h n) -> p h n", h=HPG)
                last = nc.tensor.matmul(out, k_rows[0:S64.stop, u % 2, j * P:(j + 1) * P], q_rows[0:S64.stop, i, :, :],
                                        start=True, stop=(j < i))
                if j == i:
                    last = nc.tensor.matmul(out, m.ident_b[:, :], m.mask_t_b[:, :].unsqueeze(1).to_broadcast([P, HPG, P]),
                                            start=False, stop=True)
                last.then_inc(t_scored, 1)

            def weigh(mm):
                u, i, j = pair(mm)
                pe.wait_ge(p_ready, mm + 1)
                if j == 0 and QT * u + i >= 1:
                    pe.wait_ge(c_read, QT * u + i)
                v = m.vw[:, (u % 2) * QT + j, u // 2, :, :]
                nc.tensor.matmul(cbank[0:VW, :], v[:, 0, :], p_hi[:, mm % NP, :], start=(j == 0), stop=False)
                nc.tensor.matmul(cbank[0:VW, :], v[:, 1, :], p_lo[:, mm % NP, :], start=False,
                                 stop=(j == i)).then_inc(weighed, 1)

            def shift_maxima(u, i):
                pe.wait_ge(parted, 2 * (QT * u + i + 1))
                wait_qkbank()
                nc.tensor.transpose(qkbank[:, 0:P], split[:, :], m.ident[:, :]).then_inc(shifted, 1)
                count["shifted"] += 1

            def turn_back(u, i):
                n = QT * u + i
                pe.wait_ge(c_read, n + 1)
                if n >= 1:
                    pe.wait_ge(divided, 3 * n)
                for h in range(HPG):
                    last = nc.tensor.transpose(hbank[:, h * VW:(h + 1) * VW], head_t[0:VW, n % 2, h * P:(h + 1) * P],
                                               m.ident[0:VW, 0:VW])
                last.then_inc(backed, 1)

            def tick(u, k):
                mm = TICKS * u + k
                for step in planned(BACK, u, k):
                    turn_back(*step)
                for item in planned(SCORE, u, k):
                    scores(*item)
                if 0 <= mm - BEHIND < TICKS * 2 * NG:
                    weigh(mm - BEHIND)
                for step in planned(SHIFT, u, k):
                    shift_maxima(*step)
                if 0 <= mm + AHEAD < TICKS * 2 * NG:
                    turned_scores(mm + AHEAD)
                for item in planned(TURN, u, k):
                    turn_qk(*item)

            def turn_tile(t):
                pe.wait_ge(head_ready, QT * (2 * NG - (t < QT)))
                if t < 2:
                    pe.wait_ge(exped, TICKS * 2 * NG)
                else:
                    pe.wait_ge(c_ready, t - 1)
                for k in range(KT):
                    heads = slice(k * P // HD0, (k + 1) * P // HD0)
                    last = nc.tensor.transpose(turned[t % 2][:, k * P:(k + 1) * P],
                                               head[:, t, heads, :].rearrange("p h n -> p (h n)"), m.ident[:, :])
                last.then_inc(c_turned, 1)

            def project_tile(t):
                pe.wait_ge(c_ready, t + 1)
                if t == 0:
                    pe.wait_ge(wo_ready, KT)
                    pe.wait_ge(maxed, S_ALL * 2 * NG)
                if t >= NS:
                    pe.wait_ge(added, t - NS + 1)
                for k in range(KT):
                    out = score[t % NS][:, :]
                    nc.tensor.matmul(out, c_hi[:, t % 2, k, :], wo_hi[:, k, :], start=(k == 0), stop=False)
                    nc.tensor.matmul(out, c_hi[:, t % 2, k, :], wo_lo[:, k, :], start=False, stop=False)
                    last = nc.tensor.matmul(out, c_lo[:, t % 2, k, :], wo_hi[:, k, :], start=False, stop=(k == KT - 1))
                last.then_inc(projected, 1)

            for at in ticks[:DRAIN]:
                tick(*at)
            turn_tile(0)
            turn_tile(1)
            project_tile(0)
            for at in ticks[DRAIN:]:
                tick(*at)
            for t in range(1, NT):
                if t + 1 < NT:
                    turn_tile(t + 1)
                project_tile(t)

        @block.vector
        def _(dve):
            def maxima(u, i, bank):
                per, n, e = HPG // S_BANKS[i], (i + 1) * P, S_ALL * u + S_CUM[i] + bank
                dve.wait_ge(scored, e + 1)
                nc.vector.tensor_reduce(nmax[:, i, bank * per:(bank + 1) * per],
                                        score[e % NS][:, 0:per * n].rearrange("p (h n) -> p h n", h=per),
                                        AX_X, ALU.max, negate=True).then_inc(maxed, 1)

            def part_maxima(u, i):
                n = QT * u + i
                hi, lo = slice(64, 64 + HPG), slice(64 + HPG, 64 + 2 * HPG)
                dve.wait_ge(maxed, S_ALL * u + S_CUM[i] + S_BANKS[i])
                if n == 0:
                    dve.wait_ge(split_set, 1)
                else:
                    dve.wait_ge(shifted, n)
                nc.vector.tensor_copy(split[:, hi].bitcast(F32R), nmax[:, i, :]).then_inc(parted, 1)
                dve.wait_ge(parted, 2 * n + 1)
                nc.vector.tensor_tensor(split[:, lo], nmax[:, i, :], split[:, hi], ALU.subtract).then_inc(parted, 1)

            def spread_maxima(u, i):
                n = QT * u + i
                dve.wait_ge(shifted, n + 1)
                if u >= 1:
                    dve.wait_ge(t_scored, TICKS * (u - 1) + J_CUM[i] + i + 1)
                nc.vector.tensor_tensor(q_rows[S64, i, :, :],
                                        qkbank[S64, 0:P].unsqueeze(1).to_broadcast([2 * HPG, HPG, P]),
                                        m.own[S64, :].unsqueeze(2).to_broadcast([2 * HPG, HPG, P]),
                                        ALU.mult).then_inc(max_rows, 1)

            def read_heads(u, i):
                n = QT * u + i
                dve.wait_ge(weighed, TICKS * u + J_CUM[i] + i + 1)
                if n >= 2:
                    dve.wait_ge(backed, n - 1)
                nc.vector.tensor_copy(head_t[0:VW, n % 2, :], cbank[0:VW, :]).then_inc(c_read, 1)

            def head_view():
                return hbank[:, 0:HPG * VW].rearrange("p (h n) -> p h n", h=HPG)

            def take_sums(u, i):
                n = QT * u + i
                dve.wait_ge(backed, n + 1)
                nc.vector.reciprocal(rsum[:, n % 2, :], head_view()[:, :, HD0]).then_inc(divided, 1)
                nc.vector.tensor_copy(head_sum[:, n % 2, :, :], head_view()[:, :, V1:VW]).then_inc(divided, 1)

            def add_parts(u, i):
                n = QT * u + i
                dve.wait_ge(divided, 3 * n + 2)
                nc.vector.tensor_tensor(head_sum[:, n % 2, :, :], head_view()[:, :, 0:HD0], head_sum[:, n % 2, :, :],
                                        ALU.add).then_inc(divided, 1)

            def divide(u, i):
                g, t, n = u // 2, (u % 2) * QT + i, QT * u + i
                dve.wait_ge(divided, 3 * n + 3)
                nc.vector.tensor_tensor(head[:, t, HPG * g:HPG * (g + 1), :], head_sum[:, n % 2, :, :],
                                        rsum[:, n % 2, :].unsqueeze(2).to_broadcast([P, HPG, HD0]),
                                        ALU.mult).then_inc(head_ready, 1)

            def tick(u, k):
                for step in planned(BACK, u, k):
                    take_sums(*step)
                for step in planned(SHIFT, u, k):
                    part_maxima(*step)
                for item in planned(SCORE, u, k):
                    maxima(*item)
                for step in planned(END, u, k):
                    read_heads(*step)
                for step in planned(BACK, u, k):
                    add_parts(*step)
                for step in planned(BACK, u, k):
                    divide(*step)
                for step in planned(SHIFT, u, k):
                    spread_maxima(*step)

            def low(t):
                dve.wait_ge(c_hi_done, t + 1)
                nc.vector.tensor_tensor(c_lo[:, t % 2, :, :], turned[t % 2][:, :].rearrange("p (k n) -> p k n", k=KT),
                                        c_hi[:, t % 2, :, :].bitcast(F32), ALU.subtract).then_inc(c_ready, 1)

            nc.vector.memset(split[:, :], 0.0).then_inc(split_set, 1)
            for at in ticks[:DRAIN]:
                tick(*at)
            low(0)
            low(1)
            for at in ticks[DRAIN:]:
                tick(*at)
            for t in range(NT):
                if 1 <= t < NT - 1:
                    low(t + 1)
                dve.wait_ge(projected, t + 1)
                nc.vector.tensor_tensor(m.x[:, t, :], score[t % NS][:, :], m.x[:, t, :], ALU.add).then_inc(added, 1)
                dve.wait_ge(added, t + 1)
                nc.vector.bn_stats(m.stats[:, t, :], m.x[:, t, :])

        @block.scalar
        def _(act):
            def read_qk(u, s):
                act.wait_ge(qk_turned, TU * u + s + 1)
                if s == 0:
                    if u >= 2:
                        act.wait_ge(t_scored, TICKS * (u - 1))
                    to = k_rows[0:64, u % 2, :]
                    src = qkbank[0:64, :]
                else:
                    if u >= 1:
                        act.wait_ge(t_scored, TICKS * (u - 1) + J_CUM[s - 1] + s)
                    to = q_rows[0:64, s - 1, :, :]
                    src = qkbank[0:64, :].rearrange("p (h n) -> p h n", h=HPG)
                nc.scalar.activation(to, src, ACT.Copy).then_inc(qk_read, 1)

            def exponentials(mm):
                act.wait_ge(t_scored, mm + 1)
                if mm >= NE:
                    act.wait_ge(p_ready, mm - NE + 1)
                nc.scalar.activation(prob[:, mm % NE, :], turned[mm % 2][:, :], ACT.Exp).then_inc(exped, 1)

            def high(mm):
                act.wait_ge(exped, mm + 1)
                if mm >= NP:
                    act.wait_ge(weighed, mm - NP + 1)
                nc.scalar.activation(p_hi[:, mm % NP, :], prob[:, mm % NE, :], ACT.Copy).then_inc(p_hi_done, 1)

            for u, k in ticks:
                mm = TICKS * u + k
                if 0 <= mm + AHEAD < TICKS * 2 * NG:
                    exponentials(mm + AHEAD)
                for item in planned(TURN, u, k):
                    read_qk(*item)
                if 0 <= mm + AHEAD < TICKS * 2 * NG:
                    high(mm + AHEAD)
                if u == 0 and k < KT:
                    act.wait_ge(loaded, 16)
                    nc.scalar.activation(wo_hi[:, k, :], raw_wo[:, k, :], ACT.Copy).then_inc(wo_hi_done, 1)
            for t in range(NT):
                act.wait_ge(c_turned, t + 1)
                if t >= 2:
                    act.wait_ge(projected, t - 1)
                nc.scalar.activation(c_hi[:, t % 2, :, :], turned[t % 2][:, :].rearrange("p (k n) -> p k n", k=KT),
                                     ACT.Copy).then_inc(c_hi_done, 1)

        @block.gpsimd
        def _(pool):
            nc.gpsimd.memset(k_rows[S64, :, :].bitcast(F32), 1.0).then_inc(ones_set, 1)
            for mm in range(TICKS * 2 * NG):
                pool.wait_ge(p_hi_done, mm + 1)
                if mm >= NP:
                    pool.wait_ge(weighed, mm - NP + 1)
                nc.gpsimd.tensor_tensor(p_lo[:, mm % NP, :], prob[:, mm % NE, :], p_hi[:, mm % NP, :].bitcast(F32),
                                        ALU.subtract).then_inc(p_ready, 1)
                if 2 <= mm < 2 + KT:
                    k = mm - 2
                    pool.wait_ge(wo_hi_done, k + 1)
                    nc.gpsimd.tensor_tensor(wo_lo[:, k, :], raw_wo[:, k, :], wo_hi[:, k, :].bitcast(F32),
                                            ALU.subtract).then_inc(wo_ready, 1)


def feed_forward0(nc, m, inp, fresh, ahead):
    FQ = FF // 4
    ROW = [(0, 128), (128, 128), (256, FQ - 256)]
    NR = len(ROW)
    S3 = 3 * R
    tiles = [(FQ * c + ROW[r][0], ROW[r][1]) for r in range(NR) for c in range(4)]
    NM = len(tiles)
    with ExitStack() as ctx:
        sb = lambda n, shape, dt=F32: ctx.enter_context(nc.sbuf_tensor(f"f0_{n}", shape, dt))
        ps = lambda n: ctx.enter_context(nc.psum_tensor(f"f0_{n}", [P, 512], F32))
        sem = lambda n: ctx.enter_context(nc.semaphore(f"f0_{n}"))
        w_raw, w_hi, w_lo = sb("w_raw", [P, 2 * FF]), sb("w_hi", [P, 2 * FF], F32R), sb("w_lo", [P, 2 * FF], F32R)
        d_raw, d_hi, d_lo = sb("d_raw", [P, NR, D]), sb("d_hi", [P, NR, D], F32R), sb("d_lo", [P, NR, D], F32R)
        a_raw, a_hi, a_lo = sb("a_raw", [P, KT, 64]), sb("a_hi", [P, KT, 64], F32R), sb("a_lo", [P, KT, 64], F32R)
        a2 = sb("a2", [P, NM, S3])
        b_raw, b_hi, b_lo = sb("b_raw", [64, FF]), sb("b_hi", [64, FF], F32R), sb("b_lo", [64, FF])
        b_st = sb("b_st", [64, FF], F32R)
        e_raw, e_hi, e_lo = sb("e_raw", [S3, D]), sb("e_hi", [S3, D], F32R), sb("e_lo", [S3, D])
        e_st = sb("e_st", [S3, D], F32R)
        pick = sb("pick", [64, 4])
        t_raw, t_hi, t_lo = sb("t_raw", [64, T]), sb("t_hi", [64, T], F32R), sb("t_lo", [64, T])
        t_st = sb("t_st", [64, B, T], F32R)
        s_raw, s_hi, s_lo = sb("s_raw", [S3, T]), sb("s_hi", [S3, T], F32R), sb("s_lo", [S3, T])
        s_st = sb("s_st", [S3, 2, T], F32R)
        act_g, prod = sb("act_g", [P, 2, T]), sb("prod", [P, 3, T])
        quarters = sb("quarters", [P, 2, T])
        z_hi, z_lo = sb("z_hi", [P, NR, T], F32R), sb("z_lo", [P, NR, T], F32R)
        out = [ps(f"out{k}") for k in range(QT)]
        gbank, ubank, tbank = [ps("gbank0"), ps("gbank1")], ps("ubank"), ps("tbank")
        ln = LayerNorm(nc, m, ctx, "n1", out, folded=True, fresh=fresh, ring=2)
        next_ln = LayerNorm(nc, m, ctx, "n2a", [gbank[1]], count=QT, ring=1, row=ln.row)
        gate = lambda b, k: gbank[0 if b else k % 2]
        FIRST = 7
        stats_made = sem("stats_made")
        loaded_a, loaded_b, loaded_w, loaded_d = (sem(n) for n in ("loaded_a", "loaded_b", "loaded_w", "loaded_d"))
        s_hi_done, s_lo_done, stacked, chain = (sem(n) for n in ("split_hi", "split_lo", "stacked", "chain"))
        t_made, t_read, gated, upped, silued, prodded, summed, z_hi_done, z_ready = (sem(n) for n in (
            "t_made", "t_read", "gated", "upped", "silued", "prodded", "summed", "z_hi_done", "z_ready"))
        t2_made, t2_read, downed, added = (sem(n) for n in ("t2_made", "t2_read", "downed", "added"))
        block = ctx.enter_context(nc.Block())

        splits = [(a_raw[:, :, :], a_hi[:, :, :], a_lo[:, :, :])]
        splits += [(b_raw[:, :], b_hi[:, :], b_lo[:, :]), (e_raw[:, :], e_hi[:, :], e_lo[:, :])]
        NWS = 4
        wc = 2 * FF // NWS
        for k in (0, 2, 1, 3):
            splits.append(tuple(x[:, k * wc:(k + 1) * wc] for x in (w_raw, w_hi, w_lo)))
        splits.append((d_raw[:, 0:2, :], d_hi[:, 0:2, :], d_lo[:, 0:2, :]))
        wl = ROW[2][1]
        splits.append((d_raw[0:wl, 2, :], d_hi[0:wl, 2, :], d_lo[0:wl, 2, :]))
        ALL = len(splits)

        @block.sync
        def _(sp):
            sp.dma_start(a_raw[:, :, :], inp["L0_a13"].rearrange("(k p) n -> p k n", p=P)).then_inc(loaded_a, 16)
            sp.dma_start(b_raw[:, :], inp["L0_b13"]).then_inc(loaded_b, 16)
            sp.dma_start(e_raw[:, :], inp["L0_b2"]).then_inc(loaded_b, 16)
            sp.dma_start(pick[:, :], inp["c_pick"]).then_inc(loaded_b, 16)
            sp.dma_start(w_raw[:, :], inp["L0_w13_t"]).then_inc(loaded_w, 16)
            for r, (at, w) in enumerate(ROW):
                sp.dma_start(d_raw[0:w, r, :], inp["L0_w2_t"][at:at + w, :]).then_inc(loaded_d, 16)
            for n, (at, w) in enumerate(tiles):
                sp.dma_start(a2[0:w, n, :], inp["L0_a2"][at:at + w, :]).then_inc(loaded_d, 16)
            if ahead:
                for k in range(NRAW_A):
                    load_attention_piece(sp, m, inp, 0, k)

        @block.scalar
        def _(act):
            ln.roots(act)
            for n, (raw, hi, _) in enumerate(splits):
                if 3 <= n < 3 + QT:
                    ln.high(act, n - 3)
                if n == 0:
                    act.wait_ge(loaded_a, 16)
                if n == 1:
                    act.wait_ge(loaded_b, 48)
                if n == 3:
                    act.wait_ge(loaded_w, 16)
                if n == ALL - 2:
                    act.wait_ge(loaded_d, 16 * (NR + NM))
                nc.scalar.activation(hi, raw, ACT.Copy).then_inc(s_hi_done, 1)

            def silu(b, n):
                w = tiles[n][1]
                k = NM * b + n
                act.wait_ge(gated, k + 1)
                if k >= 2:
                    act.wait_ge(prodded, k - 1)
                nc.scalar.activation(act_g[0:w, k % 2, :], gate(b, k)[0:w, :], ACT.Silu).then_inc(silued, 1)

            def z_high(b, r):
                w = ROW[r][1]
                act.wait_ge(summed, 3 * (NR * b + r) + 3)
                if b:
                    act.wait_ge(downed, 1)
                nc.scalar.activation(z_hi[0:w, r, :], quarters[0:w, (NR * b + r) % 2, :], ACT.Copy).then_inc(z_hi_done, 1)

            for b in range(B):
                for n in range(NM):
                    silu(b, n)
                    if b == 0 and 1 <= n <= QT:
                        ln.high(act, QT - 1 + n)
                    if b and n == 1:
                        z_high(0, NR - 1)
                    if ahead and b and n == FIRST - 2:
                        next_ln.roots(act)
                    if ahead and b and 0 <= n - FIRST < QT:
                        next_ln.high(act, n - FIRST)
                    if n % 4 == 1 and n >= 4:
                        z_high(b, n // 4 - 1)
            z_high(B - 1, NR - 1)

        @block.gpsimd
        def _(pool):
            for n, (raw, hi, lo) in enumerate(splits):
                pool.wait_ge(s_hi_done, n + 1)
                nc.gpsimd.tensor_tensor(lo, raw, hi.bitcast(F32), ALU.subtract).then_inc(s_lo_done, 1)

            def add_quarter(b, n):
                k, r, c, w = NM * b + n, n // 4, n % 4, tiles[n][1]
                z = NR * b + r
                pool.wait_ge(prodded, k + 1)
                q = quarters[0:w, (NR * b + r) % 2, :]
                if c == 1:
                    if z >= 2:
                        pool.wait_ge(z_ready, z - 1)
                    nc.gpsimd.tensor_tensor(q, prod[0:w, (k - 1) % 3, :], prod[0:w, k % 3, :], ALU.add).then_inc(summed, 1)
                elif c:
                    pool.wait_ge(summed, 3 * z + c - 1)
                    nc.gpsimd.tensor_tensor(q, q, prod[0:w, k % 3, :], ALU.add).then_inc(summed, 1)

            def z_low(b, r):
                z, w = NR * b + r, ROW[r][1]
                pool.wait_ge(z_hi_done, z + 1)
                nc.gpsimd.tensor_tensor(z_lo[0:w, r, :], quarters[0:w, (NR * b + r) % 2, :], z_hi[0:w, r, :].bitcast(F32),
                                        ALU.subtract).then_inc(z_ready, 1)

            for b in range(B):
                for n in range(NM):
                    add_quarter(b, n)
                    if n % 4 == 3:
                        z_low(b, n // 4)

        @block.vector
        def _(dve):
            steps = [0]

            def link(ins):
                steps[0] += 1
                ins.then_inc(chain, 1)
                dve.wait_ge(chain, steps[0])

            def stack(to, hi, lo, tmp, cols):
                n = tmp.shape[0]
                link(nc.vector.tensor_scalar(tmp, lo, pick[0:n, cols + 1:cols + 2], None, ALU.mult))
                return nc.vector.scalar_tensor_tensor(to, hi.bitcast(F32), pick[0:n, cols:cols + 1], tmp, ALU.mult, ALU.add)

            ln.scales(dve)
            ln.rows(dve, 0)
            for t in range(QT):
                if t + 1 < QT:
                    ln.rows(dve, t + 1)
                ln.low(dve, t)

            def t_stack(b):
                dve.wait_ge(t_made, b + 1)
                link(nc.vector.tensor_scalar(t_raw[:, :], (tbank, out[QT - 1])[b][0:64, :], 0.5, None, ALU.mult))
                link(nc.vector.tensor_copy(t_hi[:, :], t_raw[:, :]))
                link(nc.vector.tensor_tensor(t_lo[:, :], t_raw[:, :], t_hi[:, :].bitcast(F32), ALU.subtract))
                stack(t_st[:, b, :], t_hi[:, :], t_lo[:, :], t_raw[:, :], 0).then_inc(t_read, 1)

            def t2_stack(b):
                dve.wait_ge(t2_made, NM * (b + 1))
                link(nc.vector.tensor_scalar(s_raw[:, :], tbank[0:S3, :], 0.5, None, ALU.mult))
                link(nc.vector.tensor_copy(s_hi[:, :], s_raw[:, :]))
                link(nc.vector.tensor_tensor(s_lo[:, :], s_raw[:, :], s_hi[:, :].bitcast(F32), ALU.subtract))
                stack(s_st[:, b, :], s_hi[:, :], s_lo[:, :], s_raw[:, :], 0).then_inc(t2_read, 1)

            def multiply(b, n):
                k, w = NM * b + n, tiles[n][1]
                dve.wait_ge(silued, k + 1)
                dve.wait_ge(upped, k + 1)
                if k >= 3:
                    dve.wait_ge(t2_made, k - 2)
                    j = k - 3
                    done = 3 * (j // 4) + max(j % 4, 1)
                    dve.wait_ge(summed, done)
                nc.vector.tensor_tensor(prod[0:w, k % 3, :], act_g[0:w, k % 2, :], ubank[0:w, :],
                                        ALU.mult).then_inc(prodded, 1)

            def add_out(b, t):
                xt = m.x[:, QT * b + t, :]
                dve.wait_ge(downed, QT * b + t + 1)
                nc.vector.tensor_tensor(xt, out[t][:, :], xt, ALU.add).then_inc(added, 1)
                if b == 0:
                    dve.wait_ge(added, t + 1)
                    nc.vector.bn_stats(m.stats[:, t, :], xt).then_inc(stats_made, 1)

            dve.wait_ge(s_lo_done, 3)
            stack(b_st[:, :], b_hi[:, :], b_lo[:, :], b_raw[:, :], 2).then_inc(stacked, 1)
            t_stack(0)
            for b in range(B):
                for n in range(NM):
                    multiply(b, n)
                    if b == 0 and 1 <= n <= QT:
                        ln.low(dve, QT - 1 + n)
                    if b == 0 and n < QT:
                        ln.rows(dve, QT + n)
                    if b == 0 and n == QT + 1:
                        t_stack(1)
                    if b == 0 and n == QT + 2:
                        stack(e_st[:, :], e_hi[:, :], e_lo[:, :], e_raw[:, :], 2).then_inc(stacked, 1)
                    if b and n == 0:
                        t2_stack(0)
                    if b and n in (3, 4):
                        add_out(0, 2 * (n - 3))
                        add_out(0, 2 * (n - 3) + 1)
                    if ahead and b and n == FIRST - 2:
                        dve.wait_ge(stats_made, QT)
                        next_ln.variances(dve)
                    if ahead and b and n == FIRST - 1:
                        next_ln.inverses(dve)
                    if ahead and b and 0 <= n - FIRST < QT:
                        next_ln.low(dve, n - FIRST)
                    if ahead and b and 0 <= n + 1 - FIRST < QT:
                        next_ln.rows(dve, n + 1 - FIRST)
            t2_stack(B - 1)
            for t in range(QT):
                add_out(1, t)

        @block.tensor
        def _(pe):
            def three(to, l_hi, l_lo, r_hi, r_lo, start, stop):
                nc.tensor.matmul(to, l_hi, r_hi, start=start, stop=False)
                nc.tensor.matmul(to, l_hi, r_lo, start=False, stop=False)
                return nc.tensor.matmul(to, l_lo, r_hi, start=False, stop=stop)

            def down_rank(b):
                tok = slice(b * T, (b + 1) * T)
                for k in range(KT):
                    last = three((tbank, out[QT - 1])[b][0:64, :], a_hi[:, k, :], a_lo[:, k, :], m.h_hi[:, k, tok],
                                 m.h_lo[:, k, tok], k == 0, k == KT - 1)
                last.then_inc(t_made, 1)

            for t in range(QT):
                ln.turn(pe, t)
            ln.wait(pe, QT)
            pe.wait_ge(s_lo_done, 1)
            down_rank(0)

            def up_base(b, n, second):
                at, w = tiles[n]
                k = NM * b + n
                bank = ubank if second else gate(b, k)
                tok = slice(b * T, (b + 1) * T)
                if second and k >= 1:
                    pe.wait_ge(prodded, k)
                if not second and k >= 2:
                    pe.wait_ge(silued, k if b else k - 1)
                cols = slice(FF * second + at, FF * second + at + w)
                three(bank[0:w, :], w_hi[:, cols], w_lo[:, cols], m.f_hi[:, tok], m.f_lo[:, tok], True, False)

            def up_lora(b, n, second):
                at, w = tiles[n]
                k = NM * b + n
                bank = ubank if second else gate(b, k)
                if k == 0:
                    pe.wait_ge(t_read, 1)
                    pe.wait_ge(stacked, 1)
                rows = slice(32 * second, 32 * second + S3)
                nc.tensor.matmul(bank[0:w, :], b_st[rows, at:at + w], t_st[rows, b, :], start=False,
                                 stop=True).then_inc(upped if second else gated, 1)

            def lora_down(b, n):
                k, w = NM * b + n, tiles[n][1]
                pe.wait_ge(prodded, k + 1)
                if n == 0:
                    pe.wait_ge(t2_read if b else t_read, 1)
                nc.tensor.matmul(tbank[0:S3, :], a2[0:w, n, :], prod[0:w, k % 3, :], start=(n == 0),
                                 stop=(n == NM - 1)).then_inc(t2_made, 1)

            def down(b, r):
                w = ROW[r][1]
                pe.wait_ge(z_ready, NR * b + r + 1)
                for t in range(QT):
                    if b and r == 0:
                        pe.wait_ge(added, t + 1)
                    if not b and r == 0 and t == QT - 1:
                        pe.wait_ge(t_read, 2)
                    tok = slice(t * P, (t + 1) * P)
                    three(out[t][:, :], z_hi[0:w, r, tok], z_lo[0:w, r, tok], d_hi[0:w, r, :], d_lo[0:w, r, :],
                          r == 0, False)

            def finish(b):
                pe.wait_ge(t2_read, b + 1)
                pe.wait_ge(stacked, 2)
                for t in range(QT):
                    nc.tensor.matmul(out[t][:, :], s_st[:, b, t * P:(t + 1) * P], e_st[:, :], start=False,
                                     stop=True).then_inc(downed, 1)

            pe.wait_ge(s_lo_done, 3 + NWS)
            for b in range(B):
                for n in range(NM):
                    up_base(b, n, 0)
                    if b or n:
                        up_lora(b, n, 0)
                        up_base(b, n, 1)
                    else:
                        up_base(b, n, 1)
                        up_lora(b, n, 0)
                    up_lora(b, n, 1)
                    if b and n == 0:
                        lora_down(0, NM - 1)
                    if b and n == 2:
                        down(0, NR - 1)
                        finish(0)
                        lora_down(1, 0)
                    if n == 0 and b == 0:
                        pe.wait_ge(s_lo_done, ALL)
                    if n >= 1 and not (b and n == 1):
                        lora_down(b, n - 1)
                    if b == 0 and 1 <= n <= QT:
                        ln.turn(pe, QT - 1 + n)
                    if b == 0 and n == QT + 1:
                        ln.wait(pe, NT)
                        down_rank(1)
                    if n % 4 == 2 and n >= 4:
                        down(b, n // 4 - 1)
                    if ahead and b and 0 <= n - FIRST < QT:
                        next_ln.turn(pe, n - FIRST)
            lora_down(B - 1, NM - 1)
            down(B - 1, NR - 1)
            finish(B - 1)


def feed_forward1(nc, m, inp, fresh, x_out):
    tiles = FF_TILES
    NM = len(tiles)
    piece = feed_forward_piece
    with ExitStack() as ctx:
        sb = lambda n, shape, dt=F32: ctx.enter_context(nc.sbuf_tensor(f"f1_{n}", shape, dt))
        ps = lambda n: ctx.enter_context(nc.psum_tensor(f"f1_{n}", [P, 512], F32))
        sem = lambda n: ctx.enter_context(nc.semaphore(f"f1_{n}"))
        raw = m.raw
        w_hi, w_lo = sb("w_hi", [P, NRAW, 512], F32R), sb("w_lo", [P, NRAW, 512], F32R)
        act_g, prod = sb("act_g", [P, 2, T]), sb("prod", [P, 2, T])
        z_hi, z_lo = sb("z_hi", [P, 2, T], F32R), sb("z_lo", [P, 2, T], F32R)
        out = [ps(f"out{k}") for k in range(QT)]
        gbank, ubank = [ps("gbank0"), ps("gbank1")], [ps("ubank0"), ps("ubank1")]
        done = 0 if fresh else QT
        ln = LayerNorm(nc, m, ctx, "n3", out, fresh=fresh, stats=True, first=done, count=NT - done)
        w_hi_done, w_ready, gated, upped, silued, prodded, z_hi_done, z_ready, downed = (sem(n) for n in (
            "w_hi_done", "w_ready", "gated", "upped", "silued", "prodded", "z_hi_done", "z_ready", "downed"))
        finished, added, stored = sem("finished"), sem("added"), sem("stored")
        block = ctx.enter_context(nc.Block())
        ALL = B * NM

        def wait_down(engine, s):
            b, n = s // NM, s % NM
            if n == NM - 1:
                engine.wait_ge(finished, QT * (b + 1))
            else:
                engine.wait_ge(downed, (NM - 1) * b + n + 1)

        @block.sync
        def _(sp):
            for s in range(ALL):
                for p in range(3):
                    n = 3 * s + p
                    if n >= NRAW:
                        sp.wait_ge(w_ready, n - NRAW + 1)
                    if n >= NRAW or fresh:
                        load_feed_forward_piece(sp, m, inp, s, p)
            for t in range(NT):
                sp.wait_ge(added, t + 1)
                sp.dma_start(x_out[:, t, :], m.x[:, t, :]).then_inc(stored, 16)
            sp.wait_ge(stored, 16 * NT)

        @block.tensor
        def _(pe):
            def three(to, l_hi, l_lo, r_hi, r_lo, start, stop):
                nc.tensor.matmul(to, l_hi, r_hi, start=start, stop=False)
                nc.tensor.matmul(to, l_hi, r_lo, start=False, stop=False)
                return nc.tensor.matmul(to, l_lo, r_hi, start=False, stop=stop)

            def up(s, p):
                b, w = s // NM, tiles[s % NM][1]
                bank = (gbank, ubank)[p][s % 2]
                pe.wait_ge(w_ready, 3 * s + p + 1)
                if s >= 2:
                    pe.wait_ge((silued, prodded)[p], s - 1)
                hi, lo = piece(w_hi, s, p), piece(w_lo, s, p)
                for k in range(KT):
                    tok = slice(b * T, (b + 1) * T)
                    last = three(bank[0:w, :], hi[:, k, :], lo[:, k, :], m.h_hi[:, k, tok], m.h_lo[:, k, tok],
                                 k == 0, k == KT - 1)
                last.then_inc((gated, upped)[p], 1)

            def down(s):
                b, n, w = s // NM, s % NM, tiles[s % NM][1]
                pe.wait_ge(z_ready, s + 1)
                pe.wait_ge(w_ready, 3 * s + 3)
                hi, lo = piece(w_hi, s, 2), piece(w_lo, s, 2)
                for t in range(QT):
                    if b and n == 0:
                        pe.wait_ge(added, t + 1)
                    tok = slice(t * P, (t + 1) * P)
                    last = three(out[t][:, :], z_hi[0:w, s % 2, tok], z_lo[0:w, s % 2, tok], hi, lo, n == 0, n == NM - 1)
                    if n == NM - 1:
                        last.then_inc(finished, 1)
                if n < NM - 1:
                    last.then_inc(downed, 1)

            early = 0 if done else QT + 2
            for t in range(early):
                ln.turn(pe, t)
            if not done:
                ln.wait(pe, QT)
            for s in range(ALL):
                up(s, 0)
                if s == 0:
                    for t in range(early, ln.count):
                        ln.turn(pe, t)
                up(s, 1)
                if s == 1:
                    ln.wait(pe, ln.count)
                if s >= 1:
                    down(s - 1)
            down(ALL - 1)

        @block.scalar
        def _(act):
            def weights_high(s, p):
                n = 3 * s + p
                act.wait_ge(m.loaded[n % NRAW], 16 * (m.loads_before[n % NRAW] + n // NRAW + 1))
                if s >= 2:
                    if p < 2:
                        act.wait_ge((gated, upped)[p], s - 1)
                    else:
                        wait_down(act, s - 2)
                nc.scalar.activation(piece(w_hi, s, p), piece(raw, s, p), ACT.Copy).then_inc(w_hi_done, 1)

            if not done:
                ln.roots(act)
            for p in range(2):
                weights_high(0, p)
            if done:
                ln.roots(act)
            for t in range(ln.count):
                ln.high(act, t)
                if t == 0:
                    weights_high(0, 2)
            for s in range(ALL):
                w = tiles[s % NM][1]
                if s + 1 < ALL:
                    weights_high(s + 1, 0)
                    weights_high(s + 1, 1)
                act.wait_ge(gated, s + 1)
                if s >= 2:
                    act.wait_ge(prodded, s - 1)
                nc.scalar.activation(act_g[0:w, s % 2, :], gbank[s % 2][0:w, :], ACT.Silu).then_inc(silued, 1)
                if s + 1 < ALL:
                    weights_high(s + 1, 2)
                act.wait_ge(prodded, s + 1)
                if s >= 2:
                    wait_down(act, s - 2)
                nc.scalar.activation(z_hi[0:w, s % 2, :], prod[0:w, s % 2, :], ACT.Copy).then_inc(z_hi_done, 1)

        @block.vector
        def _(dve):
            def add_out(b):
                for t in range(QT):
                    dve.wait_ge(finished, QT * b + t + 1)
                    xt = m.x[:, QT * b + t, :]
                    nc.vector.tensor_tensor(xt, out[t][:, :], xt, ALU.add).then_inc(added, 1)

            ln.parts(dve)
            for s in range(ALL):
                w = tiles[s % NM][1]
                dve.wait_ge(silued, s + 1)
                dve.wait_ge(upped, s + 1)
                if s >= 2:
                    dve.wait_ge(z_ready, s - 1)
                nc.vector.tensor_tensor(prod[0:w, s % 2, :], act_g[0:w, s % 2, :], ubank[s % 2][0:w, :],
                                        ALU.mult).then_inc(prodded, 1)
                dve.wait_ge(z_hi_done, s + 1)
                nc.vector.tensor_tensor(z_lo[0:w, s % 2, :], prod[0:w, s % 2, :], z_hi[0:w, s % 2, :].bitcast(F32),
                                        ALU.subtract).then_inc(z_ready, 1)
                if s == NM:
                    add_out(0)
            add_out(1)

        @block.gpsimd
        def _(pool):
            for s in range(ALL):
                for p in range(3):
                    pool.wait_ge(w_hi_done, 3 * s + p + 1)
                    nc.gpsimd.tensor_tensor(piece(w_lo, s, p), piece(raw, s, p), piece(w_hi, s, p).bitcast(F32),
                                            ALU.subtract).then_inc(w_ready, 1)


def program(nc, inp, out, phases=("attn0", "ffn0", "attn1", "ffn1")):
    with ExitStack() as ctx:
        sb = lambda n, shape, dt=F32: ctx.enter_context(nc.sbuf_tensor(n, shape, dt))
        sem = lambda n: ctx.enter_context(nc.semaphore(n))
        m = Memory()
        m.x = sb("x", [P, NT, D])
        m.ident, m.mask = sb("ident", [P, P]), sb("mask", [P, P])
        m.mask_t, m.own = sb("mask_t", [P, P]), sb("own", [P, HPG])
        m.ident_b, m.mask_b, m.mask_t_b = (sb(n, [P, P], BF16) for n in ("ident_b", "mask_b", "mask_t_b"))
        m.stats = sb("stats", [P, NT, 6])
        m.x_loaded = [sem(f"x_loaded{k}") for k in range(NT // 2)]
        m.fetched, cast = sem("fetched"), sem("cast")
        m.fetched_all = 16 * 4
        x_in = inp["L0_attn_x"].rearrange("b (t p) d -> p (b t) d", p=P)
        x_out = out.rearrange("b (t p) d -> p (b t) d", p=P)

        with nc.Block() as block:
            @block.sync
            def _(sp):
                for to, of in ((m.ident, "c_ident"), (m.mask, "c_mask"), (m.mask_t, "c_mask_t"), (m.own, "c_own")):
                    sp.dma_start(to[:, :], inp[of]).then_inc(m.fetched, 16)
                for k in range(NT // 2):
                    sp.dma_start(m.x[:, 2 * k:2 * k + 2, :], x_in[:, 2 * k:2 * k + 2, :]).then_inc(m.x_loaded[k], 16)

            @block.vector
            def _(dve):
                dve.wait_ge(m.fetched, m.fetched_all)
                for to, of in ((m.ident_b, m.ident), (m.mask_b, m.mask), (m.mask_t_b, m.mask_t)):
                    nc.vector.tensor_copy(to[:, :], of[:, :]).then_inc(cast, 1)

        def stage(name):
            scope = ExitStack()
            return scope, lambda n, shape, dt=F32: scope.enter_context(nc.sbuf_tensor(n, shape, dt)), name == phases[0]

        if "attn0" in phases:
            scope, ssb, fresh = stage("attn0")
            with scope:
                m.q2 = ssb("q2", [P, NT, NG * HPG, 4, HD0], F32R)
                m.k2 = ssb("k2", [P, NT, NG, 4, HD0], F32R)
                m.vw = ssb("vw", [P, NT, NG, 2, 2 * HD0 + 1], F32R)
                with ExitStack() as inner:
                    isb = lambda n, shape, dt=F32: inner.enter_context(nc.sbuf_tensor(n, shape, dt))
                    m.h_hi, m.h_lo = isb("h0_hi", [P, KT, NT * P], F32R), isb("h0_lo", [P, KT, NT * P], F32R)
                    m.cos0, m.sin0, m.nsin0 = (isb(n, [P, QT, HD0 // 2]) for n in ("cos0", "sin0", "nsin0"))
                    m.tables0 = [(m.cos0, inp["c_cos0"]), (m.sin0, inp["c_sin0"]), (m.nsin0, inp["c_nsin0"])]
                    project0(nc, m, inp["L0_qkv"], fresh)
                attend0(nc, m, inp["L0_attn_Wo"])
        m.h_hi, m.h_lo = sb("h_hi", [P, KT, NT * P], F32R), sb("h_lo", [P, KT, NT * P], F32R)
        m.raw = sb("raw", [P, NRAW, 512])
        m.loaded, m.loads_before = [sem(f"loaded{k}") for k in range(NRAW)], [0] * NRAW
        if "ffn0" in phases:
            scope, ssb, fresh = stage("ffn0")
            with scope:
                m.f_hi, m.f_lo = ssb("f_hi", [P, NT * P], F32R), ssb("f_lo", [P, NT * P], F32R)
                feed_forward0(nc, m, inp, fresh, "attn1" in phases)
        if "attn1" in phases:
            scope, ssb, fresh = stage("attn1")
            with scope:
                m.cos1, m.sin1 = ssb("cos1", [P, T]), ssb("sin1", [P, T])
                m.cos1_in, m.sin1_in = inp["c_cos1"], inp["c_sin1"]
                attention1(nc, m, inp, fresh, "ffn1" in phases)
        if "ffn1" in phases:
            scope, ssb, fresh = stage("ffn1")
            with scope:
                feed_forward1(nc, m, inp, fresh, x_out)
            return

        stored = sem("stored")
        with nc.Block() as block:
            @block.sync
            def _(sp):
                sp.dma_start(x_out, m.x[:, :, :]).then_inc(stored, 16)
                sp.wait_ge(stored, 16)


class Memory:
    pass


def laid_out(inputs):
    import numpy as np

    a = {n: np.asarray(v) for n, v in inputs.items()}
    same = ["L0_attn_x", "L0_attn_Wo", "L1_attn_wq", "L1_attn_wk", "L1_attn_wv", "L1_attn_wo"]
    out = {n: np.ascontiguousarray(a[n]) for n in same}
    out["L0_qkv"] = np.concatenate([a["L0_attn_Wq"], a["L0_attn_Wk"], a["L0_attn_Wv"]], axis=1)
    out["L1_gate_up_t"] = np.ascontiguousarray(a["L1_ffn_w_gate_up"].T)
    out["L1_down_t"] = np.ascontiguousarray(a["L1_ffn_w_down"].T)
    out["L0_w13_t"] = np.ascontiguousarray(np.concatenate([a["L0_ffn_w1q"], a["L0_ffn_w3q"]], axis=0).T)
    out["L0_w2_t"] = np.ascontiguousarray(a["L0_ffn_w2q"].T)

    def stack(first, second, axis):
        shape = list(first.shape)
        shape[axis] = 32 - 3 * R
        gap = np.zeros(shape, first.dtype)
        return np.concatenate([first] * 3 + [gap] + [second] * 3 + [gap], axis=axis)

    out["L0_a13"] = stack(a["L0_ffn_a1"].T, a["L0_ffn_a3"].T, 1)
    out["L0_b13"] = stack(a["L0_ffn_b1"].T, a["L0_ffn_b3"].T, 0)
    out["L0_a2"] = np.concatenate([a["L0_ffn_a2"].T] * 3, axis=1)
    out["L0_b2"] = np.concatenate([a["L0_ffn_b2"].T] * 3, axis=0)
    out.update(constants())
    return out


def constants():
    import numpy as np

    ident = np.eye(P, dtype=np.float32)
    key, query = np.arange(P)[None, :], np.arange(P)[:, None]
    mask = np.where(key > query, np.float32(-1e30), np.float32(0))
    row, h = np.arange(P)[:, None], np.arange(HPG)[None, :]
    own = ((row == 64 + h) | (row == 64 + HPG + h)).astype(np.float32)
    one, lora = np.float32(1), np.arange(32) // R
    rows = np.stack([(lora == 0) | (lora == 2), lora == 1, lora <= 1, lora == 2], axis=1)
    pick = np.concatenate([rows, rows], axis=0) * one
    pos = np.arange(T, dtype=np.float32)
    inv0 = (np.float32(1) / np.float32(500000.0) ** (np.arange(0, HD0, 2, dtype=np.float32) / np.float32(HD0)))
    f0 = (pos[:, None] * inv0.astype(np.float32)[None, :]).astype(np.float32).reshape(QT, P, HD0 // 2).transpose(1, 0, 2)
    inv = 1.0 / 500000.0 ** (np.arange(0, HD1, 2, dtype=np.float64) / HD1)
    wavelen = 2.0 * np.pi / inv
    low_wl, high_wl = 1024 / 1.0, 1024 / 4.0
    smooth = (1024 / wavelen - 1.0) / (4.0 - 1.0)
    scaled = np.where(wavelen > low_wl, inv / 8.0, inv)
    mid = (wavelen <= low_wl) & (wavelen >= high_wl)
    scaled = np.where(mid, (1 - smooth) * inv / 8.0 + smooth * inv, scaled).astype(np.float32)
    f1 = (pos[:, None] * scaled[None, :]).T
    return {
        "c_ident": ident,
        "c_mask": mask,
        "c_mask_t": np.ascontiguousarray(mask.T),
        "c_own": own,
        "c_pick": pick,
        "c_cos0": np.ascontiguousarray(np.cos(f0)),
        "c_sin0": np.ascontiguousarray(np.sin(f0)),
        "c_nsin0": np.ascontiguousarray(-np.sin(f0)),
        "c_cos1": np.concatenate([np.cos(f1), np.cos(f1)], axis=0),
        "c_sin1": np.concatenate([np.sin(f1), -np.sin(f1)], axis=0),
    }


def kernel(**inputs):
    import concourse.bacc as _bacc
    from concourse import mybir as _mybir
    from concourse.bass_utils import run_bass_kernel_spmd as _run

    nc = _bacc.Bacc("TRN2", target_bir_lowering=False, num_devices=1)
    arrays = laid_out(inputs)
    args = {}
    for name, a in arrays.items():
        args[name] = nc.dram_tensor(f"in_{name}", a.shape, _mybir.dt.from_np(a.dtype), kind="ExternalInput").ap()
    out = nc.dram_tensor("out_0", (B, T, D), _mybir.dt.float32, kind="ExternalOutput").ap()
    program(nc, args, out)
    r = _run(nc, [{f"in_{name}": a for name, a in arrays.items()}], core_ids=[0])
    return r.results[0]["out_0"]
```
